# Optimizing a Trainium2 kernel written in Bass

```python
import numpy as np
import jax
import jax.numpy as jnp

def _softmax(x, axis=-1):
    return jax.nn.softmax(x, axis=axis)

def _gelu(x):
    return jax.nn.gelu(x, approximate=True)

def _silu(x):
    return jax.nn.silu(x)

def _sigmoid(x):
    return jax.nn.sigmoid(x)

def _layernorm(x, axis=-1, eps=1e-05):
    m = jnp.mean(x, axis=axis, keepdims=True)
    v = jnp.var(x, axis=axis, keepdims=True)
    return (x - m) / jnp.sqrt(v + eps)

def _scatter_add(tgt, idx, src, axis=0):
    return tgt.at[idx].add(src)

def _segment_sum(src, seg, n):
    return jax.ops.segment_sum(src, seg, n)
kernel_name = 'mk_xattn_ffn_d2_seqx_r8_9327f2'

def setup_inputs(seed: int=0):
    np.random.seed(seed)
    _w = jnp.asarray

    def _rec_inputs():
        import jax
        import jax.numpy as jnp
        _rk = jax.random.key(seed)
        x = 7.22e-05 + 1 * jax.random.normal(jax.random.fold_in(_rk, 1), (128, 64, 128), jnp.float32)
        _lenS = 64 - jax.random.randint(jax.random.fold_in(_rk, 7), (128,), 0, max(1, 64 // 4) + 1, jnp.int32)
        _lenS2 = 64 - jax.random.randint(jax.random.fold_in(_rk, 8), (128,), 0, max(1, 64 // 4) + 1, jnp.int32)
        _ctx_1024P = jax.random.normal(jax.random.fold_in(_rk, 11), (128, 16, 128), jnp.float32)
        _ctx_1024c = jax.random.dirichlet(jax.random.fold_in(_rk, 511), 0.3 * jnp.ones((16,), jnp.float32), (128, 64))
        _ctx_1024t = jnp.einsum('bsk,bkd->bsd', _ctx_1024c, _ctx_1024P)
        _ctx_1024t = _ctx_1024t * jax.lax.rsqrt(jnp.mean(jnp.square(_ctx_1024t)) + 1e-12) * 0.953939
        ctx_1024 = 4.13588e-05 + 0.999923 * (_ctx_1024t + 0.3 * jax.random.normal(jax.random.fold_in(_rk, 611), (128, 64, 128), jnp.float32))
        return (x, ctx_1024)
    x, ctx_1024 = _rec_inputs()

    def _L0_xattn_setup():
        import jax, jax.numpy as jnp
        import numpy as np
        D_MODEL = 128
        NUM_HEADS = 16
        NEG_BIG = 10000000000.0
        key = jax.random.key(seed)
        ks = jax.random.split(key, 7)
        B, S, D = (4, 256, D_MODEL)
        sc = 1.0 / np.sqrt(D)
        return {'q': jax.random.normal(ks[0], (B, S, D), jnp.float32), 'k': jax.random.normal(ks[1], (B, S, D), jnp.float32), 'v': jax.random.normal(ks[2], (B, S, D), jnp.float32), 'Wq': jax.random.normal(ks[3], (D, D), jnp.float32) * sc, 'bq': jnp.zeros((D,), jnp.float32), 'Wo': jax.random.normal(ks[4], (D, D), jnp.float32) * sc, 'bo': jnp.zeros((D,), jnp.float32)}
    _L0_xattn_all = _L0_xattn_setup()
    _L0_xattn_in = {k: v for k, v in _L0_xattn_all.items() if k in ('Wq', 'bq', 'Wo', 'bo')}
    del _L0_xattn_all

    def _L0_ffn_setup():
        import jax, jax.numpy as jnp
        import numpy as np
        TOP_K = 8
        key = jax.random.key(seed)
        ks = jax.random.split(key, 6)
        B, S, D, F, E = (2, 128, 128, 64, 64)
        x = jax.random.normal(ks[0], (B, S, D), dtype=jnp.float32)
        centroids = jax.random.normal(ks[1], (E, D), dtype=jnp.float32) * 0.05
        expert_biases = jnp.zeros((E,), dtype=jnp.float32)
        Ws_up = jax.random.normal(ks[2], (D, F), dtype=jnp.float32) / np.sqrt(D)
        Ws_down = jax.random.normal(ks[3], (F, D), dtype=jnp.float32) / np.sqrt(F)
        W_up = jax.random.normal(ks[4], (E, D, F), dtype=jnp.float32) / np.sqrt(D)
        W_down = jax.random.normal(ks[5], (E, F, D), dtype=jnp.float32) / np.sqrt(F)
        return {'x': x, 'centroids': centroids, 'expert_biases': expert_biases, 'Ws_up': Ws_up, 'Ws_down': Ws_down, 'W_up': W_up, 'W_down': W_down}
    _L0_ffn_all = _L0_ffn_setup()
    _L0_ffn_in = {k: v for k, v in _L0_ffn_all.items() if k in ('centroids', 'expert_biases', 'Ws_up', 'Ws_down', 'W_up', 'W_down')}
    del _L0_ffn_all

    def _L1_xattn_setup():
        import jax, jax.numpy as jnp
        import numpy as np
        import math
        B, L, D, H = (8, 512, 128, 16)
        DK = D // H
        FACTOR = 1

        def _linear(x, W, b):
            return jnp.einsum('bld,od->blo', x, W) + b
        rng = jax.random.key(seed)
        ks = jax.random.split(rng, 11)
        s = 0.02
        return {'query': jax.random.normal(ks[0], (B, L, D), jnp.float32), 'key': jax.random.normal(ks[1], (B, L, D), jnp.float32), 'value': jax.random.normal(ks[2], (B, L, D), jnp.float32), 'Wq': jax.random.normal(ks[3], (D, D), jnp.float32) * s, 'bq': jax.random.normal(ks[4], (D,), jnp.float32) * s, 'Wk': jax.random.normal(ks[5], (D, D), jnp.float32) * s, 'bk': jax.random.normal(ks[6], (D,), jnp.float32) * s, 'Wv': jax.random.normal(ks[7], (D, D), jnp.float32) * s, 'bv': jax.random.normal(ks[8], (D,), jnp.float32) * s, 'Wo': jax.random.normal(ks[9], (D, D), jnp.float32) * s, 'bo': jax.random.normal(ks[10], (D,), jnp.float32) * s}
    _L1_xattn_all = _L1_xattn_setup()
    _L1_xattn_in = {k: v for k, v in _L1_xattn_all.items() if k in ('Wq', 'bq', 'Wk', 'bk', 'Wv', 'bv', 'Wo', 'bo')}
    del _L1_xattn_all

    def _L1_ffn_setup():
        import jax, jax.numpy as jnp
        import numpy as np
        LN_EPS = 0.001
        EPS = 1e-05
        QB = 128.0

        def ste_round(x):
            return x + jax.lax.stop_gradient(jnp.round(x) - x)
        key = jax.random.key(seed)
        k1, k2 = jax.random.split(key)
        x = jax.random.normal(k1, (4, 1024, 128), dtype=jnp.float32)
        weight = jax.random.normal(k2, (128, 128), dtype=jnp.float32) * 0.02
        ln_gamma = jnp.ones((128,), dtype=jnp.float32)
        ln_beta = jnp.zeros((128,), dtype=jnp.float32)
        return {'x': x, 'weight': weight, 'ln_gamma': ln_gamma, 'ln_beta': ln_beta}
    _L1_ffn_all = _L1_ffn_setup()
    _L1_ffn_in = {k: v for k, v in _L1_ffn_all.items() if k in ('weight', 'ln_gamma', 'ln_beta')}
    del _L1_ffn_all
    return {'x': x, 'ctx_1024': ctx_1024, 'L0_xattn_Wq': _L0_xattn_in['Wq'], 'L0_xattn_bq': _L0_xattn_in['bq'], 'L0_xattn_Wo': _L0_xattn_in['Wo'], 'L0_xattn_bo': _L0_xattn_in['bo'], 'L0_ffn_centroids': _L0_ffn_in['centroids'], 'L0_ffn_expert_biases': _L0_ffn_in['expert_biases'], 'L0_ffn_Ws_up': _L0_ffn_in['Ws_up'], 'L0_ffn_Ws_down': _L0_ffn_in['Ws_down'], 'L0_ffn_W_up': _L0_ffn_in['W_up'], 'L0_ffn_W_down': _L0_ffn_in['W_down'], 'L1_xattn_Wq': _L1_xattn_in['Wq'], 'L1_xattn_bq': _L1_xattn_in['bq'], 'L1_xattn_Wk': _L1_xattn_in['Wk'], 'L1_xattn_bk': _L1_xattn_in['bk'], 'L1_xattn_Wv': _L1_xattn_in['Wv'], 'L1_xattn_bv': _L1_xattn_in['bv'], 'L1_xattn_Wo': _L1_xattn_in['Wo'], 'L1_xattn_bo': _L1_xattn_in['bo'], 'L1_ffn_weight': _L1_ffn_in['weight'], 'L1_ffn_ln_gamma': _L1_ffn_in['ln_gamma'], 'L1_ffn_ln_beta': _L1_ffn_in['ln_beta']}

def reference(x, ctx_1024, L0_xattn_Wq, L0_xattn_bq, L0_xattn_Wo, L0_xattn_bo, L0_ffn_centroids, L0_ffn_expert_biases, L0_ffn_Ws_up, L0_ffn_Ws_down, L0_ffn_W_up, L0_ffn_W_down, L1_xattn_Wq, L1_xattn_bq, L1_xattn_Wk, L1_xattn_bk, L1_xattn_Wv, L1_xattn_bv, L1_xattn_Wo, L1_xattn_bo, L1_ffn_weight, L1_ffn_ln_gamma, L1_ffn_ln_beta):
    import jax
    import jax.numpy as jnp

    def _L0_xattn_ref(q, k, v, Wq, bq, Wo, bo):
        import jax, jax.numpy as jnp
        import numpy as np
        D_MODEL = 128
        NUM_HEADS = 16
        NEG_BIG = 10000000000.0
        B, S, D = q.shape
        H = NUM_HEADS
        hd = D // H

        def proj_split(x):
            y = x @ Wq + bq
            return y.reshape(B, -1, H, hd).transpose(0, 2, 1, 3)
        qh, kh, vh = (proj_split(q), proj_split(k), proj_split(v))
        scale = jnp.sqrt(jnp.asarray(hd, jnp.float32))
        scores = jnp.einsum('bhqd,bhkd->bhqk', qh, kh) / scale
        i = jnp.arange(S)[:, None]
        j = jnp.arange(S)[None, :]
        mask = (i >= j).astype(scores.dtype)
        scores = scores * mask - jnp.asarray(NEG_BIG, scores.dtype) * (1.0 - mask)
        weights = jax.nn.softmax(scores, axis=-1)
        attn = jnp.einsum('bhqk,bhkd->bhqd', weights, vh)
        concat = attn.transpose(0, 2, 1, 3).reshape(B, S, D)
        return concat @ Wo + bo

    def _L0_ffn_ref(x, centroids, expert_biases, Ws_up, Ws_down, W_up, W_down):
        import jax, jax.numpy as jnp
        import numpy as np
        TOP_K = 8
        B, S, D = x.shape
        E = centroids.shape[0]
        T = B * S
        xf = x.reshape(T, D)
        shared = jax.nn.silu(xf @ Ws_up) @ Ws_down
        aff = xf @ centroids.T
        biased = aff + expert_biases
        _, idx = jax.lax.top_k(biased, TOP_K)
        sel = jnp.take_along_axis(aff, idx, axis=1)
        w = jax.nn.sigmoid(sel)
        w = w / (jnp.sum(w, axis=-1, keepdims=True) + 1e-08)
        cw = jnp.zeros((T, E), dtype=x.dtype).at[jnp.arange(T)[:, None], idx].add(w)
        h = jax.nn.silu(jnp.einsum('td,edf->etf', xf, W_up))
        y = jnp.einsum('etf,efd->etd', h, W_down)
        routed = jnp.einsum('etd,te->td', y, cw)
        return (shared + routed).reshape(B, S, D)

    def _L1_xattn_ref(query, key, value, Wq, bq, Wk, bk, Wv, bv, Wo, bo):
        import jax, jax.numpy as jnp
        import numpy as np
        import math
        B, L, D, H = (8, 512, 128, 16)
        DK = D // H
        FACTOR = 1

        def _linear(x, W, b):
            return jnp.einsum('bld,od->blo', x, W) + b
        Bx, Lx, _ = query.shape
        Q = _linear(query, Wq, bq).reshape(Bx, Lx, H, DK).transpose(0, 2, 1, 3)
        K = _linear(key, Wk, bk).reshape(Bx, Lx, H, DK).transpose(0, 2, 1, 3)
        V = _linear(value, Wv, bv).reshape(Bx, Lx, H, DK).transpose(0, 2, 1, 3)
        Qf = jnp.fft.rfft(Q, axis=2)
        Kf = jnp.fft.rfft(K, axis=2)
        corr = jnp.fft.irfft(Qf * jnp.conj(Kf), n=Lx, axis=2)
        corr_mean = corr.mean(axis=-1)
        top_k = max(1, int(FACTOR * math.log(Lx + 1)))
        top_k = min(top_k, Lx)
        top_w, top_idx = jax.lax.top_k(corr_mean, top_k)
        top_w = jax.nn.softmax(top_w, axis=-1)
        pos = jnp.arange(Lx)
        out = jnp.zeros_like(V)
        for i in range(top_k):
            gidx = (pos[None, None, :] - top_idx[:, :, i, None]) % Lx
            rolled = jnp.take_along_axis(V, gidx[..., None], axis=2)
            out = out + top_w[:, :, i, None, None] * rolled
        out = out.transpose(0, 2, 1, 3).reshape(Bx, Lx, D)
        out = _linear(out, Wo, bo)
        return out

    def _L1_ffn_ref(x, weight, ln_gamma, ln_beta):
        import jax, jax.numpy as jnp
        import numpy as np
        LN_EPS = 0.001
        EPS = 1e-05
        QB = 128.0

        def ste_round(x):
            return x + jax.lax.stop_gradient(jnp.round(x) - x)
        mu = jnp.mean(x, axis=-1, keepdims=True)
        var = jnp.var(x, axis=-1, keepdims=True)
        xn = (x - mu) * jax.lax.rsqrt(var + LN_EPS) * ln_gamma + ln_beta
        beta = jnp.mean(jnp.abs(weight))
        w_q = jnp.clip(ste_round(weight / (beta + EPS)), -1.0, 1.0)
        gamma = jnp.max(jnp.abs(xn))
        xq = jnp.clip(xn * QB / gamma, -QB + EPS, QB - EPS)
        y = jnp.einsum('bsd,du->bsu', xq, w_q)
        return y * (gamma * beta / QB)
    x = x + _L0_xattn_ref(_layernorm(x, axis=-1), ctx_1024, ctx_1024, L0_xattn_Wq, L0_xattn_bq, L0_xattn_Wo, L0_xattn_bo)
    x = x + _L0_ffn_ref(_layernorm(x, axis=-1), L0_ffn_centroids, L0_ffn_expert_biases, L0_ffn_Ws_up, L0_ffn_Ws_down, L0_ffn_W_up, L0_ffn_W_down)
    x = x + _L1_xattn_ref(_layernorm(x, axis=-1), ctx_1024, ctx_1024, L1_xattn_Wq, L1_xattn_bq, L1_xattn_Wk, L1_xattn_bk, L1_xattn_Wv, L1_xattn_bv, L1_xattn_Wo, L1_xattn_bo)
    x = x + _L1_ffn_ref(_layernorm(x, axis=-1), L1_ffn_weight, L1_ffn_ln_gamma, L1_ffn_ln_beta)
    return x

_drawn_inputs = setup_inputs


def setup_inputs(seed=0):
    import zlib

    import numpy as np

    out = dict(_drawn_inputs(seed))
    spreads = {'L0_xattn_bq': (0.0, 0.1),
     'L0_xattn_bo': (0.0, 0.1),
     'L0_ffn_expert_biases': (0.0, 0.1),
     'L1_ffn_ln_gamma': (1.0, 0.591),
     'L1_ffn_ln_beta': (0.0, 0.768)}
    factors = {'L1_xattn_Wq': 11.602,
     'L1_xattn_bq': 64.0,
     'L1_xattn_Wk': 11.491,
     'L1_xattn_bk': 64.0,
     'L1_xattn_bv': 8.0,
     'L1_xattn_bo': 3.393}
    for name, (base, spread) in spreads.items():
        noise = np.random.default_rng([zlib.crc32(name.encode()), seed]).standard_normal(out[name].shape)
        drawn = base * np.exp(spread * noise) if base else spread * noise
        out[name] = jnp.asarray(drawn.astype(out[name].dtype))
    for name, factor in factors.items():
        out[name] = (out[name] * factor).astype(out[name].dtype)
    return out
```

```python
from contextlib import ExitStack

import numpy as np

import concourse.bass as bass
from concourse import mybir

F32 = mybir.dt.float32
F32R = mybir.dt.float32r
BF16 = mybir.dt.bfloat16
F16 = mybir.dt.float16
I32 = mybir.dt.int32
ALU = mybir.AluOpType
ACT = mybir.ActivationFunctionType
AX = mybir.AxisListType

P = 128
S = 64
D = 128
TILES = 64
H = 16
HD = D // H
E = 64
FH = 64
PAIRS = E // 2 + 1
TOP = 8
DELAYS = 4
QB = 128.0
BIG = 1e10
SENTINEL = 3.0e38


def at_least(eng, sem, value):
    if isinstance(value, int) and value <= 0:
        return
    eng.wait_ge(sem, value)


def wait_apart(eng, sem, value, idle):
    at_least(eng, sem, value)
    if not isinstance(value, int):
        eng.sem_inc(idle, 1)


def pipeline(eng, count, lag, unroll, step):
    first = -(-lag // unroll) * unroll
    for t in range(first):
        step(t, t % unroll)
    with eng.Fori(first // unroll, count // unroll) as g:
        for r in range(unroll):
            step(g * unroll + r, r)
    for t in range(count, count + lag):
        step(t, t % unroll)


def live(t, lag, count):
    return not isinstance(t, int) or 0 <= t - lag < count


def setup(nc, cst, dram, sem):
    landed = sem("s_landed")
    made = sem("s_made")
    done = sem("s_done")
    bias = sem("s_bias")
    with ExitStack() as mem:
        bqB = mem.enter_context(nc.sbuf_tensor("s_bqB", [P, P], F32))
        borow = mem.enter_context(nc.sbuf_tensor("s_borow", [1, P], F32))
        onerow = mem.enter_context(nc.sbuf_tensor("s_onerow", [1, P], F32))
        bqc = mem.enter_context(nc.sbuf_tensor("s_bqc", [P, 1], F32))
        pbias = mem.enter_context(nc.psum_tensor("s_pbias", [P, 512], F32))
        loads = [(cst[name][:], dram[name]) for name in ("ident", "ident16", "hmask", "Wq", "Wo")]
        loads += [(cst["bqH"][64 * b:64 * b + 64, :], dram["bq"].rearrange("(h c) -> c h", h=2)) for b in range(2)]
        loads += [(bqc[:], dram["bq"].unsqueeze(1)), (borow[:], dram["bo"].unsqueeze(0))]
        cent = mem.enter_context(nc.sbuf_tensor("s_cent", [E, D], F32))
        loads += [(cent[:], dram["centroids"]), (cst["eb"][:], dram["eb"].unsqueeze(0).to_broadcast([P, E]))]
        shared = mem.enter_context(nc.sbuf_tensor("s_shared", [P, 2, P], F32))
        raw = mem.enter_context(nc.sbuf_tensor("s_raw", [P, 2, E // 2 * P], F32))
        loads += [(raw[:, 0, :].rearrange("p (e f) -> p e f", f=FH), dram["W_up"].rearrange("e d f -> d e f"))]
        loads += [(raw[64 * k:64 * k + 64, 1, :].rearrange("f (j d) -> f j d", d=D),
                   dram["W_down"].rearrange("(j k) f d -> k f j d", k=2)[k]) for k in range(2)]
        w1 = mem.enter_context(nc.sbuf_tensor("s_w1", [P, 4, P], F32))
        loads += [(w1[:, k, :], dram[name]) for k, name in enumerate(("Wq1", "Wk1", "Wv1", "Wo1"))]
        loads += [(cst[name][:], dram[name]) for name in ("dft", "idft_corr", "idft_conv")]
        loads += [(cst["bo1"][:], dram["bo1"].unsqueeze(0).to_broadcast([P, D]))]
        loads += [(cst[name][:], dram[name].unsqueeze(1)) for name in ("ln_gamma", "ln_beta")]
        mask_raw = mem.enter_context(nc.sbuf_tensor("s_mask", [S, P + 512], F32))
        loads += [(mask_raw[:, 0:P], dram["maskq"]), (mask_raw[:, P:], dram["maskk"])]
        wt_raw = mem.enter_context(nc.sbuf_tensor("s_wt", [P, D], F32))
        loads += [(wt_raw[:], dram["wt"])]
        wabs = mem.enter_context(nc.sbuf_tensor("s_wabs", [P, 1], F32))
        wrec = mem.enter_context(nc.sbuf_tensor("s_wrec", [P, 1], F32))
        pw = mem.enter_context(nc.psum_tensor("s_pw", [P, 4, P], F32))
        w_turned = sem("s_w_turned")
        w_chain = sem("s_w_chain")
        zeroed = sem("s_zeroed")
        high = sem("s_high")
        shared_loads = [(cst["fbias"][64 * b:64 * b + 1, k, :], dram[name].unsqueeze(0))
                        for b in range(2) for k, name in ((0, "bq1"), (1, "bk1"), (3, "bv1"))]
        shared_loads += [(shared[:, 0, 0:FH], dram["Ws_up"]), (shared[0:FH, 1, :], dram["Ws_down"])]
        with nc.Block() as block:
            @block.gpsimd
            def _(pool):
                nc.gpsimd.memset(cst["fbias"][:], 0.0).then_inc(zeroed, 1)
                nc.gpsimd.memset(shared[:], 0.0).then_inc(zeroed, 1)

            @block.scalar
            def _(act):
                act.wait_ge(landed, 16 * (len(loads) + len(shared_loads)))
                for k, name in enumerate(("wuh", "wdh")):
                    nc.scalar.copy(cst[name][:, 0:E // 2 * P], raw[:, k, :])
                    nc.scalar.copy(cst[name][:, E // 2 * P:], shared[:, k, :]).then_inc(high, 1)

            @block.sync
            def _(sp):
                with nc.allow_non_contiguous_dma("biases by column, 128 words each"):
                    for dst, src in loads:
                        sp.dma_start(dst, src).then_inc(landed, 16)
                    sp.wait_ge(zeroed, 2)
                    for dst, src in shared_loads:
                        sp.dma_start(dst, src).then_inc(landed, 16)

            @block.vector
            def _(dve):
                nc.vector.memset(cst["mhalf"][:], -0.5)
                nc.vector.memset(cst["ones"][:], 1.0)
                nc.vector.memset(onerow[:], 1.0).then_inc(made, 1)
                dve.wait_ge(landed, 16 * (len(loads) + len(shared_loads)))
                nc.vector.tensor_copy(cst["maskq"][:], mask_raw[:, 0:P])
                nc.vector.tensor_copy(cst["maskk"][:], mask_raw[:, P:])
                nc.vector.tensor_scalar(cst["bqs"][:], cst["bqH"][:], float(HD) ** -0.5, None, ALU.mult)
                nc.vector.tensor_copy(bqB[:], bqc[:].to_broadcast([P, P])).then_inc(made, 1)
                for k, name in enumerate(("wuh", "wdh")):
                    low = cst["wul" if k == 0 else "wdl"]
                    dve.wait_ge(high, k + 1)
                    nc.vector.tensor_tensor(low[:, 0:E // 2 * P], raw[:, k, :], cst[name][:, 0:E // 2 * P].bitcast(F32), ALU.subtract)
                    nc.vector.tensor_tensor(low[:, E // 2 * P:], shared[:, k, :], cst[name][:, E // 2 * P:].bitcast(F32), ALU.subtract)
                dve.wait_ge(bias, 1)
                nc.vector.tensor_copy(cst["centT"][:], pbias[:, P:P + E]).then_inc(done, 1)
                nc.vector.tensor_copy(cst["boe"][:], pbias[:, 0:P]).then_inc(done, 1)
                nc.vector.tensor_scalar(cst["fbias"][:], cst["fbias"][:], float(S), None, ALU.mult)
                dve.wait_ge(w_turned, 1)
                nc.vector.tensor_copy(cst["w1T"][:], pw[:]).then_inc(done, 1)
                nc.vector.tensor_reduce(wabs[:], wt_raw[:], AX.X, ALU.add, apply_absolute_value=True).then_inc(w_chain, 1)
                dve.wait_ge(w_turned, 2)
                nc.vector.tensor_scalar(cst["beta"][:], pbias[:, 256:257], 1.0 / (D * D), None, ALU.mult).then_inc(w_chain, 1)
                dve.wait_ge(w_chain, 2)
                nc.vector.tensor_scalar(wrec[:], cst["beta"][:], 1e-5, None, ALU.add).then_inc(w_chain, 1)
                dve.wait_ge(w_chain, 3)
                nc.vector.reciprocal(wabs[:], wrec[:]).then_inc(w_chain, 1)
                dve.wait_ge(w_chain, 4)
                nc.vector.tensor_scalar(cst["wt"][:], wt_raw[:], wabs[:], 1.5 * 2 ** 23, ALU.mult, ALU.add).then_inc(w_chain, 1)
                dve.wait_ge(w_chain, 5)
                nc.vector.tensor_scalar(cst["wt"][:], cst["wt"][:], 1.5 * 2 ** 23, 1.0, ALU.subtract, ALU.min).then_inc(w_chain, 1)
                dve.wait_ge(w_chain, 6)
                nc.vector.tensor_scalar(cst["wt"][:], cst["wt"][:], -1.0, None, ALU.max).then_inc(done, 1)
                dve.wait_ge(done, 4)

            @block.tensor
            def _(pe):
                pe.wait_ge(made, 2)
                pe.wait_ge(landed, 16 * (len(loads) + len(shared_loads)))
                nc.tensor.transpose(pbias[:, P:P + E], cent[:], cst["ident"][0:E, 0:E])
                nc.tensor.matmul(pbias[:, 0:P], bqB[:], cst["Wo"][:], start=True, stop=False)
                nc.tensor.matmul(pbias[:, 0:P], onerow[:], borow[:], start=False, stop=True).then_inc(bias, 1)

                for k in range(4):
                    ins = nc.tensor.transpose(pw[:, k, :], w1[:, k, :], cst["ident"][:])
                ins.then_inc(w_turned, 1)
                pe.wait_ge(w_chain, 1)
                pe.wait_ge(done, 3)
                nc.tensor.matmul(pbias[:, 256:257], cst["ones"][:], wabs[:], start=True, stop=True).then_inc(w_turned, 1)


def attention(nc, cst, x, ctx, x_res, sem, n_tiles=TILES):
    with ExitStack() as mem:
        def sb(name, shape, dt=F32):
            return mem.enter_context(nc.sbuf_tensor(name, shape, dt))

        def psum(name, shape, dt=F32):
            return mem.enter_context(nc.psum_tensor(name, shape, dt))

        cin = sb("cin", [P, 4, D])
        st = sb("a_stats", [P, 2, 6])
        mv = sb("a_mv", [P, 2, 2])
        ve = sb("a_ve", [P, 2, 1])
        rstd = sb("a_rstd", [P, 2, 1])
        xn = sb("a_xn", [P, 2, D])
        xcT = sb("xcT", [P, 2, 2, 2, S])
        qb = sb("qb", [P, 2, 2, 2, S])
        kraw = sb("kraw", [P, 2, 2, S])
        kx = sb("kx", [P, 2, 2, 8, S])
        vx = sb("vx", [P, 4, 8, 2, 2, 9])
        sub = sb("sub", [P, 2, H, S])
        prob = sb("prob", [P, 2, H, S])
        pT = sb("pT", [P, 2, 8, P])
        mx = sb("mx", [P, 2, H])
        rden = sb("rden", [P, 2, H])
        o = sb("o", [P, 2, H, HD])
        oT = sb("oT", [P, 2, P])

        pt_in = psum("pt_in", [P, 4, P])
        pj = psum("pj", [P, 4, P])
        ps = psum("ps", [P, H, S])
        ppT = psum("ppT", [P, 8, P])
        po = psum("po", [P, 512])[:, 0:288].rearrange("p (j b c d) -> p j b c d", j=8, b=2, c=2)
        pb = psum("pb", [P, 4, P])

        loaded = [sem(f"a_loaded{r}") for r in range(4)]
        stats = sem("a_stats_done")
        mean_var = sem("a_mean_var")
        rstd_done = sem("a_rstd_done")
        normed = sem("a_normed")
        biased = sem("a_biased")
        turned = sem("a_turned")
        turned_out = sem("a_turned_out")
        projected = sem("a_projected")
        split_out = sem("a_split_out")
        keys = sem("a_keys")
        scored = sem("a_scored")
        maxed = sem("a_maxed")
        shifted = sem("a_shifted")
        exped = sem("a_exped")
        p_turned = sem("a_p_turned")
        p_out = sem("a_p_out")
        weighed = sem("a_weighed")
        recip = sem("a_recip")
        scaled = sem("a_scaled")
        o_turned = sem("a_o_turned")
        o_out = sem("a_o_out")
        wo_done = sem("a_wo_done")
        added = sem("a_added")
        preset = sem("a_preset")
        idle = {e: sem(f"a_idle_{e}") for e in ("dve", "sp", "pool")}

        with nc.Block() as block:
            @block.sync
            def _(sp):
                def step(t, r):
                    if not live(t, 0, n_tiles):
                        return
                    wait_apart(sp, turned, t - 3, idle["sp"])
                    wait_apart(sp, stats, 2 * (t - 3), idle["sp"])
                    sp.dma_start(x_res[:, bass.ds(t, 1), :], x[bass.ds(t, 1)].rearrange("a p d -> p a d")).then_inc(loaded[r], 16)
                    sp.dma_start(cin[:, r:r + 1, :], ctx[bass.ds(t, 1)].rearrange("a p d -> p a d")).then_inc(loaded[r], 16)
                pipeline(sp, n_tiles, 5, 4, step)

            @block.vector
            def _(dve):
                def stats_of(t, r):
                    at_least(dve, loaded[r], t // 4 * 32 + 32 if isinstance(t, int) else (t - r) * 8 + 32)
                    wait_apart(dve, rstd_done, 2 * (t - 1), idle["dve"])
                    nc.vector.bn_stats(st[:, r % 2, :], x_res[:, bass.ds(t, 1), :]).then_inc(stats, 1)
                    wait_apart(dve, stats, 2 * t + 1, idle["dve"])
                    nc.vector.bn_aggr(mv[:, r % 2, :], st[:, r % 2, :]).then_inc(stats, 1)

                def norm(t, r):
                    at_least(dve, rstd_done, 2 * t + 2)
                    at_least(dve, turned, t - 1)
                    nc.vector.tensor_scalar(xn[:, r % 2, :], x_res[:, bass.ds(t, 1), :], mv[:, r % 2, 0:1],
                                            rstd[:, r % 2, :], ALU.subtract, ALU.mult).then_inc(normed, 1)

                def row_max(t, r):
                    at_least(dve, scored, t + 1)
                    nc.vector.tensor_reduce(mx[:, r % 2, :], ps[:], AX.X, ALU.max).then_inc(maxed, 1)
                    at_least(dve, maxed, t + 1)
                    at_least(dve, exped, t - 1)
                    nc.vector.tensor_tensor(sub[:, r % 2], ps[:], mx[:, r % 2, :].unsqueeze(2).to_broadcast([P, H, S]),
                                            ALU.subtract).then_inc(shifted, 1)

                def expand_keys(t, r):
                    at_least(dve, split_out, t + 1)
                    at_least(dve, scored, t - 1)
                    for h in range(2):
                        ins = nc.vector.scalar_tensor_tensor(
                            kx[:, r % 2, h], kraw[:, r % 2, h, :].unsqueeze(1).to_broadcast([P, 8, S]), cst["bqH"][:, h:h + 1],
                            cst["hmask"][:].unsqueeze(2).to_broadcast([P, 8, S]), ALU.add, ALU.mult)
                    ins.then_inc(keys, 1)

                def scale_out(t, r):
                    at_least(dve, weighed, t + 1)
                    for b in range(2):
                        q = slice(64 * b, 64 * b + 64)
                        ins = nc.vector.reciprocal(rden[q, r % 2, :].rearrange("p (a c) -> p a c", c=2), po[q, :, b, :, 8])
                    ins.then_inc(recip, 1)
                    at_least(dve, recip, t + 1)
                    at_least(dve, o_turned, t - 1)
                    for b in range(2):
                        q = slice(64 * b, 64 * b + 64)
                        ins = nc.vector.tensor_tensor(
                            o[q, r % 2].rearrange("p (a c) d -> p a c d", c=2), po[q, :, b, :, 0:8],
                            rden[q, r % 2, :].rearrange("p (a c) -> p a c", c=2).unsqueeze(3).to_broadcast([64, 8, 2, 8]),
                            ALU.mult)
                    ins.then_inc(scaled, 1)

                def add_out(t, r):
                    at_least(dve, wo_done, t + 1)
                    at_least(dve, biased, t + 1)
                    nc.vector.tensor_tensor(x_res[:, bass.ds(t, 1), :], x_res[:, bass.ds(t, 1), :], pb[:, 1:2, :],
                                            ALU.add).then_inc(added, 1)

                def step(t, r):
                    if live(t, 0, n_tiles):
                        stats_of(t, r)
                    if live(t, 2, n_tiles):
                        row_max(t - 2, r + 2)
                    if live(t, 0, n_tiles):
                        norm(t, r)
                    if live(t, 1, n_tiles):
                        expand_keys(t - 1, r + 3)
                    if live(t, 3, n_tiles):
                        scale_out(t - 3, r + 1)
                    if live(t, 4, n_tiles):
                        add_out(t - 4, r)
                pipeline(dve, n_tiles, 5, 4, step)

            @block.gpsimd
            def _(pool):
                nc.gpsimd.memset(qb[:], 0.0).then_inc(preset, 1)
                nc.gpsimd.memset(vx[:], 0.0).then_inc(preset, 1)
                pool.wait_ge(preset, 2)
                for d in range(2):
                    nc.gpsimd.memset(vx[64 * d:64 * d + 64, :, :, :, d, 8], 1.0).then_inc(preset, 1)

                pool.wait_ge(preset, 4)

                def step(t, r):
                    if live(t, 0, n_tiles):
                        at_least(pool, stats, 2 * t + 2)
                        wait_apart(pool, normed, t - 1, idle["pool"])
                        nc.gpsimd.tensor_scalar(ve[:, r % 2, :], mv[:, r % 2, 1:2], 1e-5, None, ALU.add).then_inc(rstd_done, 1)
                        at_least(pool, rstd_done, 2 * t + 1)
                        nc.gpsimd.tensor_tensor(rstd[:, r % 2, :], ve[:, r % 2, :], cst["mhalf"][:], ALU.pow).then_inc(rstd_done, 1)
                    if live(t, 1, n_tiles):
                        at_least(pool, normed, t)
                        nc.gpsimd.tensor_tensor(x_res[:, bass.ds(t - 1, 1), :], x_res[:, bass.ds(t - 1, 1), :],
                                                cst["boe"][:].unsqueeze(1), ALU.add).then_inc(biased, 1)
                pipeline(pool, n_tiles, 5, 4, step)

            @block.scalar
            def _(act):
                act.wait_ge(preset, 4)

                def probs_out(t, r):
                    at_least(act, p_turned, t + 1)
                    at_least(act, weighed, t - 1)
                    nc.scalar.copy(pT[:, r % 2], ppT[:]).then_inc(p_out, 1)

                def turned_copy(t, r):
                    at_least(act, turned, t + 1)
                    at_least(act, projected, t - 1)
                    nc.scalar.copy(xcT[:, r % 2].rearrange("p b c s -> p c b s"),
                                   pt_in[:, 0:2, :].rearrange("p c (b s) -> p c b s", b=2)).then_inc(turned_out, 1)

                def o_copy(t, r):
                    at_least(act, o_turned, t + 1)
                    at_least(act, wo_done, t - 1)
                    nc.scalar.copy(oT[:, r % 2], pb[:, 0, :]).then_inc(o_out, 1)

                def split(t, r):
                    at_least(act, projected, t + 1)
                    at_least(act, scored, t - 1)
                    at_least(act, keys, t - 1)
                    at_least(act, weighed, t - 3)
                    for b in range(2):
                        q = slice(64 * b, 64 * b + 64)
                        for h in range(2):
                            nc.scalar.activation(qb[q, r % 2, h, b, :], pj[q, h, 0:64], ACT.Identity,
                                                 bias=cst["bqs"][q, h:h + 1], scale=float(HD) ** -0.5)
                        for d in range(2):
                            nc.scalar.copy(vx[64 * d:64 * d + 64, r % 4, :, b, d, 0:8],
                                           pj[q, 2, :].rearrange("p (a c d) -> p a c d", c=2, d=8)[:, :, d, :])
                    nc.scalar.copy(kraw[:, r % 2], pj[:, 0:2, 64:128]).then_inc(split_out, 1)

                def exponent(t, r):
                    at_least(act, shifted, t + 1)
                    at_least(act, p_turned, t - 1)
                    nc.scalar.activation(prob[:, r % 2], sub[:, r % 2], ACT.Exp).then_inc(exped, 1)

                def step(t, r):
                    if live(t, 3, n_tiles):
                        probs_out(t - 3, r + 1)
                    if live(t, 1, n_tiles):
                        turned_copy(t - 1, r + 3)
                    if live(t, 4, n_tiles):
                        o_copy(t - 4, r)
                    if live(t, 1, n_tiles):
                        split(t - 1, r + 3)
                    if live(t, 2, n_tiles):
                        exponent(t - 2, r + 2)
                pipeline(act, n_tiles, 5, 4, step)

            @block.tensor
            def _(pe):
                def scores(t, r):
                    at_least(pe, keys, t + 1)
                    at_least(pe, split_out, t + 1)
                    at_least(pe, shifted, t)
                    for h in range(2):
                        out = ps[:, 8 * h:8 * h + 8, :]
                        nc.tensor.matmul(out, cst["maskq"][:], cst["maskk"][:], start=True, stop=False)
                        ins = nc.tensor.matmul(out, qb[:, r % 2, h].rearrange("p b q -> p (b q)"), kx[:, r % 2, h],
                                               start=False, stop=True)
                    ins.then_inc(scored, 1)

                def turn_probs(t, r):
                    at_least(pe, exped, t + 1)
                    at_least(pe, p_out, t)
                    for j in range(8):
                        ins = nc.tensor.transpose(ppT[:, j, :], prob[:, r % 2, 2 * j:2 * j + 2].rearrange("p a k -> p (a k)"),
                                                  cst["ident"][:])
                    ins.then_inc(p_turned, 1)

                def turn_in(t, r):
                    at_least(pe, normed, t + 1)
                    at_least(pe, loaded[r % 4], (t // 4) * 32 + 32 if isinstance(t, int) else (t - r % 4) * 8 + 32)
                    at_least(pe, turned_out, t)
                    nc.tensor.transpose(pt_in[:, 0, :], xn[:, r % 2, :], cst["ident"][:])
                    nc.tensor.transpose(pt_in[:, 1, :], cin[:, r % 4, :], cst["ident"][:]).then_inc(turned, 1)

                def turn_o(t, r):
                    at_least(pe, scaled, t + 1)
                    at_least(pe, added, t)
                    nc.tensor.transpose(pb[:, 0, :], o[:, r % 2].rearrange("p h d -> p (h d)"), cst["ident"][:]).then_inc(o_turned, 1)

                def project(t, r):
                    at_least(pe, turned_out, t + 1)
                    at_least(pe, split_out, t)
                    for b in range(2):
                        for h in range(2):
                            nc.tensor.matmul(pj[64 * b:64 * b + 64, h, :], cst["Wq"][:, 64 * h:64 * h + 64],
                                             xcT[:, r % 2, b].rearrange("p c s -> p (c s)"), start=True, stop=True)
                    for b in range(2):
                        ins = nc.tensor.matmul(pj[64 * b:64 * b + 64, 2, :], xcT[:, r % 2, b, 1, :], cst["Wq"][:],
                                               start=True, stop=True)
                    ins.then_inc(projected, 1)

                def weigh(t, r):
                    at_least(pe, p_out, t + 1)
                    at_least(pe, scaled, t)
                    for j in range(8):
                        ins = nc.tensor.matmul(po[:, j], pT[:, r % 2, j, :], vx[:, r % 4, j], start=True, stop=True)
                    ins.then_inc(weighed, 1)

                def out_project(t, r):
                    at_least(pe, o_out, t + 1)
                    nc.tensor.matmul(pb[:, 1, :], oT[:, r % 2], cst["Wo"][:], start=True, stop=True).then_inc(wo_done, 1)

                def step(t, r):
                    if live(t, 2, n_tiles):
                        scores(t - 2, r + 2)
                    if live(t, 3, n_tiles):
                        turn_probs(t - 3, r + 1)
                    if live(t, 1, n_tiles):
                        turn_in(t - 1, r + 3)
                    if live(t, 4, n_tiles):
                        turn_o(t - 4, r)
                    if live(t, 1, n_tiles):
                        project(t - 1, r + 3)
                    if live(t, 3, n_tiles):
                        weigh(t - 3, r + 1)
                    if live(t, 4, n_tiles):
                        out_project(t - 4, r)
                pipeline(pe, n_tiles, 5, 4, step)


def router(nc, cst, x_res, xnT, cwT, sem, groups=TILES // 4):
    with ExitStack() as mem:
        def sb(name, shape, dt=F32):
            return mem.enter_context(nc.sbuf_tensor(name, shape, dt))

        def psum(name, shape, dt=F32):
            return mem.enter_context(nc.psum_tensor(name, shape, dt))

        st = sb("r_st", [P, 2, 4, 6])
        mv = sb("r_mv", [P, 2, 4, 2])
        ve = sb("r_ve", [P, 2, 4])
        rstd = sb("r_rstd", [P, 2, 4])
        xn = sb("r_xn", [P, 2, 4, D])
        xs = sb("r_xs", [P, 2, 4, P])
        aff = sb("r_aff", [P, 2, 4, E])
        en = sb("r_en", [P, 2, 4, E])
        biased = sb("r_biased", [P, 4, E])
        m8 = sb("r_m8", [P, 4, TOP])
        rep = sb("r_rep", [P, 4, E])
        chosen = sb("r_chosen", [P, 4, E])
        gate = sb("r_gate", [P, 4, E])
        w = sb("r_w", [P, 4, E])
        wsum = sb("r_wsum", [P, 4])
        wrec = sb("r_wrec", [P, 4])
        cw = sb("r_cw", [P, 4, E])
        cwp = sb("r_cwp", [P, 2, 4, 2, E], F16)
        pt = psum("r_pt", [P, 4, P])
        pa = psum("r_pa", [P, 512])[:, 0:4 * E].rearrange("p (t e) -> p t e", t=4)
        pc = psum("r_pc", [P, 1024], F16)[:, 0:512].rearrange("p (t e) -> p t e", t=4)

        stats = sem("r_stats")
        rstd_done = sem("r_rstd")
        normed = sem("r_normed")
        turned = sem("r_turned")
        turned_out = sem("r_turned_out")
        kept = sem("r_kept")
        affine = sem("r_affine")
        exped = sem("r_exped")
        chain = sem("r_chain")
        gates = sem("r_gates")
        g_turned = sem("r_g_turned")
        g_out = sem("r_g_out")
        idle = {e: sem(f"r_idle_{e}") for e in ("dve", "pool", "act")}

        with nc.Block() as block:
            @block.vector
            def _(dve):
                def stats_of(g, r):
                    wait_apart(dve, rstd_done, 2 * (g - 1), idle["dve"])
                    for j in range(4):
                        ins = nc.vector.bn_stats(st[:, r, j, :], x_res[:, bass.ds(g * 4 + j, 1), :])
                    ins.then_inc(stats, 1)
                    wait_apart(dve, stats, 2 * g + 1, idle["dve"])
                    for j in range(4):
                        ins = nc.vector.bn_aggr(mv[:, r, j, :], st[:, r, j, :])
                    ins.then_inc(stats, 1)

                def norm(g, r):
                    at_least(dve, rstd_done, 2 * g + 2)
                    at_least(dve, turned, g - 1)
                    for j in range(4):
                        ins = nc.vector.tensor_scalar(xn[:, r, j, :], x_res[:, bass.ds(g * 4 + j, 1), :], mv[:, r, j, 0:1],
                                                      rstd[:, r, j:j + 1], ALU.subtract, ALU.mult)
                    ins.then_inc(normed, 1)

                def gates_of(g, r):
                    at_least(dve, exped, g + 1)

                    def then(ins, n):
                        ins.then_inc(chain, 1)
                        wait_apart(dve, chain, g * 10 + n, idle["dve"])
                    then(nc.vector.tensor_tensor(biased[:], aff[:, r], cst["eb"][:].unsqueeze(1).to_broadcast([P, 4, E]), ALU.add), 1)
                    for j in range(4):
                        ins = nc.vector.max(out=m8[:, j, :], in_=biased[:, j, :])
                    then(ins, 2)
                    for j in range(4):
                        nc.vector.match_replace(out=rep[:, j, :], in_to_replace=m8[:, j, :], in_values=biased[:, j, :],
                                                imm_value=-SENTINEL)
                    then(nc.vector.tensor_scalar(en[:, r], en[:, r], 1.0, None, ALU.add), 3)
                    nc.vector.tensor_tensor(chosen[:], rep[:], biased[:], ALU.not_equal)
                    then(nc.vector.reciprocal(gate[:], en[:, r]), 4)
                    then(nc.vector.tensor_tensor(w[:], gate[:], chosen[:], ALU.mult), 5)
                    then(nc.vector.tensor_reduce(wsum[:], w[:], AX.X, ALU.add), 6)
                    then(nc.vector.tensor_scalar(wsum[:], wsum[:], 1e-8, None, ALU.add), 7)
                    then(nc.vector.reciprocal(wrec[:], wsum[:]), 8)
                    at_least(dve, g_turned, g - 1)
                    then(nc.vector.tensor_tensor(cw[:], w[:], wrec[:].unsqueeze(2).to_broadcast([P, 4, E]), ALU.mult), 9)
                    then(nc.vector.tensor_copy(cwp[:, r, :, 0, :], cw[:]), 10)
                    nc.vector.tensor_tensor(cwp[:, r, :, 1, :], cw[:], cwp[:, r, :, 0, :], ALU.subtract).then_inc(gates, 1)

                def step(g, r):
                    if live(g, 0, groups):
                        stats_of(g, r)
                    if live(g, 2, groups):
                        gates_of(g - 2, r)
                    if live(g, 0, groups):
                        norm(g, r)
                pipeline(dve, groups, 6, 2, step)

            @block.gpsimd
            def _(pool):
                def step(g, r):
                    if live(g, 1, groups):
                        wait_apart(pool, turned_out, g, idle["pool"])
                        nc.gpsimd.tensor_copy(xnT[:, bass.ds((g - 1) * 512, 512)], xs[:, 1 - r].rearrange("p j t -> p (j t)")).then_inc(kept, 1)
                    if live(g, 0, groups):
                        wait_apart(pool, normed, g - 1, idle["pool"])
                        wait_apart(pool, stats, 2 * g + 2, idle["pool"])
                        nc.gpsimd.tensor_scalar(ve[:, r, :], mv[:, r, :, 1], 1e-5, None, ALU.add).then_inc(rstd_done, 1)
                        at_least(pool, rstd_done, 2 * g + 1)
                        nc.gpsimd.tensor_tensor(rstd[:, r, :], ve[:, r, :], cst["mhalf"][:].to_broadcast([P, 4]), ALU.pow).then_inc(rstd_done, 1)
                pipeline(pool, groups, 6, 2, step)

            @block.scalar
            def _(act):
                def step(g, r):
                    if live(g, 3, groups):
                        wait_apart(act, g_turned, g - 2, idle["act"])
                        nc.scalar.copy(cwT[:, bass.ds((g - 3) * 512, 512)], pc.rearrange("p t e -> p (t e)")).then_inc(g_out, 1)
                    if live(g, 1, groups):
                        at_least(act, turned, g)
                        at_least(act, kept, g - 2)
                        at_least(act, affine, g - 2)
                        nc.scalar.copy(xs[:, 1 - r], pt[:]).then_inc(turned_out, 1)
                        at_least(act, affine, g)
                        at_least(act, gates, g - 2)
                        nc.scalar.copy(aff[:, 1 - r], pa)
                        nc.scalar.activation(en[:, 1 - r], pa, ACT.Exp, scale=-1.0).then_inc(exped, 1)
                pipeline(act, groups, 6, 2, step)

            @block.tensor
            def _(pe):
                def step(g, r):
                    if live(g, 3, groups):
                        at_least(pe, gates, g - 2)
                        at_least(pe, g_out, g - 3)
                        for j in range(4):
                            ins = nc.tensor.transpose(pc[:, j, :], cwp[:, 1 - r, j].rearrange("p a e -> p (a e)"), cst["ident16"][:])
                        ins.then_inc(g_turned, 1)
                    if live(g, 1, groups):
                        at_least(pe, normed, g)
                        at_least(pe, turned_out, g - 1)
                        for j in range(4):
                            ins = nc.tensor.transpose(pt[:, j, :], xn[:, 1 - r, j, :], cst["ident"][:])
                        ins.then_inc(turned, 1)
                        at_least(pe, turned_out, g)
                        at_least(pe, exped, g - 1)
                        for j in range(4):
                            ins = nc.tensor.matmul(pa[:, j, :], xs[:, 1 - r, j, :], cst["centT"][:], start=True, stop=True)
                        ins.then_inc(affine, 1)
                pipeline(pe, groups, 6, 2, step)


def experts(nc, cst, dram, x_res, xnT, cwT, sem, chunks=TILES // 4):
    turns = chunks * PAIRS
    with ExitStack() as mem:
        def sb(name, shape, dt=F32):
            return mem.enter_context(nc.sbuf_tensor(name, shape, dt))

        def psum(name, shape, dt=F32):
            return mem.enter_context(nc.psum_tensor(name, shape, dt))

        sel = sb("e_sel", [P, (PAIRS - 1) * P], F16)
        xh = sb("e_xh", [P, 2, 512], F32R)
        xl = sb("e_xl", [P, 2, 512], F32R)
        s = sb("e_s", [P, 3, 512])
        m = sb("e_m", [P, 3, 512])
        mh = sb("e_mh", [P, 3, 512], F32R)
        ml = sb("e_ml", [P, 3, 512], F32R)
        yT = sb("e_yT", [P, 512])
        pu = [psum(f"e_pu{i}", [P, 512]) for i in range(3)]
        pg = [psum(f"e_pg{i}", [P, 512]) for i in range(2)]
        py = [psum(f"e_py{i}", [P, 512]) for i in range(2)]
        pt = psum("e_pt", [P, 4, P])

        landed = sem("e_landed")
        x_high = sem("e_x_high")
        x_low = sem("e_x_low")
        up_done = sem("e_up")
        gate_done = sem("e_gate")
        silued = sem("e_silu")
        gated = sem("e_gated")
        m_high = sem("e_m_high")
        m_low = sem("e_m_low")
        down_done = sem("e_down")
        y_out = sem("e_y_out")
        y_turned = sem("e_y_turned")
        y_added = sem("e_y_added")
        idle = sem("e_idle")

        def drive(eng, step):
            unroll = 2 * PAIRS
            for n in range(unroll):
                step(n, n, lambda lag, n=n: (n - lag) // PAIRS)
            with eng.Fori(1, turns // unroll) as g:
                for r in range(unroll):
                    step(g * unroll + r, r, lambda lag, g=g, r=r: g * 2 + (r - lag) // PAIRS)
            for n in range(turns, turns + 9):
                step(n, n % unroll, lambda lag, n=n: (n - lag) // PAIRS)

        padded = sem("e_padded")

        with nc.Block() as block:
            @block.gpsimd
            def _(pool):
                nc.gpsimd.memset(xnT[:, chunks * 512:chunks * 512 + 512], 0.0).then_inc(padded, 1)

            @block.sync
            def _(sp):
                sp.dma_start(sel[:], dram["sel"]).then_inc(landed, 16)

            @block.vector
            def _(dve):
                def low_part(c, b):
                    at_least(dve, x_high, c + 1)
                    nc.vector.tensor_tensor(xl[:, b, :], xnT[:, bass.ds(c * 512, 512)], xh[:, b, :].bitcast(F32),
                                            ALU.subtract).then_inc(x_low, 1)

                def step(n, r, chunk):
                    if isinstance(n, int) and n == 0:
                        dve.wait_ge(padded, 1)
                        low_part(0, 0)
                    if live(n, 0, turns):
                        pair = r % PAIRS
                        at_least(dve, silued, n + 1)
                        at_least(dve, m_low, n - 2)
                        if pair < PAIRS - 1:
                            at_least(dve, gate_done, chunk(0) * (PAIRS - 1) + pair + 1)
                            ins = nc.vector.tensor_tensor(m[:, r % 3, :], s[:, r % 3, :], pg[r % 2][:], ALU.mult)
                        else:
                            ins = nc.vector.tensor_scalar(m[:, r % 3, :], s[:, r % 3, :], 1.0, None, ALU.mult)
                        ins.then_inc(gated, 1)
                    if live(n, 1, turns):
                        at_least(dve, m_high, n)
                        at_least(dve, down_done, n - 3)
                        nc.vector.tensor_tensor(ml[:, (r - 1) % 3, :], m[:, (r - 1) % 3, :], mh[:, (r - 1) % 3, :].bitcast(F32),
                                                ALU.subtract).then_inc(m_low, 1)
                    if live(n, 0, turns) and r % PAIRS == 10:
                        low_part(chunk(0) + 1, (r // PAIRS + 1) % 2)
                    if live(n, 8, turns) and (r - 8) % PAIRS == PAIRS - 1:
                        c = chunk(8)
                        at_least(dve, y_turned, c + 1)
                        nc.vector.tensor_tensor(x_res[:, bass.ds(c * 4, 4), :], x_res[:, bass.ds(c * 4, 4), :], pt[:],
                                                ALU.add).then_inc(y_added, 1)
                drive(dve, step)

            @block.scalar
            def _(act):
                def high_part(c, b):
                    wait_apart(act, up_done, (c - 1) * PAIRS, idle)
                    nc.scalar.copy(xh[:, b, :], xnT[:, bass.ds(c * 512, 512)]).then_inc(x_high, 1)

                def step(n, r, chunk):
                    if isinstance(n, int) and n == 0:
                        act.wait_ge(padded, 1)
                        high_part(0, 0)
                    if live(n, 0, turns):
                        at_least(act, up_done, n + 1)
                        at_least(act, gated, n - 2)
                        nc.scalar.activation(s[:, r % 3, :], pu[r % 3][:], ACT.Silu).then_inc(silued, 1)
                    if live(n, 1, turns):
                        at_least(act, gated, n)
                        at_least(act, down_done, n - 3)
                        nc.scalar.copy(mh[:, (r - 1) % 3, :], m[:, (r - 1) % 3, :]).then_inc(m_high, 1)
                    if live(n, 0, turns) and r % PAIRS == 10:
                        high_part(chunk(0) + 1, (r // PAIRS + 1) % 2)
                    if live(n, 4, turns) and (r - 4) % PAIRS == PAIRS - 1:
                        c = chunk(4)
                        at_least(act, down_done, (c + 1) * PAIRS)
                        at_least(act, y_turned, c)
                        nc.scalar.copy(yT[:], py[((r - 4) // PAIRS) % 2][:]).then_inc(y_out, 1)
                drive(act, step)

            @block.tensor
            def _(pe):
                pe.wait_ge(landed, 16)

                def step(n, r, chunk):
                    pair = r % PAIRS
                    w = slice(pair * P, pair * P + P)
                    if live(n, 0, turns):
                        b = (r // PAIRS) % 2
                        at_least(pe, x_low, chunk(0) + 1)
                        at_least(pe, silued, n - 2)
                        nc.tensor.matmul(pu[r % 3][:], cst["wuh"][:, w], xh[:, b, :], start=True, stop=False)
                        nc.tensor.matmul(pu[r % 3][:], cst["wul"][:, w], xh[:, b, :], start=False, stop=False)
                        nc.tensor.matmul(pu[r % 3][:], cst["wuh"][:, w], xl[:, b, :], start=False, stop=True).then_inc(up_done, 1)
                        if pair < PAIRS - 1:
                            at_least(pe, gated, n - 1)
                            nc.tensor.matmul(pg[r % 2][:], sel[:, w], cwT[:, bass.ds(chunk(0) * 512, 512)],
                                             start=True, stop=True).then_inc(gate_done, 1)
                    if live(n, 3, turns):
                        pd = (r - 3) % PAIRS
                        w = slice(pd * P, pd * P + P)
                        k = (r - 3) % 3
                        out = py[((r - 3) // PAIRS) % 2][:]
                        at_least(pe, m_low, n - 2)
                        if pd == 0:
                            at_least(pe, y_out, chunk(3) - 1)
                        nc.tensor.matmul(out, cst["wdh"][:, w], mh[:, k, :], start=(pd == 0), stop=False)
                        nc.tensor.matmul(out, cst["wdl"][:, w], mh[:, k, :], start=False, stop=False)
                        nc.tensor.matmul(out, cst["wdh"][:, w], ml[:, k, :], start=False, stop=(pd == PAIRS - 1)).then_inc(down_done, 1)
                    if live(n, 6, turns) and (r - 6) % PAIRS == PAIRS - 1:
                        c = chunk(6)
                        at_least(pe, y_out, c + 1)
                        at_least(pe, y_added, c)
                        for j in range(4):
                            ins = nc.tensor.transpose(pt[:, j, :], yT[:, j * P:(j + 1) * P], cst["ident"][:])
                        ins.then_inc(y_turned, 1)
                drive(pe, step)


def dft_tables():
    f = np.concatenate([np.arange(S // 2 + 1), np.arange(1, S // 2)])
    second = np.arange(S) > S // 2
    angle = 2 * np.pi * np.outer(f, np.arange(S)) / S
    cos, sin = np.cos(angle), np.sin(angle)
    weight = np.where((f == 0) | (f == S // 2), 1.0, 2.0)[:, None] / S
    sign = np.where(second, -1.0, 1.0)[:, None]
    both = lambda m: np.kron(np.eye(2), m)
    return {
        "dft": np.concatenate([both(np.where(second[:, None], -sin, cos).T), both(np.where(second[:, None], cos, -sin).T)], 1),
        "idft_corr": np.concatenate([both(weight * cos), both(weight * sign * sin)], 1) / HD,
        "idft_conv": np.concatenate([both(weight * sign * cos), both(-weight * sin)], 1),
    }


def spectrum(nc, cst, ctx, x_res, vf, corr, sem, n_tiles=TILES):
    with ExitStack() as mem:
        def sb(name, shape, dt=F32):
            return mem.enter_context(nc.sbuf_tensor(name, shape, dt))

        def psum(name, shape, dt=F32):
            return mem.enter_context(nc.psum_tensor(name, shape, dt))

        cin = sb("c_cin", [P, 4, D])
        st = sb("c_st", [P, 2, 6])
        mv = sb("c_mv", [P, 2, 2])
        ve = sb("c_ve", [P, 2, 1])
        rstd = sb("c_rstd", [P, 2, 1])
        xn = sb("c_xn", [P, 2, D])
        xf = sb("c_xf", [P, 2, 3, P])
        qf = sb("c_qf", [P, 2, 3, D])
        pp = sb("c_pp", [P, 2, 2, D])
        pf = [psum(f"c_pf{i}", [P, 4, P]) for i in range(2)]
        pq = [psum(f"c_pq{i}", [P, 4, P]) for i in range(2)]
        pc = [psum(f"c_pc{i}", [P, 4, P]) for i in range(2)]

        loaded = [sem(f"c_loaded{r}") for r in range(4)]
        stats = sem("c_stats")
        rstd_done = sem("c_rstd")
        normed = sem("c_normed")
        transformed = sem("c_transformed")
        f_out = sem("c_f_out")
        projected = sem("c_projected")
        q_out = sem("c_q_out")
        products = sem("c_products")
        inverted = sem("c_inverted")
        summed = sem("c_summed")
        idle = {e: sem(f"c_idle_{e}") for e in ("dve", "sp", "pool")}

        with nc.Block() as block:
            @block.sync
            def _(sp):
                def step(t, r):
                    if live(t, 0, n_tiles):
                        wait_apart(sp, transformed, t - 3, idle["sp"])
                        sp.dma_start(cin[:, r:r + 1, :], ctx[bass.ds(t, 1)].rearrange("a p d -> p a d")).then_inc(loaded[r], 16)
                pipeline(sp, n_tiles, 5, 4, step)

            @block.vector
            def _(dve):
                def step(t, r):
                    p = r % 2
                    if live(t, 0, n_tiles):
                        wait_apart(dve, rstd_done, 2 * (t - 1), idle["dve"])
                        nc.vector.bn_stats(st[:, p, :], x_res[:, bass.ds(t, 1), :]).then_inc(stats, 1)
                        wait_apart(dve, stats, 2 * t + 1, idle["dve"])
                        nc.vector.bn_aggr(mv[:, p, :], st[:, p, :]).then_inc(stats, 1)
                    if live(t, 3, n_tiles):
                        wait_apart(dve, inverted, t - 2, idle["dve"])
                        nc.vector.tensor_reduce(corr[:, bass.ds(t - 3, 1), :], pc[1 - p][:, 0, :].rearrange("p (h d) -> p h d", d=HD),
                                                AX.X, ALU.add).then_inc(summed, 1)
                    if live(t, 1, n_tiles):
                        at_least(dve, projected, t)
                        at_least(dve, products, t - 2)
                        nc.vector.tensor_tensor(qf[:, 1 - p], pq[1 - p][:, 0:3, :], cst["fbias"][:, 0:3, :], ALU.add)
                        nc.vector.tensor_tensor(vf[:, bass.ds(t - 1, 1), :], pq[1 - p][:, 3:4, :], cst["fbias"][:, 3:4, :],
                                                ALU.add).then_inc(q_out, 1)
                    if live(t, 0, n_tiles):
                        at_least(dve, rstd_done, 2 * t + 2)
                        at_least(dve, transformed, t - 1)
                        nc.vector.tensor_scalar(xn[:, p, :], x_res[:, bass.ds(t, 1), :], mv[:, p, 0:1], rstd[:, p, :],
                                                ALU.subtract, ALU.mult).then_inc(normed, 1)
                pipeline(dve, n_tiles, 5, 4, step)

            @block.gpsimd
            def _(pool):
                def step(t, r):
                    p = r % 2
                    if live(t, 0, n_tiles):
                        wait_apart(pool, stats, 2 * t + 2, idle["pool"])
                        wait_apart(pool, normed, t - 1, idle["pool"])
                        nc.gpsimd.tensor_scalar(ve[:, p, :], mv[:, p, 1:2], 1e-5, None, ALU.add).then_inc(rstd_done, 1)
                        at_least(pool, rstd_done, 2 * t + 1)
                        nc.gpsimd.tensor_tensor(rstd[:, p, :], ve[:, p, :], cst["mhalf"][:], ALU.pow).then_inc(rstd_done, 1)
                    if live(t, 2, n_tiles):
                        at_least(pool, q_out, t - 1)
                        at_least(pool, inverted, t - 3)
                        nc.gpsimd.tensor_tensor(pp[:, p], qf[:, p, 0, :].unsqueeze(1).to_broadcast([P, 2, D]), qf[:, p, 1:3, :],
                                                ALU.mult).then_inc(products, 1)
                pipeline(pool, n_tiles, 5, 4, step)

            @block.scalar
            def _(act):
                def step(t, r):
                    p = r % 2
                    if live(t, 1, n_tiles):
                        at_least(act, transformed, t)
                        at_least(act, projected, t - 2)
                        nc.scalar.copy(xf[:, 1 - p], pf[1 - p][:, 0:3, :]).then_inc(f_out, 1)
                pipeline(act, n_tiles, 5, 4, step)

            @block.tensor
            def _(pe):
                def step(t, r):
                    p = r % 2
                    if live(t, 1, n_tiles):
                        u, q, k = t - 1, 1 - p, (r + 3) % 4
                        at_least(pe, normed, u + 1)
                        at_least(pe, loaded[k], (u // 4) * 16 + 16 if isinstance(t, int) else (u - k) * 4 + 16)
                        at_least(pe, f_out, u - 1)
                        nc.tensor.matmul(pf[q][:, 0, :], xn[:, q, :], cst["dft"][:, 0:P], start=True, stop=True)
                        nc.tensor.matmul(pf[q][:, 1:3, :], cin[:, k, :], cst["dft"][:], start=True, stop=True).then_inc(transformed, 1)
                    if live(t, 2, n_tiles):
                        u, q = t - 2, p
                        at_least(pe, products, u + 1)
                        at_least(pe, summed, u - 1)
                        for k in range(2):
                            ins = nc.tensor.matmul(pc[q][:, 0, :], cst["idft_corr"][:, k * P:k * P + P], pp[:, q, k, :],
                                                   start=(k == 0), stop=(k == 1))
                        ins.then_inc(inverted, 1)
                    if live(t, 1, n_tiles):
                        u, q = t - 1, 1 - p
                        at_least(pe, f_out, u + 1)
                        at_least(pe, q_out, u - 1)
                        for k, (src, w) in enumerate(((0, 0), (1, 1), (2, 1), (1, 2))):
                            ins = nc.tensor.matmul(pq[q][:, k, :], xf[:, q, src, :], cst["w1T"][:, w, :], start=True, stop=True)
                        ins.then_inc(projected, 1)
                pipeline(pe, n_tiles, 5, 4, step)


def delays(nc, cst, corr, cf, sem):
    G = TILES // 8
    with ExitStack() as mem:
        def sb(name, shape, dt=F32):
            return mem.enter_context(nc.sbuf_tensor(name, shape, dt))

        ext = sb("d_ext", [P, 2 * G, S + TOP - DELAYS])
        rep = sb("d_rep", [P, 2 * G, S + TOP - DELAYS])
        m8 = sb("d_m8", [P, 2 * G, TOP])
        e = sb("d_e", [P, 2 * G, S])
        w = sb("d_w", [P, 2 * G, S])
        wsum = sb("d_wsum", [P, 2 * G])
        cT = sb("d_cT", [P, G, P])
        pc = mem.enter_context(nc.psum_tensor("d_pc", [P, G, P], F32))
        pa = mem.enter_context(nc.psum_tensor("d_pa", [P, G, P], F32))
        pb = mem.enter_context(nc.psum_tensor("d_pb", [P, G, P], F32))
        turned = sem("d_turned")
        chain = sem("d_chain")
        shifted = sem("d_shifted")
        exped = sem("d_exped")
        weights = sem("d_weights")
        w_turned = sem("d_w_turned")
        w_out = sem("d_w_out")
        transformed = sem("d_transformed")

        with nc.Block() as block:
            @block.tensor
            def _(pe):
                for g in range(G):
                    ins = nc.tensor.transpose(pc[:, g, :], corr[:, 8 * g:8 * g + 8, :].rearrange("p t h -> p (t h)"), cst["ident"][:])
                ins.then_inc(turned, 1)
                pe.wait_ge(weights, 1)
                for g in range(G):
                    ins = nc.tensor.transpose(pc[:, g, :], w[:, 2 * g:2 * g + 2, :].rearrange("p b d -> p (b d)"), cst["ident"][:])
                ins.then_inc(w_turned, 1)
                pe.wait_ge(w_out, 1)
                for k, out in enumerate((pa, pb)):
                    for h in range(2):
                        ins = nc.tensor.matmul(out[:, 4 * h:4 * h + 4, :], cst["dft"][:, k * P:k * P + P], cT[:, 4 * h:4 * h + 4, :],
                                               start=True, stop=True)
                    ins.then_inc(transformed, 1)

            @block.vector
            def _(dve):
                nc.vector.memset(ext[:, :, S:], SENTINEL).then_inc(chain, 1)
                dve.wait_ge(turned, 1)
                nc.vector.tensor_copy(ext[:, :, 0:S], pc[:].rearrange("p g (b d) -> p (g b) d", b=2)).then_inc(chain, 1)
                dve.wait_ge(chain, 2)
                for g in range(2 * G):
                    ins = nc.vector.max(out=m8[:, g, :], in_=ext[:, g, :])
                ins.then_inc(chain, 1)
                dve.wait_ge(chain, 3)
                nc.vector.tensor_tensor(e[:], ext[:, :, 0:S], m8[:, :, TOP - DELAYS:TOP - DELAYS + 1].to_broadcast([P, 2 * G, S]),
                                        ALU.subtract).then_inc(shifted, 1)
                for g in range(2 * G):
                    ins = nc.vector.match_replace(out=rep[:, g, :], in_to_replace=m8[:, g, :], in_values=ext[:, g, :],
                                                  imm_value=-SENTINEL)
                ins.then_inc(chain, 1)
                dve.wait_ge(chain, 4)
                nc.vector.tensor_tensor(w[:], rep[:, :, 0:S], ext[:, :, 0:S], ALU.not_equal).then_inc(chain, 1)
                dve.wait_ge(chain, 5)
                dve.wait_ge(exped, 1)
                nc.vector.tensor_tensor(w[:], w[:], e[:], ALU.mult).then_inc(chain, 1)
                dve.wait_ge(chain, 6)
                nc.vector.tensor_reduce(wsum[:], w[:], AX.X, ALU.add).then_inc(chain, 1)
                dve.wait_ge(chain, 7)
                nc.vector.reciprocal(wsum[:], wsum[:]).then_inc(chain, 1)
                dve.wait_ge(chain, 8)
                nc.vector.tensor_tensor(w[:], w[:], wsum[:].unsqueeze(2).to_broadcast([P, 2 * G, S]), ALU.mult).then_inc(weights, 1)

            @block.scalar
            def _(act):
                act.wait_ge(shifted, 1)
                nc.scalar.activation(e[:], e[:], ACT.Exp).then_inc(exped, 1)
                act.wait_ge(w_turned, 1)
                nc.scalar.copy(cT[:], pc[:]).then_inc(w_out, 1)
                for k, src in enumerate((pa, pb)):
                    act.wait_ge(transformed, k + 1)
                    nc.scalar.copy(cf[:, k].rearrange("p t h -> p (t h)"), src[:].rearrange("p g c -> p (g c)"))


def mix(nc, cst, x_res, vf, cf, xnT, amax, sem, n_tiles=TILES):
    with ExitStack() as mem:
        def sb(name, shape, dt=F32):
            return mem.enter_context(nc.sbuf_tensor(name, shape, dt))

        rr = sb("m_rr", [P, 2, 2, D])
        oT = sb("m_oT", [P, 2, P])
        st = sb("m_st", [P, 2, 6])
        mv = sb("m_mv", [P, 2, 2])
        ve = sb("m_ve", [P, 2, 1])
        rstd = sb("m_rstd", [P, 2, 1])
        xn = sb("m_xn", [P, 2, D])
        po = [mem.enter_context(nc.psum_tensor(f"m_po{i}", [P, 4, P], F32)) for i in range(2)]
        py = [mem.enter_context(nc.psum_tensor(f"m_py{i}", [P, 4, P], F32)) for i in range(2)]
        pt = [mem.enter_context(nc.psum_tensor(f"m_pt{i}", [P, 4, P], F32)) for i in range(2)]
        products = sem("m_products")
        biased = sem("m_biased")
        inverted = sem("m_inverted")
        o_out = sem("m_o_out")
        projected = sem("m_projected")
        added = sem("m_added")
        stats = sem("m_stats")
        rstd_done = sem("m_rstd")
        normed = sem("m_normed")
        turned = sem("m_turned")
        t_out = sem("m_t_out")
        idle = {e: sem(f"m_idle_{e}") for e in ("dve", "act", "pool")}

        with nc.Block() as block:
            @block.gpsimd
            def _(pool):
                def step(t, r):
                    p = r % 2
                    if live(t, 0, n_tiles):
                        wait_apart(pool, inverted, t - 1, idle["pool"])
                        for k in range(2):
                            ins = nc.gpsimd.tensor_tensor(
                                rr[:, p, k].rearrange("p (h d) -> p h d", d=HD),
                                vf[:, bass.ds(t, 1), :].rearrange("p a (h d) -> p (a h) d", d=HD),
                                cf[:, k, bass.ds(t, 1), :].rearrange("p a h -> p (a h)").unsqueeze(2).to_broadcast([P, H, HD]), ALU.mult)
                        ins.then_inc(products, 1)
                        nc.gpsimd.tensor_tensor(x_res[:, bass.ds(t, 1), :], x_res[:, bass.ds(t, 1), :], cst["bo1"][:].unsqueeze(1),
                                                ALU.add).then_inc(biased, 1)
                    if live(t, 2, n_tiles):
                        wait_apart(pool, stats, 2 * t - 2, idle["pool"])
                        wait_apart(pool, normed, t - 3, idle["pool"])
                        nc.gpsimd.tensor_scalar(ve[:, p, :], mv[:, p, 1:2], 1e-3, None, ALU.add).then_inc(rstd_done, 1)
                        at_least(pool, rstd_done, 2 * t - 3)
                        nc.gpsimd.tensor_tensor(rstd[:, p, :], ve[:, p, :], cst["mhalf"][:], ALU.pow).then_inc(rstd_done, 1)
                pipeline(pool, n_tiles, 6, 2, step)

            @block.vector
            def _(dve):
                def step(t, r):
                    p = r % 2
                    if live(t, 2, n_tiles):
                        at_least(dve, projected, t - 1)
                        at_least(dve, biased, t - 1)
                        nc.vector.tensor_tensor(x_res[:, bass.ds(t - 2, 1), :], x_res[:, bass.ds(t - 2, 1), :], py[p][:, 0:1, :],
                                                ALU.add).then_inc(added, 1)
                    if live(t, 4, n_tiles):
                        wait_apart(dve, t_out, t - 3, idle["dve"])
                        nc.vector.tensor_reduce(amax[:, bass.ds(t - 4, 1)], xnT[:, bass.ds((t - 4) * P, P)], AX.X, ALU.max,
                                                apply_absolute_value=True)
                    if live(t, 2, n_tiles):
                        wait_apart(dve, added, t - 1, idle["dve"])
                        wait_apart(dve, rstd_done, 2 * (t - 3), idle["dve"])
                        nc.vector.bn_stats(st[:, p, :], x_res[:, bass.ds(t - 2, 1), :]).then_inc(stats, 1)
                        wait_apart(dve, stats, 2 * t - 3, idle["dve"])
                        nc.vector.bn_aggr(mv[:, p, :], st[:, p, :]).then_inc(stats, 1)
                    if live(t, 3, n_tiles):
                        at_least(dve, rstd_done, 2 * t - 4)
                        at_least(dve, turned, t - 4)
                        nc.vector.tensor_scalar(xn[:, 1 - p, :], x_res[:, bass.ds(t - 3, 1), :], mv[:, 1 - p, 0:1], rstd[:, 1 - p, :],
                                                ALU.subtract, ALU.mult).then_inc(normed, 1)
                pipeline(dve, n_tiles, 6, 2, step)

            @block.scalar
            def _(act):
                def step(t, r):
                    p = r % 2
                    if live(t, 3, n_tiles):
                        at_least(act, turned, t - 2)
                        wait_apart(act, turned, t - 2, idle["act"])
                        nc.scalar.activation(xnT[:, bass.ds((t - 3) * P, P)], pt[1 - p][:, 0, :], ACT.Identity,
                                             bias=cst["ln_beta"][:], scale=cst["ln_gamma"][:]).then_inc(t_out, 1)
                    if live(t, 1, n_tiles):
                        at_least(act, inverted, t)
                        at_least(act, projected, t - 2)
                        nc.scalar.copy(oT[:, 1 - p], po[1 - p][:, 0, :]).then_inc(o_out, 1)
                pipeline(act, n_tiles, 6, 2, step)

            @block.tensor
            def _(pe):
                def step(t, r):
                    p = r % 2
                    if live(t, 1, n_tiles):
                        u, q = t - 1, 1 - p
                        at_least(pe, products, u + 1)
                        at_least(pe, o_out, u - 1)
                        for k in range(2):
                            ins = nc.tensor.matmul(po[q][:, 0, :], rr[:, q, k, :], cst["idft_conv"][:, k * P:k * P + P],
                                                   start=(k == 0), stop=(k == 1))
                        ins.then_inc(inverted, 1)
                    if live(t, 3, n_tiles):
                        at_least(pe, normed, t - 2)
                        at_least(pe, t_out, t - 4)
                        nc.tensor.transpose(pt[1 - p][:, 0, :], xn[:, 1 - p, :], cst["ident"][:]).then_inc(turned, 1)
                    if live(t, 1, n_tiles):
                        at_least(pe, o_out, u + 1)
                        at_least(pe, added, u - 1)
                        nc.tensor.matmul(py[q][:, 0, :], oT[:, q], cst["w1T"][:, 3, :], start=True, stop=True).then_inc(projected, 1)
                pipeline(pe, n_tiles, 6, 2, step)


def ternary(nc, cst, x_res, xnT, amax, out, sem, chunks=TILES // 4):
    with ExitStack() as mem:
        def sb(name, shape, dt=F32):
            return mem.enter_context(nc.sbuf_tensor(name, shape, dt))

        gcol = sb("t_gcol", [P, 1])
        grow = sb("t_grow", [1, 1])
        bound = sb("t_bound", [P, 2])
        xq = sb("t_xq", [P, 2, 4, P])
        res = sb("t_res", [P, 2, 4, D])
        pg = mem.enter_context(nc.psum_tensor("t_pg", [P, 512], F32))
        py = [mem.enter_context(nc.psum_tensor(f"t_py{i}", [P, 4, P], F32)) for i in range(2)]
        chain = sem("t_chain")
        across = sem("t_across")
        clipped = sem("t_clipped")
        multiplied = sem("t_multiplied")
        summed = sem("t_summed")
        stored = [sem(f"t_stored{i}") for i in range(2)]
        idle = {e: sem(f"t_idle_{e}") for e in ("dve", "sp")}

        with nc.Block() as block:
            @block.vector
            def _(dve):
                nc.vector.tensor_reduce(gcol[:], amax[:, 0:4 * chunks], AX.X, ALU.max).then_inc(chain, 1)
                dve.wait_ge(across, 1)
                nc.vector.tensor_reduce(grow[:], pg[0:1, 0:P], AX.X, ALU.max).then_inc(chain, 1)
                dve.wait_ge(across, 2)
                edge = float(np.float32(QB - 1e-5)) / QB
                nc.vector.tensor_scalar(bound[:, 0:1], pg[:, P:P + 1], edge, None, ALU.mult)
                nc.vector.tensor_scalar(bound[:, 1:2], pg[:, P:P + 1], -edge, None, ALU.mult).then_inc(chain, 1)
                dve.wait_ge(chain, 3)

                def step(c, r):
                    if live(c, 0, chunks):
                        at_least(dve, multiplied, c - 1)
                        nc.vector.tensor_scalar(xq[:, r].rearrange("p j t -> p (j t)"), xnT[:, bass.ds(c * 512, 512)],
                                                bound[:, 0:1], bound[:, 1:2], ALU.min, ALU.max).then_inc(clipped, 1)
                    if live(c, 1, chunks):
                        at_least(dve, multiplied, c)
                        at_least(dve, stored[1 - r], (c - 1) // 2 * 16 if isinstance(c, int) else (c - 1 - (1 - r)) * 8)
                        nc.vector.scalar_tensor_tensor(res[:, 1 - r].rearrange("p j d -> p (j d)"), py[1 - r][:].rearrange("p j d -> p (j d)"),
                                                       cst["beta"][:], x_res[:, bass.ds((c - 1) * 4, 4), :].rearrange("p j d -> p (j d)"),
                                                       ALU.mult, ALU.add).then_inc(summed, 1)
                pipeline(dve, chunks, 3, 2, step)

            @block.tensor
            def _(pe):
                pe.wait_ge(chain, 1)
                nc.tensor.transpose(pg[0:1, 0:P], gcol[:], cst["ident"][:]).then_inc(across, 1)
                pe.wait_ge(chain, 2)
                nc.tensor.matmul(pg[:, P:P + 1], cst["ones"][0:1, :], grow[:], start=True, stop=True).then_inc(across, 1)

                def step(c, r):
                    if live(c, 0, chunks):
                        at_least(pe, clipped, c + 1)
                        at_least(pe, summed, c - 1)
                        for j in range(4):
                            ins = nc.tensor.matmul(py[r][:, j, :], xq[:, r, j, :], cst["wt"][:], start=True, stop=True)
                        ins.then_inc(multiplied, 1)
                pipeline(pe, chunks, 3, 2, step)

            @block.sync
            def _(sp):
                def step(c, r):
                    if live(c, 1, chunks):
                        wait_apart(sp, summed, c, idle["sp"])
                        sp.dma_start(out[bass.ds((c - 1) * 4, 4)].rearrange("j p d -> p j d"), res[:, 1 - r]).then_inc(stored[1 - r], 16)
                pipeline(sp, chunks, 3, 2, step)
                for q in stored:
                    sp.wait_ge(q, 16 * (chunks // 2))


def host_tables():
    r = np.arange(S)
    return {
        "ident": np.eye(P, dtype=np.float32),
        "ident16": np.eye(P, dtype=np.float16),
        "hmask": np.kron(np.ones((2, 1)), np.kron(np.eye(8), np.ones((HD, 1)))).astype(np.float32),
        "maskq": np.tile(np.where(r[:, None] > r[None, :], -BIG, 0.0), (1, 2)).astype(np.float32),
        "maskk": np.tile(np.eye(S), (1, 8)).astype(np.float32),
        "sel": np.kron(np.arange(P)[:, None] % E == np.arange(E)[None, :], np.ones((1, FH))).astype(np.float16),
        **{k: v.astype(np.float32) for k, v in dft_tables().items()},
    }


def two_layers(nc, d, out):
    with ExitStack() as mem:
        def sb(name, shape, dt=F32):
            return mem.enter_context(nc.sbuf_tensor(name, shape, dt))

        def sem(name):
            return mem.enter_context(nc.semaphore(name))

        shapes = {
            "ident": ([P, P], F32), "ident16": ([P, P], F16), "hmask": ([P, 8], F32), "maskq": ([S, P], BF16),
            "maskk": ([S, 512], BF16), "ones": ([P, P], F32), "mhalf": ([P, 1], F32),
            "Wq": ([D, D], F32), "Wo": ([D, D], F32), "bqH": ([P, 2], F32), "bqs": ([P, 2], F32), "boe": ([P, D], F32),
            "centT": ([D, E], F32), "eb": ([P, E], F32),
            "w1T": ([D, 4, D], F32), "fbias": ([P, 4, D], F32), "bo1": ([P, D], F32),
            "dft": ([P, 2 * P], F32), "idft_corr": ([P, 2 * P], F32), "idft_conv": ([P, 2 * P], F32),
            "ln_gamma": ([D, 1], F32), "ln_beta": ([D, 1], F32), "beta": ([P, 1], F32), "wt": ([D, D], F32),
        }
        cst = {name: sb(name, shape, dt) for name, (shape, dt) in shapes.items()}
        x_res = sb("x_res", [P, TILES, D])
        tile = "(t p) s d -> t (p s) d"
        x = d["x"].rearrange(tile, p=2)
        ctx = d["ctx"].rearrange(tile, p=2)
        with ExitStack() as ffn:
            for name in ("wuh", "wul", "wdh", "wdl"):
                cst[name] = ffn.enter_context(nc.sbuf_tensor(name, [P, PAIRS * P], F32R))
            cwT = ffn.enter_context(nc.sbuf_tensor("cwT", [P, TILES * P], F16))
            setup(nc, cst, d, sem)
            attention(nc, cst, x, ctx, x_res, sem)
            with nc.sbuf_tensor("xnT", [P, TILES * P + 512], F32) as xnT:
                router(nc, cst, x_res, xnT, cwT, sem)
                experts(nc, cst, d, x_res, xnT, cwT, sem)
        xnT2 = sb("xnT2", [P, TILES * P])
        vf = sb("vf", [P, TILES, D])
        corr = sb("corr", [P, TILES, H])
        cf = sb("cf", [P, 2, TILES, H])
        amax = sb("amax", [P, TILES])
        spectrum(nc, cst, ctx, x_res, vf, corr, sem)
        delays(nc, cst, corr, cf, sem)
        mix(nc, cst, x_res, vf, cf, xnT2, amax, sem)
        ternary(nc, cst, x_res, xnT2, amax, out.rearrange(tile, p=2), sem)


_NAMES = {
    "x": "x", "ctx": "ctx_1024", "Wq": "L0_xattn_Wq", "bq": "L0_xattn_bq", "Wo": "L0_xattn_Wo", "bo": "L0_xattn_bo",
    "centroids": "L0_ffn_centroids", "eb": "L0_ffn_expert_biases", "Ws_up": "L0_ffn_Ws_up", "Ws_down": "L0_ffn_Ws_down",
    "W_up": "L0_ffn_W_up", "W_down": "L0_ffn_W_down",
    "Wq1": "L1_xattn_Wq", "bq1": "L1_xattn_bq", "Wk1": "L1_xattn_Wk", "bk1": "L1_xattn_bk",
    "Wv1": "L1_xattn_Wv", "bv1": "L1_xattn_bv", "Wo1": "L1_xattn_Wo", "bo1": "L1_xattn_bo",
    "wt": "L1_ffn_weight", "ln_gamma": "L1_ffn_ln_gamma", "ln_beta": "L1_ffn_ln_beta",
}


def kernel(**inputs):
    import concourse.bacc as _bacc
    from concourse.bass_utils import run_bass_kernel_spmd as _run

    nc = _bacc.Bacc("TRN2", target_bir_lowering=False, num_devices=1)
    arrays, d = {}, {}
    for short, name in _NAMES.items():
        a = np.ascontiguousarray(inputs[name])
        arrays[f"in_{name}_dram"] = a
        d[short] = nc.dram_tensor(f"in_{name}_dram", a.shape, mybir.dt.from_np(a.dtype), kind="ExternalInput").ap()
    for name, a in host_tables().items():
        arrays[f"table_{name}_dram"] = a
        d[name] = nc.dram_tensor(f"table_{name}_dram", a.shape, mybir.dt.from_np(a.dtype), kind="ExternalInput").ap()
    out = nc.dram_tensor("out_0_dram", (2 * TILES, S, D), F32, kind="ExternalOutput").ap()
    two_layers(nc, d, out)
    r = _run(nc, [arrays], core_ids=[0])
    return r.results[0]["out_0_dram"]
```

```python
from contextlib import ExitStack

import numpy as np

import concourse.bass as bass
from concourse import mybir

F32 = mybir.dt.float32
F32R = mybir.dt.float32r
BF16 = mybir.dt.bfloat16
F16 = mybir.dt.float16
I32 = mybir.dt.int32
ALU = mybir.AluOpType
ACT = mybir.ActivationFunctionType
AX = mybir.AxisListType

P = 128
S = 64
D = 128
TILES = 64
H = 16
HD = D // H
E = 64
FH = 64
PAIRS = E // 2 + 1
TOP = 8
DELAYS = 4
QB = 128.0
BIG = 1e10
SENTINEL = 3.0e38


def at_least(eng, sem, value):
    if isinstance(value, int) and value <= 0:
        return
    eng.wait_ge(sem, value)


def wait_apart(eng, sem, value, idle):
    at_least(eng, sem, value)
    if not isinstance(value, int):
        eng.sem_inc(idle, 1)


def pipeline(eng, count, lag, unroll, step):
    first = -(-lag // unroll) * unroll
    for t in range(first):
        step(t, t % unroll)
    with eng.Fori(first // unroll, count // unroll) as g:
        for r in range(unroll):
            step(g * unroll + r, r)
    for t in range(count, count + lag):
        step(t, t % unroll)


def live(t, lag, count):
    return not isinstance(t, int) or 0 <= t - lag < count


def in_order(stages, count):
    def step(t, r):
        for stage, lag in stages:
            if live(t, lag, count):
                stage(t - lag, (r - lag) % 4)
    return step


def setup(nc, cst, dram, sem):
    landed = sem("s_landed")
    made = sem("s_made")
    done = sem("s_done")
    bias = sem("s_bias")
    with ExitStack() as mem:
        bqB = mem.enter_context(nc.sbuf_tensor("s_bqB", [P, P], F32))
        borow = mem.enter_context(nc.sbuf_tensor("s_borow", [1, P], F32))
        onerow = mem.enter_context(nc.sbuf_tensor("s_onerow", [1, P], F32))
        bqc = mem.enter_context(nc.sbuf_tensor("s_bqc", [P, 1], F32))
        pbias = mem.enter_context(nc.psum_tensor("s_pbias", [P, 512], F32))
        loads = [(cst[name][:], dram[name]) for name in ("ident", "ident16", "hmask", "Wq", "Wo")]
        loads += [(cst["bqH"][64 * b:64 * b + 64, :], dram["bq"].rearrange("(h c) -> c h", h=2)) for b in range(2)]
        loads += [(bqc[:], dram["bq"].unsqueeze(1)), (borow[:], dram["bo"].unsqueeze(0))]
        cent = mem.enter_context(nc.sbuf_tensor("s_cent", [E, D], F32))
        loads += [(cent[:], dram["centroids"]), (cst["eb"][:], dram["eb"].unsqueeze(0).to_broadcast([P, E]))]
        shared = mem.enter_context(nc.sbuf_tensor("s_shared", [P, 2, P], F32))
        raw = mem.enter_context(nc.sbuf_tensor("s_raw", [P, 2, E // 2 * P], F32))
        loads += [(raw[:, 0, :].rearrange("p (e f) -> p e f", f=FH), dram["W_up"].rearrange("e d f -> d e f"))]
        loads += [(raw[64 * k:64 * k + 64, 1, :].rearrange("f (j d) -> f j d", d=D),
                   dram["W_down"].rearrange("(j k) f d -> k f j d", k=2)[k]) for k in range(2)]
        w1 = mem.enter_context(nc.sbuf_tensor("s_w1", [P, 4, P], F32))
        loads += [(w1[:, k, :], dram[name]) for k, name in enumerate(("Wq1", "Wk1", "Wv1", "Wo1"))]
        loads += [(cst[name][:], dram[name]) for name in ("dft", "idft_corr", "idft_conv")]
        loads += [(cst["bo1"][:], dram["bo1"].unsqueeze(0))]
        loads += [(cst[name][:], dram[name].unsqueeze(1)) for name in ("ln_gamma", "ln_beta")]
        mask_raw = mem.enter_context(nc.sbuf_tensor("s_mask", [S, P + 512], F32))
        loads += [(mask_raw[:, 0:P], dram["maskq"]), (mask_raw[:, P:], dram["maskk"])]
        wt_raw = mem.enter_context(nc.sbuf_tensor("s_wt", [P, D], F32))
        loads += [(wt_raw[:], dram["wt"])]
        wabs = mem.enter_context(nc.sbuf_tensor("s_wabs", [P, 1], F32))
        wrec = mem.enter_context(nc.sbuf_tensor("s_wrec", [P, 1], F32))
        pw = mem.enter_context(nc.psum_tensor("s_pw", [P, 4, P], F32))
        w_turned = sem("s_w_turned")
        w_chain = sem("s_w_chain")
        zeroed = sem("s_zeroed")
        high = sem("s_high")
        shared_loads = [(cst["fbias"][64 * b:64 * b + 1, k, :], dram[name].unsqueeze(0))
                        for b in range(2) for k, name in ((0, "bq1"), (1, "bk1"), (3, "bv1"))]
        shared_loads += [(shared[:, 0, 0:FH], dram["Ws_up"]), (shared[0:FH, 1, :], dram["Ws_down"])]
        with nc.Block() as block:
            @block.gpsimd
            def _(pool):
                nc.gpsimd.memset(cst["fbias"][:], 0.0).then_inc(zeroed, 1)
                nc.gpsimd.memset(shared[:], 0.0).then_inc(zeroed, 1)

            @block.scalar
            def _(act):
                act.wait_ge(landed, 16 * (len(loads) + len(shared_loads)))
                for k, name in enumerate(("wuh", "wdh")):
                    nc.scalar.copy(cst[name][:, 0:E // 2 * P], raw[:, k, :])
                    nc.scalar.copy(cst[name][:, E // 2 * P:], shared[:, k, :]).then_inc(high, 1)

            @block.sync
            def _(sp):
                with nc.allow_non_contiguous_dma("biases by column, 128 words each"):
                    for dst, src in loads:
                        sp.dma_start(dst, src).then_inc(landed, 16)
                    sp.wait_ge(zeroed, 2)
                    for dst, src in shared_loads:
                        sp.dma_start(dst, src).then_inc(landed, 16)

            @block.vector
            def _(dve):
                nc.vector.memset(cst["mhalf"][:], -0.5)
                nc.vector.memset(cst["ones"][:], 1.0)
                nc.vector.memset(onerow[:], 1.0).then_inc(made, 1)
                dve.wait_ge(landed, 16 * (len(loads) + len(shared_loads)))
                nc.vector.tensor_copy(cst["maskq"][:], mask_raw[:, 0:P])
                nc.vector.tensor_copy(cst["maskk"][:], mask_raw[:, P:])
                nc.vector.tensor_scalar(cst["bqs"][:], cst["bqH"][:], float(HD) ** -0.5, None, ALU.mult)
                nc.vector.tensor_copy(bqB[:], bqc[:].to_broadcast([P, P])).then_inc(made, 1)
                for k, name in enumerate(("wuh", "wdh")):
                    low = cst["wul" if k == 0 else "wdl"]
                    dve.wait_ge(high, k + 1)
                    nc.vector.tensor_tensor(low[:, 0:E // 2 * P], raw[:, k, :], cst[name][:, 0:E // 2 * P].bitcast(F32), ALU.subtract)
                    nc.vector.tensor_tensor(low[:, E // 2 * P:], shared[:, k, :], cst[name][:, E // 2 * P:].bitcast(F32), ALU.subtract)
                dve.wait_ge(bias, 1)
                nc.vector.tensor_copy(cst["centT"][:], pbias[:, P:P + E]).then_inc(done, 1)
                nc.vector.tensor_copy(cst["boe"][:], pbias[:, 0:P]).then_inc(done, 1)
                nc.vector.tensor_scalar(cst["fbias"][:], cst["fbias"][:], float(S), None, ALU.mult)
                dve.wait_ge(w_turned, 1)
                nc.vector.tensor_copy(cst["w1T"][:], pw[:]).then_inc(done, 1)
                nc.vector.tensor_reduce(wabs[:], wt_raw[:], AX.X, ALU.add, apply_absolute_value=True).then_inc(w_chain, 1)
                dve.wait_ge(w_turned, 2)
                nc.vector.tensor_scalar(cst["beta"][:], pbias[:, 256:257], 1.0 / (D * D), None, ALU.mult).then_inc(w_chain, 1)
                dve.wait_ge(w_chain, 2)
                nc.vector.tensor_scalar(wrec[:], cst["beta"][:], 1e-5, None, ALU.add).then_inc(w_chain, 1)
                dve.wait_ge(w_chain, 3)
                nc.vector.reciprocal(wabs[:], wrec[:]).then_inc(w_chain, 1)
                dve.wait_ge(w_chain, 4)
                nc.vector.tensor_scalar(cst["wt"][:], wt_raw[:], wabs[:], 1.5 * 2 ** 23, ALU.mult, ALU.add).then_inc(w_chain, 1)
                dve.wait_ge(w_chain, 5)
                nc.vector.tensor_scalar(cst["wt"][:], cst["wt"][:], 1.5 * 2 ** 23, 1.0, ALU.subtract, ALU.min).then_inc(w_chain, 1)
                dve.wait_ge(w_chain, 6)
                nc.vector.tensor_scalar(cst["wt"][:], cst["wt"][:], -1.0, None, ALU.max).then_inc(done, 1)
                dve.wait_ge(done, 4)

            @block.tensor
            def _(pe):
                pe.wait_ge(made, 2)
                pe.wait_ge(landed, 16 * (len(loads) + len(shared_loads)))
                nc.tensor.transpose(pbias[:, P:P + E], cent[:], cst["ident"][0:E, 0:E])
                nc.tensor.matmul(pbias[:, 0:P], bqB[:], cst["Wo"][:], start=True, stop=False)
                nc.tensor.matmul(pbias[:, 0:P], onerow[:], borow[:], start=False, stop=True).then_inc(bias, 1)

                for k in range(4):
                    ins = nc.tensor.transpose(pw[:, k, :], w1[:, k, :], cst["ident"][:])
                ins.then_inc(w_turned, 1)
                pe.wait_ge(w_chain, 1)
                pe.wait_ge(done, 3)
                nc.tensor.matmul(pbias[:, 256:257], cst["ones"][:], wabs[:], start=True, stop=True).then_inc(w_turned, 1)


def attention(nc, cst, x, ctx, x_res, sem, n_tiles=TILES):
    with ExitStack() as mem:
        def sb(name, shape, dt=F32):
            return mem.enter_context(nc.sbuf_tensor(name, shape, dt))

        def psum(name, shape, dt=F32):
            return mem.enter_context(nc.psum_tensor(name, shape, dt))

        cin = sb("cin", [P, 4, D])
        st = sb("a_stats", [P, 2, 6])
        mv = sb("a_mv", [P, 2, 2])
        ve = sb("a_ve", [P, 2, 1])
        rstd = sb("a_rstd", [P, 2, 1])
        xn = sb("a_xn", [P, 2, D])
        xcT = sb("xcT", [P, 2, 2, P])
        qb = sb("qb", [P, 2, 2, 2, S])
        kraw = sb("kraw", [P, 2, 2, S])
        kx = sb("kx", [P, 2, 2, 8, S])
        vx = sb("vx", [P, 4, 8, 2, 2, 9])
        sub = sb("sub", [P, 2, H, S])
        prob = sb("prob", [P, 2, H, S])
        pT = sb("pT", [P, 2, 8, P])
        mx = sb("mx", [P, 2, H])
        rden = sb("rden", [P, 2, H])
        o = sb("o", [P, 2, H, HD])
        oT = sb("oT", [P, 2, P])

        pt_in = psum("pt_in", [P, 4, P])
        pj = psum("pj", [P, 4, P])
        ps = psum("ps", [P, H, S])
        ppT = psum("ppT", [P, 8, P])
        po = psum("po", [P, 512])[:, 0:288].rearrange("p (j b c d) -> p j b c d", j=8, b=2, c=2)
        pb = psum("pb", [P, 4, P])

        loaded = [sem(f"a_loaded{r}") for r in range(4)]
        stats = sem("a_stats_done")
        mean_var = sem("a_mean_var")
        rstd_done = sem("a_rstd_done")
        normed = sem("a_normed")
        biased = sem("a_biased")
        turned = sem("a_turned")
        turned_out = sem("a_turned_out")
        projected = sem("a_projected")
        split_out = sem("a_split_out")
        keys = sem("a_keys")
        scored = sem("a_scored")
        maxed = sem("a_maxed")
        shifted = sem("a_shifted")
        exped = sem("a_exped")
        p_turned = sem("a_p_turned")
        p_out = sem("a_p_out")
        weighed = sem("a_weighed")
        recip = sem("a_recip")
        scaled = sem("a_scaled")
        o_turned = sem("a_o_turned")
        o_out = sem("a_o_out")
        wo_done = sem("a_wo_done")
        added = sem("a_added")
        preset = sem("a_preset")
        idle = {e: sem(f"a_idle_{e}") for e in ("dve", "sp", "pool")}

        with nc.Block() as block:
            @block.sync
            def _(sp):
                def step(t, r):
                    if not live(t, 0, n_tiles):
                        return
                    wait_apart(sp, turned, t - 3, idle["sp"])
                    wait_apart(sp, stats, 2 * (t - 3), idle["sp"])
                    sp.dma_start(x_res[:, bass.ds(t, 1), :], x[bass.ds(t, 1)].rearrange("a p d -> p a d")).then_inc(loaded[r], 16)
                    sp.dma_start(cin[:, r:r + 1, :], ctx[bass.ds(t, 1)].rearrange("a p d -> p a d")).then_inc(loaded[r], 16)
                pipeline(sp, n_tiles, 8, 4, step)

            @block.vector
            def _(dve):
                def stats_of(t, r):
                    at_least(dve, loaded[r], t // 4 * 32 + 32 if isinstance(t, int) else (t - r) * 8 + 32)
                    wait_apart(dve, rstd_done, 2 * (t - 1), idle["dve"])
                    nc.vector.bn_stats(st[:, r % 2, :], x_res[:, bass.ds(t, 1), :]).then_inc(stats, 1)
                    wait_apart(dve, stats, 2 * t + 1, idle["dve"])
                    nc.vector.bn_aggr(mv[:, r % 2, :], st[:, r % 2, :]).then_inc(stats, 1)

                def norm(t, r):
                    at_least(dve, rstd_done, 2 * t + 2)
                    at_least(dve, turned, t - 1)
                    nc.vector.tensor_scalar(xn[:, r % 2, :], x_res[:, bass.ds(t, 1), :], mv[:, r % 2, 0:1],
                                            rstd[:, r % 2, :], ALU.subtract, ALU.mult).then_inc(normed, 1)

                def row_max(t, r):
                    at_least(dve, scored, t + 1)
                    nc.vector.tensor_reduce(mx[:, r % 2, :], ps[:], AX.X, ALU.max).then_inc(maxed, 1)
                    at_least(dve, maxed, t + 1)
                    at_least(dve, exped, t - 1)
                    nc.vector.tensor_tensor(sub[:, r % 2], ps[:], mx[:, r % 2, :].unsqueeze(2).to_broadcast([P, H, S]),
                                            ALU.subtract).then_inc(shifted, 1)

                def expand_keys(t, r):
                    at_least(dve, split_out, t + 1)
                    at_least(dve, scored, t - 1)
                    for h in range(2):
                        ins = nc.vector.scalar_tensor_tensor(
                            kx[:, r % 2, h], kraw[:, r % 2, h, :].unsqueeze(1).to_broadcast([P, 8, S]), cst["bqH"][:, h:h + 1],
                            cst["hmask"][:].unsqueeze(2).to_broadcast([P, 8, S]), ALU.add, ALU.mult)
                    ins.then_inc(keys, 1)

                def scale_out(t, r):
                    at_least(dve, weighed, t + 1)
                    for b in range(2):
                        q = slice(64 * b, 64 * b + 64)
                        ins = nc.vector.reciprocal(rden[q, r % 2, :].rearrange("p (a c) -> p a c", c=2), po[q, :, b, :, 8])
                    ins.then_inc(recip, 1)
                    at_least(dve, recip, t + 1)
                    at_least(dve, o_turned, t - 1)
                    for b in range(2):
                        q = slice(64 * b, 64 * b + 64)
                        ins = nc.vector.tensor_tensor(
                            o[q, r % 2].rearrange("p (a c) d -> p a c d", c=2), po[q, :, b, :, 0:8],
                            rden[q, r % 2, :].rearrange("p (a c) -> p a c", c=2).unsqueeze(3).to_broadcast([64, 8, 2, 8]),
                            ALU.mult)
                    ins.then_inc(scaled, 1)

                def add_out(t, r):
                    at_least(dve, wo_done, t + 1)
                    at_least(dve, biased, t + 1)
                    nc.vector.tensor_tensor(x_res[:, bass.ds(t, 1), :], x_res[:, bass.ds(t, 1), :], pb[:, 1:2, :],
                                            ALU.add).then_inc(added, 1)

                def step(t, r):
                    if live(t, 6, n_tiles):
                        add_out(t - 6, (r - 6) % 4)
                    if live(t, 2, n_tiles):
                        expand_keys(t - 2, (r - 2) % 4)
                    if live(t, 0, n_tiles):
                        stats_of(t, r)
                    if live(t, 3, n_tiles):
                        row_max(t - 3, (r - 3) % 4)
                    if live(t, 0, n_tiles):
                        norm(t, r)
                    if live(t, 4, n_tiles):
                        scale_out(t - 4, (r - 4) % 4)
                pipeline(dve, n_tiles, 8, 4, step)

            @block.gpsimd
            def _(pool):
                nc.gpsimd.memset(qb[:], 0.0).then_inc(preset, 1)
                nc.gpsimd.memset(vx[:], 0.0).then_inc(preset, 1)
                pool.wait_ge(preset, 2)
                for d in range(2):
                    nc.gpsimd.memset(vx[64 * d:64 * d + 64, :, :, :, d, 8], 1.0).then_inc(preset, 1)

                pool.wait_ge(preset, 4)

                def step(t, r):
                    if live(t, 0, n_tiles):
                        at_least(pool, stats, 2 * t + 2)
                        wait_apart(pool, normed, t - 1, idle["pool"])
                        nc.gpsimd.tensor_scalar(ve[:, r % 2, :], mv[:, r % 2, 1:2], 1e-5, None, ALU.add).then_inc(rstd_done, 1)
                        at_least(pool, rstd_done, 2 * t + 1)
                        nc.gpsimd.tensor_tensor(rstd[:, r % 2, :], ve[:, r % 2, :], cst["mhalf"][:], ALU.pow).then_inc(rstd_done, 1)
                    if live(t, 1, n_tiles):
                        at_least(pool, normed, t)
                        nc.gpsimd.tensor_tensor(x_res[:, bass.ds(t - 1, 1), :], x_res[:, bass.ds(t - 1, 1), :],
                                                cst["boe"][:].unsqueeze(1), ALU.add).then_inc(biased, 1)
                pipeline(pool, n_tiles, 8, 4, step)

            @block.scalar
            def _(act):
                act.wait_ge(preset, 4)

                def probs_out(t, r):
                    at_least(act, p_turned, t + 1)
                    at_least(act, weighed, t - 1)
                    nc.scalar.copy(pT[:, r % 2], ppT[:]).then_inc(p_out, 1)

                def turned_copy(t, r):
                    at_least(act, turned, t + 1)
                    at_least(act, projected, t - 1)
                    nc.scalar.copy(xcT[:, r % 2], pt_in[:, 0:2, :]).then_inc(turned_out, 1)

                def o_copy(t, r):
                    at_least(act, o_turned, t + 1)
                    at_least(act, wo_done, t - 1)
                    nc.scalar.copy(oT[:, r % 2], pb[:, 0, :]).then_inc(o_out, 1)

                def split(t, r):
                    at_least(act, projected, t + 1)
                    at_least(act, scored, t - 1)
                    at_least(act, keys, t - 1)
                    at_least(act, weighed, t - 3)
                    for b in range(2):
                        q = slice(64 * b, 64 * b + 64)
                        for h in range(2):
                            nc.scalar.activation(qb[q, r % 2, h, b, :], pj[q, h, 0:64], ACT.Identity,
                                                 bias=cst["bqs"][q, h:h + 1], scale=float(HD) ** -0.5)
                        for d in range(2):
                            nc.scalar.copy(vx[64 * d:64 * d + 64, r % 4, :, b, d, 0:8],
                                           pj[q, 2, :].rearrange("p (a c d) -> p a c d", c=2, d=8)[:, :, d, :])
                    nc.scalar.copy(kraw[:, r % 2], pj[:, 0:2, 64:128]).then_inc(split_out, 1)

                def exponent(t, r):
                    at_least(act, shifted, t + 1)
                    at_least(act, p_turned, t - 1)
                    nc.scalar.activation(prob[:, r % 2], sub[:, r % 2], ACT.Exp).then_inc(exped, 1)

                def step(t, r):
                    if live(t, 1, n_tiles):
                        turned_copy(t - 1, (r - 1) % 4)
                    if live(t, 5, n_tiles):
                        o_copy(t - 5, (r - 5) % 4)
                    if live(t, 4, n_tiles):
                        probs_out(t - 4, (r - 4) % 4)
                    if live(t, 3, n_tiles):
                        exponent(t - 3, (r - 3) % 4)
                    if live(t, 1, n_tiles):
                        split(t - 1, (r - 1) % 4)
                pipeline(act, n_tiles, 8, 4, step)

            @block.tensor
            def _(pe):
                def scores(t, r):
                    at_least(pe, keys, t + 1)
                    at_least(pe, split_out, t + 1)
                    at_least(pe, shifted, t)
                    for h in range(2):
                        out = ps[:, 8 * h:8 * h + 8, :]
                        nc.tensor.matmul(out, cst["maskq"][:], cst["maskk"][:], start=True, stop=False)
                        ins = nc.tensor.matmul(out, qb[:, r % 2, h].rearrange("p b q -> p (b q)"), kx[:, r % 2, h],
                                               start=False, stop=True)
                    ins.then_inc(scored, 1)

                def turn_probs(t, r):
                    at_least(pe, exped, t + 1)
                    at_least(pe, p_out, t)
                    for j in range(8):
                        ins = nc.tensor.transpose(ppT[:, j, :], prob[:, r % 2, 2 * j:2 * j + 2].rearrange("p a k -> p (a k)"),
                                                  cst["ident"][:])
                    ins.then_inc(p_turned, 1)

                def turn_in(t, r):
                    at_least(pe, normed, t + 1)
                    at_least(pe, loaded[r % 4], (t // 4) * 32 + 32 if isinstance(t, int) else (t - r % 4) * 8 + 32)
                    at_least(pe, turned_out, t)
                    nc.tensor.transpose(pt_in[:, 0, :], xn[:, r % 2, :], cst["ident"][:])
                    nc.tensor.transpose(pt_in[:, 1, :], cin[:, r % 4, :], cst["ident"][:]).then_inc(turned, 1)

                def turn_o(t, r):
                    at_least(pe, scaled, t + 1)
                    at_least(pe, added, t)
                    nc.tensor.transpose(pb[:, 0, :], o[:, r % 2].rearrange("p h d -> p (h d)"), cst["ident"][:]).then_inc(o_turned, 1)

                def project(t, r):
                    at_least(pe, turned_out, t + 1)
                    at_least(pe, split_out, t)
                    for b in range(2):
                        for h in range(2):
                            nc.tensor.matmul(pj[64 * b:64 * b + 64, h, :], cst["Wq"][:, 64 * h:64 * h + 64],
                                             xcT[:, r % 2, :, 64 * b:64 * b + 64], start=True, stop=True)
                    nc.tensor.matmul(pj[:, 2, :], xcT[:, r % 2, 1, :], cst["Wq"][:], start=True, stop=True).then_inc(projected, 1)

                def weigh(t, r):
                    at_least(pe, p_out, t + 1)
                    at_least(pe, scaled, t)
                    for j in range(8):
                        ins = nc.tensor.matmul(po[:, j], pT[:, r % 2, j, :], vx[:, r % 4, j], start=True, stop=True)
                    ins.then_inc(weighed, 1)

                def out_project(t, r):
                    at_least(pe, o_out, t + 1)
                    nc.tensor.matmul(pb[:, 1, :], oT[:, r % 2], cst["Wo"][:], start=True, stop=True).then_inc(wo_done, 1)

                def step(t, r):
                    if live(t, 3, n_tiles):
                        scores(t - 3, (r - 3) % 4)
                    if live(t, 1, n_tiles):
                        turn_in(t - 1, (r - 1) % 4)
                    if live(t, 5, n_tiles):
                        turn_o(t - 5, (r - 5) % 4)
                    if live(t, 4, n_tiles):
                        turn_probs(t - 4, (r - 4) % 4)
                    if live(t, 1, n_tiles):
                        project(t - 1, (r - 1) % 4)
                    if live(t, 4, n_tiles):
                        weigh(t - 4, (r - 4) % 4)
                    if live(t, 5, n_tiles):
                        out_project(t - 5, (r - 5) % 4)
                pipeline(pe, n_tiles, 8, 4, step)


def router(nc, cst, x_res, xnT, cwT, sem, groups=TILES // 4):
    with ExitStack() as mem:
        def sb(name, shape, dt=F32):
            return mem.enter_context(nc.sbuf_tensor(name, shape, dt))

        def psum(name, shape, dt=F32):
            return mem.enter_context(nc.psum_tensor(name, shape, dt))

        st = sb("r_st", [P, 2, 4, 6])
        mv = sb("r_mv", [P, 2, 4, 2])
        ve = sb("r_ve", [P, 2, 4])
        rstd = sb("r_rstd", [P, 2, 4])
        xn = sb("r_xn", [P, 2, 4, D])
        xs = sb("r_xs", [P, 2, 4, P])
        aff = sb("r_aff", [P, 2, 4, E])
        en = sb("r_en", [P, 2, 4, E])
        biased = sb("r_biased", [P, 4, E])
        m8 = sb("r_m8", [P, 4, TOP])
        rep = sb("r_rep", [P, 4, E])
        chosen = sb("r_chosen", [P, 4, E])
        gate = sb("r_gate", [P, 4, E])
        w = sb("r_w", [P, 4, E])
        wsum = sb("r_wsum", [P, 4])
        wrec = sb("r_wrec", [P, 4])
        cw = sb("r_cw", [P, 4, E])
        cwp = sb("r_cwp", [P, 2, 4, 2, E], F16)
        pt = psum("r_pt", [P, 4, P])
        pa = psum("r_pa", [P, 512])[:, 0:4 * E].rearrange("p (t e) -> p t e", t=4)
        pc = psum("r_pc", [P, 1024], F16)[:, 0:512].rearrange("p (t e) -> p t e", t=4)

        stats = sem("r_stats")
        rstd_done = sem("r_rstd")
        normed = sem("r_normed")
        turned = sem("r_turned")
        turned_out = sem("r_turned_out")
        kept = sem("r_kept")
        affine = sem("r_affine")
        exped = sem("r_exped")
        chain = sem("r_chain")
        gates = sem("r_gates")
        g_turned = sem("r_g_turned")
        g_out = sem("r_g_out")
        idle = {e: sem(f"r_idle_{e}") for e in ("dve", "pool", "act")}

        with nc.Block() as block:
            @block.vector
            def _(dve):
                def stats_of(g, r):
                    wait_apart(dve, rstd_done, 2 * (g - 1), idle["dve"])
                    for j in range(4):
                        ins = nc.vector.bn_stats(st[:, r, j, :], x_res[:, bass.ds(g * 4 + j, 1), :])
                    ins.then_inc(stats, 1)
                    wait_apart(dve, stats, 2 * g + 1, idle["dve"])
                    for j in range(4):
                        ins = nc.vector.bn_aggr(mv[:, r, j, :], st[:, r, j, :])
                    ins.then_inc(stats, 1)

                def norm(g, r):
                    at_least(dve, rstd_done, 2 * g + 2)
                    at_least(dve, turned, g - 1)
                    for j in range(4):
                        ins = nc.vector.tensor_scalar(xn[:, r, j, :], x_res[:, bass.ds(g * 4 + j, 1), :], mv[:, r, j, 0:1],
                                                      rstd[:, r, j:j + 1], ALU.subtract, ALU.mult)
                    ins.then_inc(normed, 1)

                def gates_of(g, r):
                    at_least(dve, exped, g + 1)

                    def then(ins, n):
                        ins.then_inc(chain, 1)
                        wait_apart(dve, chain, g * 10 + n, idle["dve"])
                    then(nc.vector.tensor_tensor(biased[:], aff[:, r], cst["eb"][:].unsqueeze(1).to_broadcast([P, 4, E]), ALU.add), 1)
                    for j in range(4):
                        ins = nc.vector.max(out=m8[:, j, :], in_=biased[:, j, :])
                    then(ins, 2)
                    for j in range(4):
                        nc.vector.match_replace(out=rep[:, j, :], in_to_replace=m8[:, j, :], in_values=biased[:, j, :],
                                                imm_value=-SENTINEL)
                    then(nc.vector.tensor_scalar(en[:, r], en[:, r], 1.0, None, ALU.add), 3)
                    nc.vector.tensor_tensor(chosen[:], rep[:], biased[:], ALU.not_equal)
                    then(nc.vector.reciprocal(gate[:], en[:, r]), 4)
                    then(nc.vector.tensor_tensor(w[:], gate[:], chosen[:], ALU.mult), 5)
                    then(nc.vector.tensor_reduce(wsum[:], w[:], AX.X, ALU.add), 6)
                    then(nc.vector.tensor_scalar(wsum[:], wsum[:], 1e-8, None, ALU.add), 7)
                    then(nc.vector.reciprocal(wrec[:], wsum[:]), 8)
                    at_least(dve, g_turned, g - 1)
                    then(nc.vector.tensor_tensor(cw[:], w[:], wrec[:].unsqueeze(2).to_broadcast([P, 4, E]), ALU.mult), 9)
                    then(nc.vector.tensor_copy(cwp[:, r, :, 0, :], cw[:]), 10)
                    nc.vector.tensor_tensor(cwp[:, r, :, 1, :], cw[:], cwp[:, r, :, 0, :], ALU.subtract).then_inc(gates, 1)

                def step(g, r):
                    if live(g, 0, groups):
                        stats_of(g, r)
                    if live(g, 2, groups):
                        gates_of(g - 2, r)
                    if live(g, 0, groups):
                        norm(g, r)
                pipeline(dve, groups, 6, 2, step)

            @block.gpsimd
            def _(pool):
                def step(g, r):
                    if live(g, 1, groups):
                        wait_apart(pool, turned_out, g, idle["pool"])
                        nc.gpsimd.tensor_copy(xnT[:, bass.ds((g - 1) * 512, 512)], xs[:, 1 - r].rearrange("p j t -> p (j t)")).then_inc(kept, 1)
                    if live(g, 0, groups):
                        wait_apart(pool, normed, g - 1, idle["pool"])
                        wait_apart(pool, stats, 2 * g + 2, idle["pool"])
                        nc.gpsimd.tensor_scalar(ve[:, r, :], mv[:, r, :, 1], 1e-5, None, ALU.add).then_inc(rstd_done, 1)
                        at_least(pool, rstd_done, 2 * g + 1)
                        nc.gpsimd.tensor_tensor(rstd[:, r, :], ve[:, r, :], cst["mhalf"][:].to_broadcast([P, 4]), ALU.pow).then_inc(rstd_done, 1)
                pipeline(pool, groups, 6, 2, step)

            @block.scalar
            def _(act):
                def step(g, r):
                    if live(g, 3, groups):
                        wait_apart(act, g_turned, g - 2, idle["act"])
                        nc.scalar.copy(cwT[:, bass.ds((g - 3) * 512, 512)], pc.rearrange("p t e -> p (t e)")).then_inc(g_out, 1)
                    if live(g, 1, groups):
                        at_least(act, turned, g)
                        at_least(act, kept, g - 2)
                        at_least(act, affine, g - 2)
                        nc.scalar.copy(xs[:, 1 - r], pt[:]).then_inc(turned_out, 1)
                        at_least(act, affine, g)
                        at_least(act, gates, g - 2)
                        nc.scalar.copy(aff[:, 1 - r], pa)
                        nc.scalar.activation(en[:, 1 - r], pa, ACT.Exp, scale=-1.0).then_inc(exped, 1)
                pipeline(act, groups, 6, 2, step)

            @block.tensor
            def _(pe):
                def step(g, r):
                    if live(g, 3, groups):
                        at_least(pe, gates, g - 2)
                        at_least(pe, g_out, g - 3)
                        for j in range(4):
                            ins = nc.tensor.transpose(pc[:, j, :], cwp[:, 1 - r, j].rearrange("p a e -> p (a e)"), cst["ident16"][:])
                        ins.then_inc(g_turned, 1)
                    if live(g, 1, groups):
                        at_least(pe, normed, g)
                        at_least(pe, turned_out, g - 1)
                        for j in range(4):
                            ins = nc.tensor.transpose(pt[:, j, :], xn[:, 1 - r, j, :], cst["ident"][:])
                        ins.then_inc(turned, 1)
                        at_least(pe, turned_out, g)
                        at_least(pe, exped, g - 1)
                        for j in range(4):
                            ins = nc.tensor.matmul(pa[:, j, :], xs[:, 1 - r, j, :], cst["centT"][:], start=True, stop=True)
                        ins.then_inc(affine, 1)
                pipeline(pe, groups, 6, 2, step)


def experts(nc, cst, dram, x_res, xnT, cwT, sem, chunks=TILES // 4):
    turns = chunks * PAIRS
    with ExitStack() as mem:
        def sb(name, shape, dt=F32):
            return mem.enter_context(nc.sbuf_tensor(name, shape, dt))

        def psum(name, shape, dt=F32):
            return mem.enter_context(nc.psum_tensor(name, shape, dt))

        sel = sb("e_sel", [P, (PAIRS - 1) * P], F16)
        xh = sb("e_xh", [P, 2, 512], F32R)
        xl = sb("e_xl", [P, 2, 512], F32R)
        s = sb("e_s", [P, 3, 512])
        m = sb("e_m", [P, 3, 512])
        mh = sb("e_mh", [P, 3, 512], F32R)
        ml = sb("e_ml", [P, 3, 512], F32R)
        yT = sb("e_yT", [P, 512])
        pu = [psum(f"e_pu{i}", [P, 512]) for i in range(3)]
        pg = [psum(f"e_pg{i}", [P, 512]) for i in range(2)]
        py = [psum(f"e_py{i}", [P, 512]) for i in range(2)]
        pt = psum("e_pt", [P, 4, P])

        landed = sem("e_landed")
        x_high = sem("e_x_high")
        x_low = sem("e_x_low")
        up_done = sem("e_up")
        gate_done = sem("e_gate")
        silued = sem("e_silu")
        gated = sem("e_gated")
        m_high = sem("e_m_high")
        m_low = sem("e_m_low")
        down_done = sem("e_down")
        y_out = sem("e_y_out")
        y_turned = sem("e_y_turned")
        y_added = sem("e_y_added")
        idle = sem("e_idle")

        def drive(eng, step):
            unroll = 2 * PAIRS
            for n in range(unroll):
                step(n, n, lambda lag, n=n: (n - lag) // PAIRS)
            with eng.Fori(1, turns // unroll) as g:
                for r in range(unroll):
                    step(g * unroll + r, r, lambda lag, g=g, r=r: g * 2 + (r - lag) // PAIRS)
            for n in range(turns, turns + 9):
                step(n, n % unroll, lambda lag, n=n: (n - lag) // PAIRS)

        padded = sem("e_padded")

        with nc.Block() as block:
            @block.gpsimd
            def _(pool):
                nc.gpsimd.memset(xnT[:, chunks * 512:chunks * 512 + 512], 0.0).then_inc(padded, 1)

            @block.sync
            def _(sp):
                sp.dma_start(sel[:], dram["sel"]).then_inc(landed, 16)

            @block.vector
            def _(dve):
                def low_part(c, b):
                    at_least(dve, x_high, c + 1)
                    nc.vector.tensor_tensor(xl[:, b, :], xnT[:, bass.ds(c * 512, 512)], xh[:, b, :].bitcast(F32),
                                            ALU.subtract).then_inc(x_low, 1)

                def step(n, r, chunk):
                    if isinstance(n, int) and n == 0:
                        dve.wait_ge(padded, 1)
                        low_part(0, 0)
                    if live(n, 0, turns):
                        pair = r % PAIRS
                        at_least(dve, silued, n + 1)
                        at_least(dve, m_low, n - 2)
                        if pair < PAIRS - 1:
                            at_least(dve, gate_done, chunk(0) * (PAIRS - 1) + pair + 1)
                            ins = nc.vector.tensor_tensor(m[:, r % 3, :], s[:, r % 3, :], pg[r % 2][:], ALU.mult)
                        else:
                            ins = nc.vector.tensor_scalar(m[:, r % 3, :], s[:, r % 3, :], 1.0, None, ALU.mult)
                        ins.then_inc(gated, 1)
                    if live(n, 1, turns):
                        at_least(dve, m_high, n)
                        at_least(dve, down_done, n - 3)
                        nc.vector.tensor_tensor(ml[:, (r - 1) % 3, :], m[:, (r - 1) % 3, :], mh[:, (r - 1) % 3, :].bitcast(F32),
                                                ALU.subtract).then_inc(m_low, 1)
                    if live(n, 0, turns) and r % PAIRS == 10:
                        low_part(chunk(0) + 1, (r // PAIRS + 1) % 2)
                    if live(n, 8, turns) and (r - 8) % PAIRS == PAIRS - 1:
                        c = chunk(8)
                        at_least(dve, y_turned, c + 1)
                        nc.vector.tensor_tensor(x_res[:, bass.ds(c * 4, 4), :], x_res[:, bass.ds(c * 4, 4), :], pt[:],
                                                ALU.add).then_inc(y_added, 1)
                drive(dve, step)

            @block.scalar
            def _(act):
                def high_part(c, b):
                    wait_apart(act, up_done, (c - 1) * PAIRS, idle)
                    nc.scalar.copy(xh[:, b, :], xnT[:, bass.ds(c * 512, 512)]).then_inc(x_high, 1)

                def step(n, r, chunk):
                    if isinstance(n, int) and n == 0:
                        act.wait_ge(padded, 1)
                        high_part(0, 0)
                    if live(n, 0, turns):
                        at_least(act, up_done, n + 1)
                        at_least(act, gated, n - 2)
                        nc.scalar.activation(s[:, r % 3, :], pu[r % 3][:], ACT.Silu).then_inc(silued, 1)
                    if live(n, 1, turns):
                        at_least(act, gated, n)
                        at_least(act, down_done, n - 3)
                        nc.scalar.copy(mh[:, (r - 1) % 3, :], m[:, (r - 1) % 3, :]).then_inc(m_high, 1)
                    if live(n, 0, turns) and r % PAIRS == 10:
                        high_part(chunk(0) + 1, (r // PAIRS + 1) % 2)
                    if live(n, 4, turns) and (r - 4) % PAIRS == PAIRS - 1:
                        c = chunk(4)
                        at_least(act, down_done, (c + 1) * PAIRS)
                        at_least(act, y_turned, c)
                        nc.scalar.copy(yT[:], py[((r - 4) // PAIRS) % 2][:]).then_inc(y_out, 1)
                drive(act, step)

            @block.tensor
            def _(pe):
                pe.wait_ge(landed, 16)

                def step(n, r, chunk):
                    pair = r % PAIRS
                    w = slice(pair * P, pair * P + P)
                    if live(n, 0, turns):
                        b = (r // PAIRS) % 2
                        at_least(pe, x_low, chunk(0) + 1)
                        at_least(pe, silued, n - 2)
                        nc.tensor.matmul(pu[r % 3][:], cst["wuh"][:, w], xh[:, b, :], start=True, stop=False)
                        nc.tensor.matmul(pu[r % 3][:], cst["wul"][:, w], xh[:, b, :], start=False, stop=False)
                        nc.tensor.matmul(pu[r % 3][:], cst["wuh"][:, w], xl[:, b, :], start=False, stop=True).then_inc(up_done, 1)
                        if pair < PAIRS - 1:
                            at_least(pe, gated, n - 1)
                            nc.tensor.matmul(pg[r % 2][:], sel[:, w], cwT[:, bass.ds(chunk(0) * 512, 512)],
                                             start=True, stop=True).then_inc(gate_done, 1)
                    if live(n, 3, turns):
                        pd = (r - 3) % PAIRS
                        w = slice(pd * P, pd * P + P)
                        k = (r - 3) % 3
                        out = py[((r - 3) // PAIRS) % 2][:]
                        at_least(pe, m_low, n - 2)
                        if pd == 0:
                            at_least(pe, y_out, chunk(3) - 1)
                        nc.tensor.matmul(out, cst["wdh"][:, w], mh[:, k, :], start=(pd == 0), stop=False)
                        nc.tensor.matmul(out, cst["wdl"][:, w], mh[:, k, :], start=False, stop=False)
                        nc.tensor.matmul(out, cst["wdh"][:, w], ml[:, k, :], start=False, stop=(pd == PAIRS - 1)).then_inc(down_done, 1)
                    if live(n, 6, turns) and (r - 6) % PAIRS == PAIRS - 1:
                        c = chunk(6)
                        at_least(pe, y_out, c + 1)
                        at_least(pe, y_added, c)
                        for j in range(4):
                            ins = nc.tensor.transpose(pt[:, j, :], yT[:, j * P:(j + 1) * P], cst["ident"][:])
                        ins.then_inc(y_turned, 1)
                drive(pe, step)


def dft_tables():
    f = np.concatenate([np.arange(S // 2 + 1), np.arange(1, S // 2)])
    second = np.arange(S) > S // 2
    angle = 2 * np.pi * np.outer(f, np.arange(S)) / S
    cos, sin = np.cos(angle), np.sin(angle)
    weight = np.where((f == 0) | (f == S // 2), 1.0, 2.0)[:, None] / S
    sign = np.where(second, -1.0, 1.0)[:, None]
    both = lambda m: np.kron(np.eye(2), m)
    return {
        "dft": np.concatenate([both(np.where(second[:, None], -sin, cos).T), both(np.where(second[:, None], cos, -sin).T)], 1),
        "idft_corr": np.concatenate([both(weight * cos), both(weight * sign * sin)], 1) / HD,
        "idft_conv": np.concatenate([both(weight * sign * cos), both(-weight * sin)], 1),
    }


def spectrum(nc, cst, ctx, x_res, vf, corr, sem, n_tiles=TILES):
    with ExitStack() as mem:
        def sb(name, shape, dt=F32):
            return mem.enter_context(nc.sbuf_tensor(name, shape, dt))

        def psum(name, shape, dt=F32):
            return mem.enter_context(nc.psum_tensor(name, shape, dt))

        cin = sb("c_cin", [P, 4, D])
        st = sb("c_st", [P, 2, 6])
        mv = sb("c_mv", [P, 2, 2])
        ve = sb("c_ve", [P, 2, 1])
        rstd = sb("c_rstd", [P, 2, 1])
        xn = sb("c_xn", [P, 2, D])
        xf = sb("c_xf", [P, 2, 3, P])
        qf = sb("c_qf", [P, 2, 3, D])
        pp = sb("c_pp", [P, 2, 2, D])
        pf = [psum(f"c_pf{i}", [P, 4, P]) for i in range(2)]
        pq = [psum(f"c_pq{i}", [P, 4, P]) for i in range(2)]
        pc = [psum(f"c_pc{i}", [P, 4, P]) for i in range(2)]

        loaded = [sem(f"c_loaded{r}") for r in range(4)]
        stats = sem("c_stats")
        rstd_done = sem("c_rstd")
        normed = sem("c_normed")
        transformed = sem("c_transformed")
        f_out = sem("c_f_out")
        projected = sem("c_projected")
        q_out = sem("c_q_out")
        products = sem("c_products")
        inverted = sem("c_inverted")
        summed = sem("c_summed")
        idle = {e: sem(f"c_idle_{e}") for e in ("dve", "sp", "pool")}

        with nc.Block() as block:
            @block.sync
            def _(sp):
                def step(t, r):
                    if live(t, 0, n_tiles):
                        wait_apart(sp, transformed, t - 3, idle["sp"])
                        sp.dma_start(cin[:, r:r + 1, :], ctx[bass.ds(t, 1)].rearrange("a p d -> p a d")).then_inc(loaded[r], 16)
                pipeline(sp, n_tiles, 8, 4, step)

            @block.vector
            def _(dve):
                def stats_of(t, k):
                    wait_apart(dve, rstd_done, 2 * (t - 1), idle["dve"])
                    nc.vector.bn_stats(st[:, k % 2, :], x_res[:, bass.ds(t, 1), :]).then_inc(stats, 1)

                def aggregate(t, k):
                    wait_apart(dve, stats, 2 * t + 1, idle["dve"])
                    nc.vector.bn_aggr(mv[:, k % 2, :], st[:, k % 2, :]).then_inc(stats, 1)

                def norm(t, k):
                    at_least(dve, rstd_done, 2 * t + 2)
                    at_least(dve, transformed, t - 1)
                    nc.vector.tensor_scalar(xn[:, k % 2, :], x_res[:, bass.ds(t, 1), :], mv[:, k % 2, 0:1], rstd[:, k % 2, :],
                                            ALU.subtract, ALU.mult).then_inc(normed, 1)

                def bias(t, k):
                    at_least(dve, projected, t + 1)
                    at_least(dve, products, t - 1)
                    nc.vector.tensor_tensor(qf[:, k % 2], pq[k % 2][:, 0:3, :], cst["fbias"][:, 0:3, :], ALU.add)
                    nc.vector.tensor_tensor(vf[:, bass.ds(t, 1), :], pq[k % 2][:, 3:4, :], cst["fbias"][:, 3:4, :],
                                            ALU.add).then_inc(q_out, 1)

                def head_sum(t, k):
                    wait_apart(dve, inverted, t + 1, idle["dve"])
                    nc.vector.tensor_reduce(corr[:, bass.ds(t, 1), :], pc[k % 2][:, 0, :].rearrange("p (h d) -> p h d", d=HD),
                                            AX.X, ALU.add).then_inc(summed, 1)

                order = ((stats_of, 0), (head_sum, 6), (bias, 3), (aggregate, 0), (norm, 1))
                pipeline(dve, n_tiles, 8, 4, in_order(order, n_tiles))

            @block.gpsimd
            def _(pool):
                def inverse_root(t, k):
                    wait_apart(pool, stats, 2 * t + 2, idle["pool"])
                    wait_apart(pool, normed, t - 1, idle["pool"])
                    nc.gpsimd.tensor_scalar(ve[:, k % 2, :], mv[:, k % 2, 1:2], 1e-5, None, ALU.add).then_inc(rstd_done, 1)
                    at_least(pool, rstd_done, 2 * t + 1)
                    nc.gpsimd.tensor_tensor(rstd[:, k % 2, :], ve[:, k % 2, :], cst["mhalf"][:], ALU.pow).then_inc(rstd_done, 1)

                def multiply(t, k):
                    at_least(pool, q_out, t + 1)
                    at_least(pool, inverted, t - 1)
                    nc.gpsimd.tensor_tensor(pp[:, k % 2], qf[:, k % 2, 0, :].unsqueeze(1).to_broadcast([P, 2, D]), qf[:, k % 2, 1:3, :],
                                            ALU.mult).then_inc(products, 1)

                pipeline(pool, n_tiles, 8, 4, in_order(((multiply, 4), (inverse_root, 0)), n_tiles))

            @block.scalar
            def _(act):
                def spectra_out(t, k):
                    at_least(act, transformed, t + 1)
                    at_least(act, projected, t - 1)
                    nc.scalar.copy(xf[:, k % 2], pf[k % 2][:, 0:3, :]).then_inc(f_out, 1)

                pipeline(act, n_tiles, 8, 4, in_order(((spectra_out, 2),), n_tiles))

            @block.tensor
            def _(pe):
                def transform(t, k):
                    at_least(pe, normed, t + 1)
                    at_least(pe, loaded[k], (t // 4) * 16 + 16 if isinstance(t, int) else (t - k) * 4 + 16)
                    at_least(pe, f_out, t - 1)
                    nc.tensor.matmul(pf[k % 2][:, 0, :], xn[:, k % 2, :], cst["dft"][:, 0:P], start=True, stop=True)
                    nc.tensor.matmul(pf[k % 2][:, 1:3, :], cin[:, k, :], cst["dft"][:], start=True, stop=True).then_inc(transformed, 1)

                def project(t, k):
                    at_least(pe, f_out, t + 1)
                    at_least(pe, q_out, t - 1)
                    for j, (src, w) in enumerate(((0, 0), (1, 1), (2, 1), (1, 2))):
                        ins = nc.tensor.matmul(pq[k % 2][:, j, :], xf[:, k % 2, src, :], cst["w1T"][:, w, :], start=True, stop=True)
                    ins.then_inc(projected, 1)

                def invert(t, k):
                    at_least(pe, products, t + 1)
                    at_least(pe, summed, t - 1)
                    for j in range(2):
                        ins = nc.tensor.matmul(pc[k % 2][:, 0, :], cst["idft_corr"][:, j * P:j * P + P], pp[:, k % 2, j, :],
                                               start=(j == 0), stop=(j == 1))
                    ins.then_inc(inverted, 1)

                pipeline(pe, n_tiles, 8, 4, in_order(((project, 3), (transform, 2), (invert, 5)), n_tiles))


def delays(nc, cst, corr, cf, sem):
    G = TILES // 8
    with ExitStack() as mem:
        def sb(name, shape, dt=F32):
            return mem.enter_context(nc.sbuf_tensor(name, shape, dt))

        ext = sb("d_ext", [P, 2 * G, S + TOP - DELAYS])
        rep = sb("d_rep", [P, 2 * G, S + TOP - DELAYS])
        m8 = sb("d_m8", [P, 2 * G, TOP])
        e = sb("d_e", [P, 2 * G, S])
        w = sb("d_w", [P, 2 * G, S])
        wsum = sb("d_wsum", [P, 2 * G])
        cT = sb("d_cT", [P, G, P])
        pc = mem.enter_context(nc.psum_tensor("d_pc", [P, G, P], F32))
        pa = mem.enter_context(nc.psum_tensor("d_pa", [P, G, P], F32))
        pb = mem.enter_context(nc.psum_tensor("d_pb", [P, G, P], F32))
        turned = sem("d_turned")
        chain = sem("d_chain")
        shifted = sem("d_shifted")
        exped = sem("d_exped")
        weights = sem("d_weights")
        w_turned = sem("d_w_turned")
        w_out = sem("d_w_out")
        transformed = sem("d_transformed")

        with nc.Block() as block:
            @block.tensor
            def _(pe):
                for g in range(G):
                    ins = nc.tensor.transpose(pc[:, g, :], corr[:, 8 * g:8 * g + 8, :].rearrange("p t h -> p (t h)"), cst["ident"][:])
                ins.then_inc(turned, 1)
                pe.wait_ge(weights, 1)
                for g in range(G):
                    ins = nc.tensor.transpose(pc[:, g, :], w[:, 2 * g:2 * g + 2, :].rearrange("p b d -> p (b d)"), cst["ident"][:])
                ins.then_inc(w_turned, 1)
                pe.wait_ge(w_out, 1)
                for k, out in enumerate((pa, pb)):
                    for h in range(2):
                        ins = nc.tensor.matmul(out[:, 4 * h:4 * h + 4, :], cst["dft"][:, k * P:k * P + P], cT[:, 4 * h:4 * h + 4, :],
                                               start=True, stop=True)
                    ins.then_inc(transformed, 1)

            @block.vector
            def _(dve):
                nc.vector.memset(ext[:, :, S:], SENTINEL).then_inc(chain, 1)
                dve.wait_ge(turned, 1)
                nc.vector.tensor_copy(ext[:, :, 0:S], pc[:].rearrange("p g (b d) -> p (g b) d", b=2)).then_inc(chain, 1)
                dve.wait_ge(chain, 2)
                for g in range(2 * G):
                    ins = nc.vector.max(out=m8[:, g, :], in_=ext[:, g, :])
                ins.then_inc(chain, 1)
                dve.wait_ge(chain, 3)
                nc.vector.tensor_tensor(e[:], ext[:, :, 0:S], m8[:, :, TOP - DELAYS:TOP - DELAYS + 1].to_broadcast([P, 2 * G, S]),
                                        ALU.subtract).then_inc(shifted, 1)
                for g in range(2 * G):
                    ins = nc.vector.match_replace(out=rep[:, g, :], in_to_replace=m8[:, g, :], in_values=ext[:, g, :],
                                                  imm_value=-SENTINEL)
                ins.then_inc(chain, 1)
                dve.wait_ge(chain, 4)
                nc.vector.tensor_tensor(w[:], rep[:, :, 0:S], ext[:, :, 0:S], ALU.not_equal).then_inc(chain, 1)
                dve.wait_ge(chain, 5)
                dve.wait_ge(exped, 1)
                nc.vector.tensor_tensor(w[:], w[:], e[:], ALU.mult).then_inc(chain, 1)
                dve.wait_ge(chain, 6)
                nc.vector.tensor_reduce(wsum[:], w[:], AX.X, ALU.add).then_inc(chain, 1)
                dve.wait_ge(chain, 7)
                nc.vector.reciprocal(wsum[:], wsum[:]).then_inc(chain, 1)
                dve.wait_ge(chain, 8)
                nc.vector.tensor_tensor(w[:], w[:], wsum[:].unsqueeze(2).to_broadcast([P, 2 * G, S]), ALU.mult).then_inc(weights, 1)

            @block.scalar
            def _(act):
                act.wait_ge(shifted, 1)
                nc.scalar.activation(e[:], e[:], ACT.Exp).then_inc(exped, 1)
                act.wait_ge(w_turned, 1)
                nc.scalar.copy(cT[:], pc[:]).then_inc(w_out, 1)
                for k, src in enumerate((pa, pb)):
                    act.wait_ge(transformed, k + 1)
                    nc.scalar.copy(cf[:, k].rearrange("p t h -> p (t h)"), src[:].rearrange("p g c -> p (g c)"))


def mix(nc, cst, x_res, vf, cf, xnT, amax, sem, n_tiles=TILES):
    with ExitStack() as mem:
        def sb(name, shape, dt=F32):
            return mem.enter_context(nc.sbuf_tensor(name, shape, dt))

        rr = sb("m_rr", [P, 2, 2, D])
        oT = sb("m_oT", [P, 2, P])
        st = sb("m_st", [P, 2, 6])
        mv = sb("m_mv", [P, 2, 2])
        ve = sb("m_ve", [P, 2, 1])
        rstd = sb("m_rstd", [P, 2, 1])
        xn = sb("m_xn", [P, 2, D])
        po = [mem.enter_context(nc.psum_tensor(f"m_po{i}", [P, 4, P], F32)) for i in range(2)]
        py = [mem.enter_context(nc.psum_tensor(f"m_py{i}", [P, 4, P], F32)) for i in range(2)]
        pt = [mem.enter_context(nc.psum_tensor(f"m_pt{i}", [P, 4, P], F32)) for i in range(2)]
        products = sem("m_products")
        products2 = sem("m_products2")
        inverted = sem("m_inverted")
        o_out = sem("m_o_out")
        projected = sem("m_projected")
        added = sem("m_added")
        stats = sem("m_stats")
        rstd_done = sem("m_rstd")
        normed = sem("m_normed")
        turned = sem("m_turned")
        t_out = sem("m_t_out")
        idle = {e: sem(f"m_idle_{e}") for e in ("dve", "act", "pool")}

        with nc.Block() as block:
            def product(eng, t, k, j):
                return eng.tensor_tensor(
                    rr[:, k % 2, j].rearrange("p (h d) -> p h d", d=HD),
                    vf[:, bass.ds(t, 1), :].rearrange("p a (h d) -> p (a h) d", d=HD),
                    cf[:, j, bass.ds(t, 1), :].rearrange("p a h -> p (a h)").unsqueeze(2).to_broadcast([P, H, HD]), ALU.mult)

            @block.gpsimd
            def _(pool):
                def multiply(t, k):
                    wait_apart(pool, inverted, t - 1, idle["pool"])
                    product(nc.gpsimd, t, k, 0).then_inc(products, 1)

                def inverse_root(t, k):
                    wait_apart(pool, stats, 2 * t + 2, idle["pool"])
                    wait_apart(pool, normed, t - 1, idle["pool"])
                    nc.gpsimd.tensor_scalar(ve[:, k % 2, :], mv[:, k % 2, 1:2], 1e-3, None, ALU.add).then_inc(rstd_done, 1)
                    at_least(pool, rstd_done, 2 * t + 1)
                    nc.gpsimd.tensor_tensor(rstd[:, k % 2, :], ve[:, k % 2, :], cst["mhalf"][:], ALU.pow).then_inc(rstd_done, 1)

                pipeline(pool, n_tiles, 12, 2, in_order(((multiply, 0), (inverse_root, 4)), n_tiles))

            @block.vector
            def _(dve):
                def multiply(t, k):
                    wait_apart(dve, inverted, t - 1, idle["dve"])
                    product(nc.vector, t, k, 1).then_inc(products2, 1)

                def add(t, k):
                    at_least(dve, projected, t + 1)
                    nc.vector.tensor_tensor(x_res[:, bass.ds(t, 1), :], x_res[:, bass.ds(t, 1), :], py[k % 2][:, 0:1, :],
                                            ALU.add).then_inc(added, 1)

                def stats_of(t, k):
                    wait_apart(dve, added, t + 1, idle["dve"])
                    wait_apart(dve, rstd_done, 2 * (t - 1), idle["dve"])
                    nc.vector.bn_stats(st[:, k % 2, :], x_res[:, bass.ds(t, 1), :]).then_inc(stats, 1)

                def aggregate(t, k):
                    wait_apart(dve, stats, 2 * t + 1, idle["dve"])
                    nc.vector.bn_aggr(mv[:, k % 2, :], st[:, k % 2, :]).then_inc(stats, 1)

                def norm(t, k):
                    at_least(dve, rstd_done, 2 * t + 2)
                    at_least(dve, turned, t - 1)
                    nc.vector.tensor_scalar(xn[:, k % 2, :], x_res[:, bass.ds(t, 1), :], mv[:, k % 2, 0:1], rstd[:, k % 2, :],
                                            ALU.subtract, ALU.mult).then_inc(normed, 1)

                def largest(t, k):
                    wait_apart(dve, t_out, t + 1, idle["dve"])
                    nc.vector.tensor_reduce(amax[:, bass.ds(t, 1)], xnT[:, bass.ds(t * P, P)], AX.X, ALU.max,
                                            apply_absolute_value=True)

                order = ((stats_of, 4), (multiply, 0), (add, 3), (aggregate, 4), (largest, 8), (norm, 5))
                pipeline(dve, n_tiles, 12, 2, in_order(order, n_tiles))

            @block.scalar
            def _(act):
                def o_copy(t, k):
                    at_least(act, inverted, t + 1)
                    at_least(act, projected, t - 1)
                    nc.scalar.copy(oT[:, k % 2], po[k % 2][:, 0, :]).then_inc(o_out, 1)

                def affine(t, k):
                    wait_apart(act, turned, t + 1, idle["act"])
                    nc.scalar.activation(xnT[:, bass.ds(t * P, P)], pt[k % 2][:, 0, :], ACT.Identity,
                                         bias=cst["ln_beta"][:], scale=cst["ln_gamma"][:]).then_inc(t_out, 1)

                pipeline(act, n_tiles, 12, 2, in_order(((o_copy, 1), (affine, 7)), n_tiles))

            @block.tensor
            def _(pe):
                def invert(t, k):
                    at_least(pe, products, t + 1)
                    at_least(pe, products2, t + 1)
                    at_least(pe, o_out, t - 1)
                    for j in range(2):
                        ins = nc.tensor.matmul(po[k % 2][:, 0, :], rr[:, k % 2, j, :], cst["idft_conv"][:, j * P:j * P + P],
                                               start=(j == 0), stop=(j == 1))
                    ins.then_inc(inverted, 1)

                def project(t, k):
                    at_least(pe, o_out, t + 1)
                    at_least(pe, added, t - 1)
                    nc.tensor.matmul(py[k % 2][:, 0, :], oT[:, k % 2], cst["w1T"][:, 3, :], start=True, stop=False)
                    nc.tensor.matmul(py[k % 2][:, 0, :], cst["ones"][0:1, :], cst["bo1"][:], start=False, stop=True).then_inc(projected, 1)

                def turn(t, k):
                    at_least(pe, normed, t + 1)
                    at_least(pe, t_out, t - 1)
                    nc.tensor.transpose(pt[k % 2][:, 0, :], xn[:, k % 2, :], cst["ident"][:]).then_inc(turned, 1)

                pipeline(pe, n_tiles, 12, 2, in_order(((project, 2), (turn, 6), (invert, 1)), n_tiles))


def ternary(nc, cst, x_res, xnT, amax, out, sem, chunks=TILES // 4):
    with ExitStack() as mem:
        def sb(name, shape, dt=F32):
            return mem.enter_context(nc.sbuf_tensor(name, shape, dt))

        gcol = sb("t_gcol", [P, 1])
        grow = sb("t_grow", [1, 1])
        bound = sb("t_bound", [P, 2])
        xq = sb("t_xq", [P, 2, 4, P])
        res = sb("t_res", [P, 2, 4, D])
        pg = mem.enter_context(nc.psum_tensor("t_pg", [P, 512], F32))
        py = [mem.enter_context(nc.psum_tensor(f"t_py{i}", [P, 4, P], F32)) for i in range(2)]
        chain = sem("t_chain")
        across = sem("t_across")
        clipped = sem("t_clipped")
        multiplied = sem("t_multiplied")
        summed = sem("t_summed")
        stored = [sem(f"t_stored{i}") for i in range(2)]
        idle = {e: sem(f"t_idle_{e}") for e in ("dve", "sp")}

        with nc.Block() as block:
            @block.vector
            def _(dve):
                nc.vector.tensor_reduce(gcol[:], amax[:, 0:4 * chunks], AX.X, ALU.max).then_inc(chain, 1)
                dve.wait_ge(across, 1)
                nc.vector.tensor_reduce(grow[:], pg[0:1, 0:P], AX.X, ALU.max).then_inc(chain, 1)
                dve.wait_ge(across, 2)
                edge = float(np.float32(QB - 1e-5)) / QB
                nc.vector.tensor_scalar(bound[:, 0:1], pg[:, P:P + 1], edge, None, ALU.mult)
                nc.vector.tensor_scalar(bound[:, 1:2], pg[:, P:P + 1], -edge, None, ALU.mult).then_inc(chain, 1)
                dve.wait_ge(chain, 3)

                def step(c, r):
                    if live(c, 0, chunks):
                        at_least(dve, multiplied, c - 1)
                        nc.vector.tensor_scalar(xq[:, r].rearrange("p j t -> p (j t)"), xnT[:, bass.ds(c * 512, 512)],
                                                bound[:, 0:1], bound[:, 1:2], ALU.min, ALU.max).then_inc(clipped, 1)
                    if live(c, 1, chunks):
                        at_least(dve, multiplied, c)
                        at_least(dve, stored[1 - r], (c - 1) // 2 * 16 if isinstance(c, int) else (c - 1 - (1 - r)) * 8)
                        nc.vector.scalar_tensor_tensor(res[:, 1 - r].rearrange("p j d -> p (j d)"), py[1 - r][:].rearrange("p j d -> p (j d)"),
                                                       cst["beta"][:], x_res[:, bass.ds((c - 1) * 4, 4), :].rearrange("p j d -> p (j d)"),
                                                       ALU.mult, ALU.add).then_inc(summed, 1)
                pipeline(dve, chunks, 3, 2, step)

            @block.tensor
            def _(pe):
                pe.wait_ge(chain, 1)
                nc.tensor.transpose(pg[0:1, 0:P], gcol[:], cst["ident"][:]).then_inc(across, 1)
                pe.wait_ge(chain, 2)
                nc.tensor.matmul(pg[:, P:P + 1], cst["ones"][0:1, :], grow[:], start=True, stop=True).then_inc(across, 1)

                def step(c, r):
                    if live(c, 0, chunks):
                        at_least(pe, clipped, c + 1)
                        at_least(pe, summed, c - 1)
                        for j in range(4):
                            ins = nc.tensor.matmul(py[r][:, j, :], xq[:, r, j, :], cst["wt"][:], start=True, stop=True)
                        ins.then_inc(multiplied, 1)
                pipeline(pe, chunks, 3, 2, step)

            @block.sync
            def _(sp):
                def step(c, r):
                    if live(c, 1, chunks):
                        wait_apart(sp, summed, c, idle["sp"])
                        sp.dma_start(out[bass.ds((c - 1) * 4, 4)].rearrange("j p d -> p j d"), res[:, 1 - r]).then_inc(stored[1 - r], 16)
                pipeline(sp, chunks, 3, 2, step)
                for q in stored:
                    sp.wait_ge(q, 16 * (chunks // 2))


def host_tables():
    r = np.arange(S)
    return {
        "ident": np.eye(P, dtype=np.float32),
        "ident16": np.eye(P, dtype=np.float16),
        "hmask": np.kron(np.ones((2, 1)), np.kron(np.eye(8), np.ones((HD, 1)))).astype(np.float32),
        "maskq": np.tile(np.where(r[:, None] > r[None, :], -BIG, 0.0), (1, 2)).astype(np.float32),
        "maskk": np.tile(np.eye(S), (1, 8)).astype(np.float32),
        "sel": np.kron(np.arange(P)[:, None] % E == np.arange(E)[None, :], np.ones((1, FH))).astype(np.float16),
        **{k: v.astype(np.float32) for k, v in dft_tables().items()},
    }


def two_layers(nc, d, out):
    with ExitStack() as mem:
        def sb(name, shape, dt=F32):
            return mem.enter_context(nc.sbuf_tensor(name, shape, dt))

        def sem(name):
            return mem.enter_context(nc.semaphore(name))

        shapes = {
            "ident": ([P, P], F32), "ident16": ([P, P], F16), "hmask": ([P, 8], F32), "maskq": ([S, P], BF16),
            "maskk": ([S, 512], BF16), "ones": ([P, P], F32), "mhalf": ([P, 1], F32),
            "Wq": ([D, D], F32), "Wo": ([D, D], F32), "bqH": ([P, 2], F32), "bqs": ([P, 2], F32), "boe": ([P, D], F32),
            "centT": ([D, E], F32), "eb": ([P, E], F32),
            "w1T": ([D, 4, D], F32), "fbias": ([P, 4, D], F32), "bo1": ([1, D], F32),
            "dft": ([P, 2 * P], F32), "idft_corr": ([P, 2 * P], F32), "idft_conv": ([P, 2 * P], F32),
            "ln_gamma": ([D, 1], F32), "ln_beta": ([D, 1], F32), "beta": ([P, 1], F32), "wt": ([D, D], F32),
        }
        cst = {name: sb(name, shape, dt) for name, (shape, dt) in shapes.items()}
        x_res = sb("x_res", [P, TILES, D])
        tile = "(t p) s d -> t (p s) d"
        x = d["x"].rearrange(tile, p=2)
        ctx = d["ctx"].rearrange(tile, p=2)
        with ExitStack() as ffn:
            for name in ("wuh", "wul", "wdh", "wdl"):
                cst[name] = ffn.enter_context(nc.sbuf_tensor(name, [P, PAIRS * P], F32R))
            cwT = ffn.enter_context(nc.sbuf_tensor("cwT", [P, TILES * P], F16))
            setup(nc, cst, d, sem)
            attention(nc, cst, x, ctx, x_res, sem)
            with nc.sbuf_tensor("xnT", [P, TILES * P + 512], F32) as xnT:
                router(nc, cst, x_res, xnT, cwT, sem)
                experts(nc, cst, d, x_res, xnT, cwT, sem)
        xnT2 = sb("xnT2", [P, TILES * P])
        vf = sb("vf", [P, TILES, D])
        corr = sb("corr", [P, TILES, H])
        cf = sb("cf", [P, 2, TILES, H])
        amax = sb("amax", [P, TILES])
        spectrum(nc, cst, ctx, x_res, vf, corr, sem)
        delays(nc, cst, corr, cf, sem)
        mix(nc, cst, x_res, vf, cf, xnT2, amax, sem)
        ternary(nc, cst, x_res, xnT2, amax, out.rearrange(tile, p=2), sem)


_NAMES = {
    "x": "x", "ctx": "ctx_1024", "Wq": "L0_xattn_Wq", "bq": "L0_xattn_bq", "Wo": "L0_xattn_Wo", "bo": "L0_xattn_bo",
    "centroids": "L0_ffn_centroids", "eb": "L0_ffn_expert_biases", "Ws_up": "L0_ffn_Ws_up", "Ws_down": "L0_ffn_Ws_down",
    "W_up": "L0_ffn_W_up", "W_down": "L0_ffn_W_down",
    "Wq1": "L1_xattn_Wq", "bq1": "L1_xattn_bq", "Wk1": "L1_xattn_Wk", "bk1": "L1_xattn_bk",
    "Wv1": "L1_xattn_Wv", "bv1": "L1_xattn_bv", "Wo1": "L1_xattn_Wo", "bo1": "L1_xattn_bo",
    "wt": "L1_ffn_weight", "ln_gamma": "L1_ffn_ln_gamma", "ln_beta": "L1_ffn_ln_beta",
}


def kernel(**inputs):
    import concourse.bacc as _bacc
    from concourse.bass_utils import run_bass_kernel_spmd as _run

    nc = _bacc.Bacc("TRN2", target_bir_lowering=False, num_devices=1)
    arrays, d = {}, {}
    for short, name in _NAMES.items():
        a = np.ascontiguousarray(inputs[name])
        arrays[f"in_{name}_dram"] = a
        d[short] = nc.dram_tensor(f"in_{name}_dram", a.shape, mybir.dt.from_np(a.dtype), kind="ExternalInput").ap()
    for name, a in host_tables().items():
        arrays[f"table_{name}_dram"] = a
        d[name] = nc.dram_tensor(f"table_{name}_dram", a.shape, mybir.dt.from_np(a.dtype), kind="ExternalInput").ap()
    out = nc.dram_tensor("out_0_dram", (2 * TILES, S, D), F32, kind="ExternalOutput").ap()
    two_layers(nc, d, out)
    r = _run(nc, [arrays], core_ids=[0])
    return r.results[0]["out_0_dram"]
```

```python
from contextlib import ExitStack

import numpy as np

import concourse.bass as bass
from concourse import mybir

F32 = mybir.dt.float32
F32R = mybir.dt.float32r
BF16 = mybir.dt.bfloat16
F16 = mybir.dt.float16
I32 = mybir.dt.int32
ALU = mybir.AluOpType
ACT = mybir.ActivationFunctionType
AX = mybir.AxisListType

P = 128
S = 64
D = 128
TILES = 64
H = 16
HD = D // H
E = 64
FH = 64
PAIRS = E // 2 + 1
TOP = 8
DELAYS = 4
QB = 128.0
BIG = 1e10
SENTINEL = 3.0e38


def at_least(eng, sem, value):
    if isinstance(value, int) and value <= 0:
        return
    eng.wait_ge(sem, value)


def wait_apart(eng, sem, value, idle):
    at_least(eng, sem, value)
    if not isinstance(value, int):
        eng.sem_inc(idle, 1)


def pipeline(eng, count, lag, unroll, step):
    first = -(-lag // unroll) * unroll
    for t in range(first):
        step(t, t % unroll)
    with eng.Fori(first // unroll, count // unroll) as g:
        for r in range(unroll):
            step(g * unroll + r, r)
    for t in range(count, count + lag):
        step(t, t % unroll)


def live(t, lag, count):
    return not isinstance(t, int) or 0 <= t - lag < count


def in_order(stages, count):
    def step(t, r):
        for stage, lag in stages:
            if live(t, lag, count):
                stage(t - lag, (r - lag) % 4)
    return step


def setup(nc, cst, dram, sem):
    landed = sem("s_landed")
    made = sem("s_made")
    done = sem("s_done")
    bias = sem("s_bias")
    with ExitStack() as mem:
        bqB = mem.enter_context(nc.sbuf_tensor("s_bqB", [P, P], F32))
        borow = mem.enter_context(nc.sbuf_tensor("s_borow", [1, P], F32))
        onerow = mem.enter_context(nc.sbuf_tensor("s_onerow", [1, P], F32))
        pbias = mem.enter_context(nc.psum_tensor("s_pbias", [P, 512], F32))
        loads = [(cst[name][:], dram[name]) for name in ("ident", "ident16", "hmask", "Wq", "Wo")]
        loads += [(cst["bqc"][:], dram["bq"].unsqueeze(1)), (borow[:], dram["bo"].unsqueeze(0))]
        cent = mem.enter_context(nc.sbuf_tensor("s_cent", [E, D], F32))
        loads += [(cent[:], dram["centroids"]), (cst["eb"][:], dram["eb"].unsqueeze(0).to_broadcast([P, E]))]
        w1 = mem.enter_context(nc.sbuf_tensor("s_w1", [P, 4, P], F32))
        loads += [(w1[:, k, :], dram[name]) for k, name in enumerate(("Wq1", "Wk1", "Wv1", "Wo1"))]
        loads += [(cst[name][:], dram[name]) for name in ("dft", "idft_corr", "idft_conv")]
        loads += [(cst["bo1"][:], dram["bo1"].unsqueeze(0).to_broadcast([P, D]))]
        loads += [(cst[name][:], dram[name].unsqueeze(1)) for name in ("ln_gamma", "ln_beta")]
        mask_raw = mem.enter_context(nc.sbuf_tensor("s_mask", [P, P + 512], F32))
        loads += [(mask_raw[:, 0:P], dram["maskq"]), (mask_raw[:, P:], dram["maskk"])]
        wt_raw = mem.enter_context(nc.sbuf_tensor("s_wt", [P, D], F32))
        loads += [(wt_raw[:], dram["wt"])]
        wabs = mem.enter_context(nc.sbuf_tensor("s_wabs", [P, 1], F32))
        wrec = mem.enter_context(nc.sbuf_tensor("s_wrec", [P, 1], F32))
        pw = mem.enter_context(nc.psum_tensor("s_pw", [P, 4, P], F32))
        w_turned = sem("s_w_turned")
        w_chain = sem("s_w_chain")
        zeroed = sem("s_zeroed")
        spectral_loads = [(cst["fbias"][64 * b:64 * b + 1, k, :], dram[name].unsqueeze(0))
                        for b in range(2) for k, name in ((0, "bq1"), (1, "bk1"), (3, "bv1"))]
        with nc.Block() as block:
            @block.gpsimd
            def _(pool):
                nc.gpsimd.memset(cst["fbias"][:], 0.0).then_inc(zeroed, 1)

            def load(eng, pairs):
                with nc.allow_non_contiguous_dma("biases by column, 128 words each"):
                    for dst, src in pairs:
                        eng.dma_start(dst, src).then_inc(landed, 16)

            @block.sync
            def _(sp):
                load(sp, loads[::2])
                sp.wait_ge(zeroed, 1)
                load(sp, spectral_loads[::2])

            @block.scalar
            def _(act):
                load(act, loads[1::2])
                act.wait_ge(zeroed, 1)
                load(act, spectral_loads[1::2])

            @block.vector
            def _(dve):
                nc.vector.memset(cst["mhalf"][:], -0.5)
                nc.vector.memset(cst["ones"][:], 1.0)
                nc.vector.memset(onerow[:], 1.0).then_inc(made, 1)
                dve.wait_ge(landed, 16 * (len(loads) + len(spectral_loads)))
                nc.vector.tensor_copy(cst["maskq"][:], mask_raw[:, 0:P])
                nc.vector.tensor_copy(cst["maskk"][:], mask_raw[:, P:])
                nc.vector.tensor_scalar(cst["bqs"][:], cst["bqc"][:], float(HD) ** -0.5, None, ALU.mult)
                nc.vector.tensor_copy(bqB[:], cst["bqc"][:].to_broadcast([P, P])).then_inc(made, 1)
                dve.wait_ge(bias, 1)
                nc.vector.tensor_copy(cst["centT"][:], pbias[:, P:P + E]).then_inc(done, 1)
                nc.vector.tensor_copy(cst["boe"][:], pbias[:, 0:P]).then_inc(done, 1)
                nc.vector.tensor_scalar(cst["fbias"][:], cst["fbias"][:], float(S), None, ALU.mult)
                dve.wait_ge(w_turned, 1)
                nc.vector.tensor_copy(cst["w1T"][:], pw[:]).then_inc(done, 1)
                nc.vector.tensor_reduce(wabs[:], wt_raw[:], AX.X, ALU.add, apply_absolute_value=True).then_inc(w_chain, 1)
                dve.wait_ge(w_turned, 2)
                nc.vector.tensor_scalar(cst["beta"][:], pbias[:, 256:257], 1.0 / (D * D), None, ALU.mult).then_inc(w_chain, 1)
                dve.wait_ge(w_chain, 2)
                nc.vector.tensor_scalar(wrec[:], cst["beta"][:], 1e-5, None, ALU.add).then_inc(w_chain, 1)
                dve.wait_ge(w_chain, 3)
                nc.vector.reciprocal(wabs[:], wrec[:]).then_inc(w_chain, 1)
                dve.wait_ge(w_chain, 4)
                nc.vector.tensor_scalar(cst["wt"][:], wt_raw[:], wabs[:], 1.5 * 2 ** 23, ALU.mult, ALU.add).then_inc(w_chain, 1)
                dve.wait_ge(w_chain, 5)
                nc.vector.tensor_scalar(cst["wt"][:], cst["wt"][:], 1.5 * 2 ** 23, 1.0, ALU.subtract, ALU.min).then_inc(w_chain, 1)
                dve.wait_ge(w_chain, 6)
                nc.vector.tensor_scalar(cst["wt"][:], cst["wt"][:], -1.0, None, ALU.max).then_inc(done, 1)
                dve.wait_ge(done, 4)

            @block.tensor
            def _(pe):
                pe.wait_ge(made, 2)
                pe.wait_ge(landed, 16 * (len(loads) + len(spectral_loads)))
                nc.tensor.transpose(pbias[:, P:P + E], cent[:], cst["ident"][0:E, 0:E])
                nc.tensor.matmul(pbias[:, 0:P], bqB[:], cst["Wo"][:], start=True, stop=False)
                nc.tensor.matmul(pbias[:, 0:P], onerow[:], borow[:], start=False, stop=True).then_inc(bias, 1)

                for k in range(4):
                    ins = nc.tensor.transpose(pw[:, k, :], w1[:, k, :], cst["ident"][:])
                ins.then_inc(w_turned, 1)
                pe.wait_ge(w_chain, 1)
                pe.wait_ge(done, 3)
                nc.tensor.matmul(pbias[:, 256:257], cst["ones"][:], wabs[:], start=True, stop=True).then_inc(w_turned, 1)


def attention(nc, cst, dram, x, ctxT, x_res, norms, sem, n_tiles=TILES):
    peeled = 16
    pieces = n_tiles // 4 - peeled // 4
    piece = PAIRS * P // pieces
    with ExitStack() as mem:
        def sb(name, shape, dt=F32):
            return mem.enter_context(nc.sbuf_tensor(name, shape, dt))

        def psum(name, shape, dt=F32):
            return mem.enter_context(nc.psum_tensor(name, shape, dt))

        st = sb("a_stats", [P, 2, 6])
        mv = sb("a_mv", [P, 2, 2])
        ve = sb("a_ve", [P, 2, 1])
        rstd = sb("a_rstd", [P, 2, 1])
        xn = sb("a_xn", [P, 2, D])
        xcT = sb("xcT", [P, 4, 2, P])
        qT = sb("qT", [P, 2, 2, S])
        kT = sb("kT", [P, 2, 2, S])
        kx = sb("kx", [P, 2, 2, 8, S])
        vx = sb("vx", [P, 4, 8, 2, 2, 9])
        prob = sb("prob", [P, 2, H, S])
        raw = sb("raw", [P, 2, PAIRS * P])
        pT = sb("pT", [P, 2, 8, P])
        mx = sb("mx", [P, 2, H])
        rden = sb("rden", [P, 2, H])
        o = sb("o", [P, 2, H, HD])
        oT = sb("oT", [P, 2, P])

        pt_in = psum("pt_in", [P, 4, P])
        pj = psum("pj", [P, 4, P])
        ps = psum("ps", [P, H, S])
        ppT = psum("ppT", [P, 8, P])
        po = psum("po", [P, 512])[:, 0:144].rearrange("p (h d) -> p h d", d=9)
        pb = psum("pb", [P, 4, P])

        loaded = [sem(f"a_loaded{r}") for r in range(4)]
        stats = sem("a_stats_done")
        mean_var = sem("a_mean_var")
        rstd_done = sem("a_rstd_done")
        normed = sem("a_normed")
        biased = sem("a_biased")
        turned = sem("a_turned")
        turned_out = sem("a_turned_out")
        projected = sem("a_projected")
        split_out = sem("a_split_out")
        keys = [sem(f"a_keys{b}") for b in range(2)]
        scored = sem("a_scored")
        maxed = sem("a_maxed")
        shifted = sem("a_shifted")
        exped = sem("a_exped")
        p_turned = sem("a_p_turned")
        p_out = sem("a_p_out")
        weighed = sem("a_weighed")
        recip = sem("a_recip")
        scaled = sem("a_scaled")
        o_turned = sem("a_o_turned")
        o_out = sem("a_o_out")
        wo_done = sem("a_wo_done")
        added = sem("a_added")
        preset = sem("a_preset")
        raw_padded = sem("a_raw_padded")
        raw_landed = sem("a_raw_landed")
        high = sem("a_high")
        idle = {e: sem(f"a_idle_{e}") for e in ("dve", "sp", "pool")}

        def expand(eng, ops, t, r, b):
            at_least(eng, split_out, t + 1)
            at_least(eng, scored, t - 1)
            ops.tensor_tensor(kx[:, r % 2, b], kT[:, r % 2, b, :].unsqueeze(1).to_broadcast([P, 8, S]),
                              cst["hmask"][:].unsqueeze(2).to_broadcast([P, 8, S]), ALU.mult).then_inc(keys[b], 1)

        with nc.Block() as block:
            @block.sync
            def _(sp):
                def step(t, r):
                    if not live(t, 0, n_tiles):
                        return
                    wait_apart(sp, projected, t - 3, idle["sp"])
                    wait_apart(sp, stats, 2 * (t - 3), idle["sp"])
                    sp.dma_start(x_res[:, bass.ds(t, 1), :], x[bass.ds(t, 1)].rearrange("a p d -> p a d")).then_inc(loaded[r], 16)
                    sp.dma_start(xcT[:, r, 1, :], ctxT[:, bass.ds(t * P, P)]).then_inc(loaded[r], 16)
                    if isinstance(t, int) and t in weight_loads:
                        at_least(sp, raw_padded, 1)
                        for dst, src in weight_loads[t]:
                            sp.dma_start(dst, src).then_inc(raw_landed, 16)
                weight_loads = {
                    5: [(raw[:, 0, 0:E // 2 * P].rearrange("p (e f) -> p e f", f=FH), dram["W_up"].rearrange("e d f -> d e f"))],
                    8: [(raw[64 * k:64 * k + 64, 1, 0:E // 2 * P].rearrange("f (j d) -> f j d", d=D),
                         dram["W_down"].rearrange("(j k) f d -> k f j d", k=2)[k]) for k in range(2)],
                    9: [(raw[:, 0, E // 2 * P:E // 2 * P + FH], dram["Ws_up"]), (raw[0:FH, 1, E // 2 * P:], dram["Ws_down"])],
                }
                pipeline(sp, n_tiles, peeled, 4, step)
                sp.wait_ge(raw_landed, 16 * 5)

            @block.vector
            def _(dve):
                def stats_of(t, r):
                    at_least(dve, loaded[r], t // 4 * 32 + 32 if isinstance(t, int) else (t - r) * 8 + 32)
                    wait_apart(dve, rstd_done, 2 * (t - 1), idle["dve"])
                    nc.vector.bn_stats(st[:, r % 2, :], x_res[:, bass.ds(t, 1), :]).then_inc(stats, 1)

                def aggregate(t, r):
                    wait_apart(dve, stats, 2 * t + 1, idle["dve"])
                    nc.vector.bn_aggr(mv[:, r % 2, :], st[:, r % 2, :]).then_inc(stats, 1)

                def norm(t, r):
                    at_least(dve, rstd_done, 2 * t + 2)
                    at_least(dve, turned, t - 1)
                    nc.vector.tensor_scalar(xn[:, r % 2, :], x_res[:, bass.ds(t, 1), :], mv[:, r % 2, 0:1],
                                            rstd[:, r % 2, :], ALU.subtract, ALU.mult).then_inc(normed, 1)

                def row_max(t, r):
                    at_least(dve, scored, t + 1)
                    nc.vector.tensor_reduce(mx[:, r % 2, :], ps[:], AX.X, ALU.max).then_inc(maxed, 1)

                def shift(t, r):
                    at_least(dve, maxed, t + 1)
                    at_least(dve, p_turned, t - 1)
                    nc.vector.tensor_tensor(prob[:, r % 2], ps[:], mx[:, r % 2, :].unsqueeze(2).to_broadcast([P, H, S]),
                                            ALU.subtract).then_inc(shifted, 1)

                def expand_keys(t, r):
                    expand(dve, nc.vector, t, r, 0)

                def invert_sum(t, r):
                    at_least(dve, weighed, t + 1)
                    nc.vector.reciprocal(rden[:, r % 2, :], po[:, :, 8]).then_inc(recip, 1)

                def scale_out(t, r):
                    at_least(dve, recip, t + 1)
                    at_least(dve, o_turned, t - 1)
                    nc.vector.tensor_tensor(o[:, r % 2], po[:, :, 0:8], rden[:, r % 2, :].unsqueeze(2).to_broadcast([P, H, HD]),
                                            ALU.mult).then_inc(scaled, 1)

                def add_out(t, r):
                    at_least(dve, wo_done, t + 1)
                    at_least(dve, biased, t + 1)
                    nc.vector.tensor_tensor(x_res[:, bass.ds(t, 1), :], x_res[:, bass.ds(t, 1), :], pb[:, 1:2, :],
                                            ALU.add).then_inc(added, 1)

                order = ((add_out, 7), (stats_of, 0), (invert_sum, 6), (aggregate, 0), (scale_out, 6), (expand_keys, 2),
                         (row_max, 3), (norm, 0), (shift, 3))
                turn = in_order(order, n_tiles)

                def step(t, r):
                    turn(t, r)
                    if isinstance(t, int) and t == n_tiles + 1:
                        at_least(dve, added, 4)
                        norms.take_stats(x_res, 0)
                    if isinstance(t, int) and t == n_tiles + 2:
                        norms.aggregate(dve, 0, idle["dve"])
                pipeline(dve, n_tiles, peeled, 4, step)

            @block.gpsimd
            def _(pool):
                nc.gpsimd.memset(raw[:, :, E // 2 * P:], 0.0).then_inc(raw_padded, 1)
                nc.gpsimd.memset(vx[:], 0.0).then_inc(preset, 1)
                pool.wait_ge(preset, 1)
                for d in range(2):
                    nc.gpsimd.memset(vx[64 * d:64 * d + 64, :, :, :, d, 8], 1.0).then_inc(preset, 1)

                pool.wait_ge(preset, 3)

                def low_part(t, k):
                    cols = bass.ds((t // 4 - peeled // 4) * piece, piece)
                    wait_apart(pool, high, t // 2 + k + 1, idle["pool"])
                    nc.gpsimd.tensor_tensor(cst[("wul", "wdl")[k]][:, cols], raw[:, k, cols],
                                            cst[("wuh", "wdh")[k]][:, cols].bitcast(F32), ALU.subtract)

                def step(t, r):
                    if live(t, 2, n_tiles):
                        expand(pool, nc.gpsimd, t - 2, (r - 2) % 4, 1)
                    if live(t, 0, n_tiles):
                        at_least(pool, stats, 2 * t + 2)
                        wait_apart(pool, normed, t - 1, idle["pool"])
                        nc.gpsimd.tensor_scalar(ve[:, r % 2, :], mv[:, r % 2, 1:2], 1e-5, None, ALU.add).then_inc(rstd_done, 1)
                        at_least(pool, rstd_done, 2 * t + 1)
                        nc.gpsimd.tensor_tensor(rstd[:, r % 2, :], ve[:, r % 2, :], cst["mhalf"][:], ALU.pow).then_inc(rstd_done, 1)
                    if live(t, 1, n_tiles):
                        at_least(pool, normed, t)
                        nc.gpsimd.tensor_tensor(x_res[:, bass.ds(t - 1, 1), :], x_res[:, bass.ds(t - 1, 1), :],
                                                cst["boe"][:].unsqueeze(1), ALU.add).then_inc(biased, 1)
                    if not isinstance(t, int) and r % 2 == 1:
                        low_part(t - r, r // 2)
                pipeline(pool, n_tiles, peeled, 4, step)
                pool.wait_ge(added, 4)
                norms.norm(pool, x_res, cst["mhalf"], 0, idle["pool"])
                nc.gpsimd.memset(x_res[:, n_tiles:n_tiles + 4, :], 0.0)

            @block.scalar
            def _(act):
                act.wait_ge(preset, 3)

                def probs_out(t, r):
                    at_least(act, p_turned, t + 1)
                    at_least(act, weighed, t - 1)
                    nc.scalar.copy(pT[:, r % 2], ppT[:]).then_inc(p_out, 1)

                def turned_copy(t, r):
                    at_least(act, turned, t + 1)
                    at_least(act, projected, t - 3)
                    nc.scalar.copy(xcT[:, r % 4, 0, :], pt_in[:, 0, :]).then_inc(turned_out, 1)

                def o_copy(t, r):
                    at_least(act, o_turned, t + 1)
                    at_least(act, wo_done, t - 1)
                    nc.scalar.copy(oT[:, r % 2], pb[:, 0, :]).then_inc(o_out, 1)

                def split(t, r):
                    at_least(act, projected, t + 1)
                    at_least(act, scored, t - 1)
                    for q in keys:
                        at_least(act, q, t - 1)
                    at_least(act, weighed, t - 3)
                    nc.scalar.activation(qT[:, r % 2].rearrange("p b q -> p (b q)"), pj[:, 0, :], ACT.Identity,
                                         bias=cst["bqs"][:], scale=float(HD) ** -0.5)
                    nc.scalar.activation(kT[:, r % 2].rearrange("p b q -> p (b q)"), pj[:, 1, :], ACT.Identity, bias=cst["bqc"][:])
                    for b in range(2):
                        for d in range(2):
                            ins = nc.scalar.copy(vx[64 * d:64 * d + 64, r % 4, :, b, d, 0:8],
                                                 pj[64 * b:64 * b + 64, 2, :].rearrange("p (a c d) -> p a c d", c=2, d=8)[:, :, d, :])
                    ins.then_inc(split_out, 1)

                def exponent(t, r):
                    at_least(act, shifted, t + 1)
                    nc.scalar.activation(prob[:, r % 2], prob[:, r % 2], ACT.Exp).then_inc(exped, 1)

                act.sem_inc(high, peeled // 2)

                def high_part(t, k):
                    if isinstance(t, int) or k % 2:
                        return
                    if k == 0:
                        at_least(act, raw_landed, 16 * 5)
                    cols = bass.ds(((t - k) // 4 - peeled // 4) * piece, piece)
                    nc.scalar.copy(cst[("wuh", "wdh")[k // 2]][:, cols], raw[:, k // 2, cols]).then_inc(high, 1)

                order = ((exponent, 4), (turned_copy, 1), (o_copy, 6), (probs_out, 4), (split, 1), (high_part, 0))
                pipeline(act, n_tiles, peeled, 4, in_order(order, n_tiles))

            @block.tensor
            def _(pe):
                def scores(t, r):
                    at_least(pe, split_out, t + 1)
                    at_least(pe, shifted, t)
                    for q in keys:
                        at_least(pe, q, t + 1)
                    for bank in range(2):
                        rows = slice(64 * bank, 64 * bank + 64)
                        nc.tensor.matmul(ps[:, 8 * bank:8 * bank + 8, :], cst["maskq"][rows, :], cst["maskk"][rows, :],
                                         start=True, stop=False)
                    for b in range(2):
                        for bank in range(2):
                            rows = slice(64 * bank, 64 * bank + 64)
                            ins = nc.tensor.matmul(ps[64 * b:64 * b + 64, 8 * bank:8 * bank + 8, :], qT[rows, r % 2, b],
                                                   kx[rows, r % 2, b], start=False, stop=True)
                    ins.then_inc(scored, 1)

                def turn_probs(t, r):
                    at_least(pe, exped, t + 1)
                    at_least(pe, p_out, t)
                    for j in range(8):
                        ins = nc.tensor.transpose(ppT[:, j, :], prob[:, r % 2, 2 * j:2 * j + 2].rearrange("p a k -> p (a k)"),
                                                  cst["ident"][:])
                    ins.then_inc(p_turned, 1)

                def turn_in(t, r):
                    at_least(pe, normed, t + 1)
                    at_least(pe, turned_out, t)
                    nc.tensor.transpose(pt_in[:, 0, :], xn[:, r % 2, :], cst["ident"][:]).then_inc(turned, 1)

                def turn_o(t, r):
                    at_least(pe, scaled, t + 1)
                    at_least(pe, added, t)
                    nc.tensor.transpose(pb[:, 0, :], o[:, r % 2].rearrange("p h d -> p (h d)"), cst["ident"][:]).then_inc(o_turned, 1)

                def project(t, r):
                    at_least(pe, turned_out, t + 1)
                    at_least(pe, loaded[r % 4], (t // 4) * 32 + 32 if isinstance(t, int) else (t - r % 4) * 8 + 32)
                    at_least(pe, split_out, t)
                    nc.tensor.matmul(pj[:, 0:2, :], cst["Wq"][:], xcT[:, r % 4], start=True, stop=True)
                    nc.tensor.matmul(pj[:, 2, :], xcT[:, r % 4, 1, :], cst["Wq"][:], start=True, stop=True).then_inc(projected, 1)

                def weigh(t, r):
                    at_least(pe, p_out, t + 1)
                    at_least(pe, scaled, t)
                    for j in range(8):
                        for b in range(2):
                            q = slice(64 * b, 64 * b + 64)
                            ins = nc.tensor.matmul(po[q, 2 * j:2 * j + 2, :], pT[:, r % 2, j, q], vx[:, r % 4, j, b], start=True, stop=True)
                    ins.then_inc(weighed, 1)

                def out_project(t, r):
                    at_least(pe, o_out, t + 1)
                    nc.tensor.matmul(pb[:, 1, :], oT[:, r % 2], cst["Wo"][:], start=True, stop=True).then_inc(wo_done, 1)

                order = ((scores, 3), (turn_in, 1), (weigh, 5), (turn_o, 6), (turn_probs, 4), (project, 1), (out_project, 6))
                pipeline(pe, n_tiles, peeled, 4, in_order(order, n_tiles))


class ChunkNorm:

    def __init__(self, nc, mem, sem):
        self.nc = nc
        sb = lambda name, shape: mem.enter_context(nc.sbuf_tensor(name, shape, F32))
        self.st = sb("r_st", [P, 4, 6])
        self.mv = sb("r_mv", [P, 4, 2])
        self.ve = sb("r_ve", [P, 4])
        self.rstd = sb("r_rstd", [P, 4])
        self.xc = sb("r_xc", [P, 4, D])
        self.xn = sb("r_xn", [P, 4, D])
        self.stats = sem("r_stats")
        self.rstd_done = sem("r_rstd")
        self.centred = sem("r_centred")
        self.normed = sem("r_normed")

    def take_stats(self, x_res, c):
        for j in range(4):
            ins = self.nc.vector.bn_stats(self.st[:, j, :], x_res[:, bass.ds(c * 4 + j, 1), :])
        ins.then_inc(self.stats, 1)

    def aggregate(self, dve, c, idle):
        wait_apart(dve, self.stats, 2 * c + 1, idle)
        for j in range(4):
            ins = self.nc.vector.bn_aggr(self.mv[:, j, :], self.st[:, j, :])
        ins.then_inc(self.stats, 1)

    def norm(self, pool, x_res, half, c, idle):
        ops = self.nc.gpsimd
        wait_apart(pool, self.stats, 2 * c + 2, idle)
        ops.tensor_scalar(self.ve[:], self.mv[:, :, 1], 1e-5, None, ALU.add).then_inc(self.rstd_done, 1)
        wait_apart(pool, self.rstd_done, 2 * c + 1, idle)
        ops.tensor_tensor(self.rstd[:], self.ve[:], half[:].to_broadcast([P, 4]), ALU.pow).then_inc(self.rstd_done, 1)
        ops.tensor_tensor(self.xc[:], x_res[:, bass.ds(c * 4, 4), :], self.mv[:, :, 0:1].to_broadcast([P, 4, D]),
                          ALU.subtract).then_inc(self.centred, 1)
        wait_apart(pool, self.rstd_done, 2 * c + 2, idle)
        wait_apart(pool, self.centred, c + 1, idle)
        ops.tensor_tensor(self.xn[:], self.xc[:], self.rstd[:].unsqueeze(2).to_broadcast([P, 4, D]), ALU.mult).then_inc(self.normed, 1)


def experts(nc, cst, dram, x_res, norms, y_mean, y_rstd, sem, chunks=TILES // 4):
    turns = chunks * PAIRS
    with ExitStack() as mem:
        def sb(name, shape, dt=F32):
            return mem.enter_context(nc.sbuf_tensor(name, shape, dt))

        def psum(name, shape, dt=F32):
            return mem.enter_context(nc.psum_tensor(name, shape, dt))

        sel = sb("e_sel", [P, (PAIRS - 1) * P], F16)
        xh = sb("e_xh", [P, 2, 512], F32R)
        xl = sb("e_xl", [P, 2, 512], F32R)
        s = sb("e_s", [P, 3, 512])
        m = sb("e_m", [P, 3, 512])
        mh = sb("e_mh", [P, 3, 512], F32R)
        ml = sb("e_ml", [P, 3, 512], F32R)
        yT = sb("e_yT", [P, 512])
        y_st = sb("e_y_st", [P, 4, 6])
        y_mv = sb("e_y_mv", [P, 4, 2])
        y_ve = sb("e_y_ve", [P, 4, 1])
        xs = sb("r_xs", [P, 4, P])
        aff = sb("r_aff", [P, 4, E])
        th = sb("r_th", [P, 4, E])
        biased = sb("r_biased", [P, 4, E])
        m8 = sb("r_m8", [P, 4, TOP])
        rep = sb("r_rep", [P, 4, E])
        chosen = sb("r_chosen", [P, 4, E])
        uv = sb("r_uv", [P, 2, 4, E])
        den = sb("r_den", [P, 4, E])
        gate = sb("r_gate", [P, 4, E])
        w_all = sb("r_w_all", [P, 4, E])
        w_top = sb("r_w_top", [P, 4, E])
        wsum = sb("r_wsum", [P, 4])
        wsum_e = sb("r_wsum_e", [P, 4])
        wrec = sb("r_wrec", [P, 4])
        cw = sb("r_cw", [P, 4, E])
        cwF = sb("r_cwF", [E, 4, P])
        cwT = sb("r_cwT", [P, 2, 512], F16)
        gt = sb("e_gt", [P, 2, 512])
        pu = [psum(f"e_pu{i}", [P, 512]) for i in range(3)]
        pg = [psum(f"e_pg{i}", [P, 512]) for i in range(2)]
        py = [psum(f"e_py{i}", [P, 512]) for i in range(2)]
        pt = psum("e_pt", [P, 4, P])
        pt_aff = pt[:, 0:2, :].rearrange("p a (b e) -> p (a b) e", e=E)
        scratch = nc.dram_tensor("gates_scratch", (2, E, 512), F32, kind="Internal").ap()

        landed = sem("e_landed")
        x_low = sem("e_x_low")
        up_done = sem("e_up")
        gate_done = sem("e_gate")
        silued = sem("e_silu")
        gated = sem("e_gated")
        m_high = sem("e_m_high")
        m_low = [sem(f"e_m_low_{e}") for e in ("dve", "pool")]
        down_done = sem("e_down")
        y_out = sem("e_y_out")
        y_turned = sem("e_y_turned")
        y_added = sem("e_y_added")
        y_stats = sem("e_y_stats")
        y_eps = sem("e_y_eps")
        y_rooted = sem("e_y_rooted")
        idle = {e: sem(f"e_idle_{e}") for e in ("dve", "act", "pool", "sp", "pe")}
        turned = sem("r_turned")
        turned_out = sem("r_turned_out")
        affine = sem("r_affine")
        aff_out = sem("r_aff_out")
        biased_done = sem("r_biased_done")
        top = sem("r_top")
        marked = sem("r_marked")
        compared = sem("r_compared")
        powers = sem("r_powers")
        summed = sem("r_summed")
        inverted = sem("r_inverted")
        weighed = sem("r_weighed")
        added_up = sem("r_added_up")
        normaliser = sem("r_normaliser")
        gates = sem("r_gates")
        g_turned = sem("r_g_turned")
        g_out = sem("r_g_out")
        g_low = sem("r_g_low")
        stored = sem("e_stored")
        spread = [sem(f"e_spread{k}") for k in range(2)]

        by_dma = tuple(range(3, 30, 2))
        by_pe = tuple(p for p in range(PAIRS - 1) if p not in by_dma)

        low_by_pool = (0, 7, 9, 19, 21, 30)
        low_by_dve = tuple(p for p in range(PAIRS) if p not in low_by_pool)

        def await_low(eng, pair, c):
            for q, pairs in zip(m_low, (low_by_dve, low_by_pool)):
                if pair in pairs:
                    at_least(eng, q, c * len(pairs) + pairs.index(pair) + 1)

        def drive(eng, step):
            unroll = 2 * PAIRS
            for n in range(unroll):
                step(n, n, lambda lag, n=n: (n - lag) // PAIRS)
            with eng.Fori(1, turns // unroll) as g:
                for r in range(unroll):
                    step(g * unroll + r, r, lambda lag, g=g, r=r: g * 2 + (r - lag) // PAIRS)
            for n in range(turns, turns + 9):
                step(n, n % unroll, lambda lag, n=n: (n - lag) // PAIRS)

        def ends(eng, ops, name, c):
            wait_apart(eng, aff_out, c + 1, idle[name])
            ops.tensor_tensor(biased[:], aff[:], cst["eb"][:].unsqueeze(1).to_broadcast([P, 4, E]), ALU.add).then_inc(biased_done, 1)
            ops.tensor_scalar(uv[:, 0], th[:], 1.0, None, ALU.add)
            ops.tensor_scalar(uv[:, 1], th[:], -1.0, 1.0, ALU.mult, ALU.add).then_inc(powers, 1)

        def fourth_powers(eng, ops, name, c):
            for k in range(2):
                wait_apart(eng, powers, 3 * c + 1 + k, idle[name])
                ops.tensor_tensor(uv[:], uv[:], uv[:], ALU.mult).then_inc(powers, 1)

        def denominator(eng, ops, name, c):
            wait_apart(eng, powers, 3 * c + 3, idle[name])
            ops.tensor_tensor(den[:], uv[:, 0], uv[:, 1], ALU.add).then_inc(summed, 1)

        def weights(eng, ops, name, c):
            wait_apart(eng, inverted, c + 1, idle[name])
            ops.tensor_tensor(w_all[:], uv[:, 0], gate[:], ALU.mult).then_inc(weighed, 1)
            wait_apart(eng, compared, c + 1, idle[name])
            wait_apart(eng, weighed, 2 * c + 1, idle[name])
            ops.tensor_tensor(w_top[:], w_all[:], chosen[:], ALU.mult).then_inc(weighed, 1)

        def gates_of(eng, ops, name, c):
            wait_apart(eng, normaliser, c + 1, idle[name])
            ops.tensor_tensor(cw[:], w_top[:], wrec[:].unsqueeze(2).to_broadcast([P, 4, E]), ALU.mult).then_inc(gates, 1)

        with nc.Block() as block:
            @block.gpsimd
            def _(pool):
                def after(semaphore, value):
                    wait_apart(pool, semaphore, value, idle["pool"])

                def y_root(c, b):
                    if isinstance(c, int) and c < 2:
                        return
                    after(y_stats, 2 * c - 2)
                    nc.gpsimd.tensor_scalar(y_ve[:], y_mv[:, :, 1:2], 1e-5, None, ALU.add).then_inc(y_eps, 1)
                    nc.gpsimd.tensor_tensor(y_mean[:, bass.ds((c - 2) * 4, 4)], y_mv[:, :, 0], cst["ones"][:, 0:4],
                                            ALU.mult).then_inc(y_rooted, 1)
                    after(y_eps, c - 1)
                    nc.gpsimd.tensor_tensor(y_rstd[:, bass.ds((c - 2) * 4, 4)], y_ve[:, :, 0], cst["mhalf"][:].to_broadcast([P, 4]),
                                            ALU.pow).then_inc(y_rooted, 1)

                def norm(c, b):
                    norms.norm(pool, x_res, cst["mhalf"], c, idle["pool"])

                def low_part(c, b):
                    after(turned_out, c + 1)
                    nc.gpsimd.tensor_tensor(xl[:, b, :], xs[:].rearrange("p j t -> p (j t)"), xh[:, b, :].bitcast(F32),
                                            ALU.subtract).then_inc(x_low, 1)

                def mine(gate_step):
                    return lambda c, b: gate_step(pool, nc.gpsimd, "pool", c)

                route = {2: norm, 11: y_root, 12: low_part, 13: mine(ends), 14: mine(fourth_powers), 17: mine(denominator),
                         24: mine(weights), 28: mine(gates_of)}

                def step(n, r, chunk):
                    if isinstance(n, int) and n == 0:
                        low_part(0, 0)
                    if live(n, 1, turns) and (r - 1) % PAIRS in low_by_pool:
                        after(m_high, n)
                        after(down_done, n - 3)
                        nc.gpsimd.tensor_tensor(ml[:, (r - 1) % 3, :], m[:, (r - 1) % 3, :], mh[:, (r - 1) % 3, :].bitcast(F32),
                                                ALU.subtract).then_inc(m_low[1], 1)
                    if live(n, 0, turns) and r % PAIRS in route:
                        route[r % PAIRS](chunk(0) + 1, (r // PAIRS + 1) % 2)
                drive(pool, step)
                y_root(chunks + 1, 0)

            @block.sync
            def _(sp):
                sp.dma_start(sel[:], dram["sel"]).then_inc(landed, 16)

                def store(c, b):
                    wait_apart(sp, gated, (c - 1) * PAIRS, idle["sp"])
                    wait_apart(sp, g_out, c + 1, idle["sp"])
                    sp.dma_start(scratch[b], cwF[:].rearrange("e j t -> e (j t)")).then_inc(stored, 16)

                def step(n, r, chunk):
                    if isinstance(n, int) and n == 0:
                        store(0, 0)
                    if live(n, 0, turns) and r % PAIRS in by_dma:
                        pair = r % PAIRS
                        i = by_dma.index(pair)
                        if i == 0:
                            wait_apart(sp, stored, 16 * (chunk(0) + 1), idle["sp"])
                        before = by_dma[i - 2] - (PAIRS if i < 2 else 0)
                        wait_apart(sp, gated, n - (pair - before) + 1, idle["sp"])
                        for e in range(2):
                            sp.dma_start(gt[64 * e:64 * e + 64, i % 2, :],
                                         scratch[(r // PAIRS) % 2, 2 * pair + e].unsqueeze(0).to_broadcast([FH, 512])).then_inc(spread[i % 2], 16)
                    if live(n, 0, turns) and r % PAIRS == PAIRS - 2:
                        store(chunk(0) + 1, (r // PAIRS + 1) % 2)
                drive(sp, step)
                sp.wait_ge(stored, 16 * (chunks + 1))

            @block.vector
            def _(dve):
                def stats_of(c, b):
                    norms.take_stats(x_res, c)

                def aggregate(c, b):
                    norms.aggregate(dve, c, idle["dve"])

                def y_stats_of(c, b):
                    if isinstance(c, int) and c < 2:
                        return
                    wait_apart(dve, y_added, c - 1, idle["dve"])
                    wait_apart(dve, y_rooted, 2 * (c - 2), idle["dve"])
                    for j in range(4):
                        ins = nc.vector.bn_stats(y_st[:, j, :], x_res[:, bass.ds((c - 2) * 4 + j, 1), :])
                    ins.then_inc(y_stats, 1)

                def y_aggregate(c, b):
                    if isinstance(c, int) and c < 2:
                        return
                    wait_apart(dve, y_stats, 2 * c - 3, idle["dve"])
                    for j in range(4):
                        ins = nc.vector.bn_aggr(y_mv[:, j, :], y_st[:, j, :])
                    ins.then_inc(y_stats, 1)

                def top_of(c, b):
                    wait_apart(dve, biased_done, c + 1, idle["dve"])
                    for j in range(4):
                        ins = nc.vector.max(out=m8[:, j, :], in_=biased[:, j, :])
                    ins.then_inc(top, 1)

                def mark(tiles):
                    def do(c, b):
                        wait_apart(dve, top, c + 1, idle["dve"])
                        for j in tiles:
                            ins = nc.vector.match_replace(out=rep[:, j, :], in_to_replace=m8[:, j, :], in_values=biased[:, j, :],
                                                          imm_value=-SENTINEL)
                        if tiles[-1] == 3:
                            ins.then_inc(marked, 1)
                    return do

                def compare(c, b):
                    at_least(dve, marked, c + 1)
                    nc.vector.tensor_tensor(chosen[:], rep[:], biased[:], ALU.not_equal).then_inc(compared, 1)

                def invert(tile):
                    def do(c, b):
                        wait_apart(dve, summed, c + 1, idle["dve"])
                        ins = nc.vector.reciprocal(gate[:, tile, :], den[:, tile, :])
                        if tile == 3:
                            ins.then_inc(inverted, 1)
                    return do

                def add_up(c, b):
                    wait_apart(dve, weighed, 2 * c + 2, idle["dve"])
                    nc.vector.tensor_reduce(wsum[:], w_top[:], AX.X, ALU.add).then_inc(added_up, 1)

                def add_eps(c, b):
                    wait_apart(dve, added_up, 2 * c + 1, idle["dve"])
                    nc.vector.tensor_scalar(wsum_e[:], wsum[:], 1e-8, None, ALU.add).then_inc(added_up, 1)

                def normalise(c, b):
                    wait_apart(dve, added_up, 2 * c + 2, idle["dve"])
                    nc.vector.reciprocal(wrec[:], wsum_e[:]).then_inc(normaliser, 1)

                def gates_low(c, b):
                    at_least(dve, g_out, c + 1)
                    nc.vector.tensor_tensor(cwT[E:P, b, :], cwF[:].rearrange("e j t -> e (j t)"), cwT[0:E, b, :], ALU.subtract).then_inc(g_low, 1)

                route = {1: stats_of, 2: aggregate, 9: y_stats_of, 10: y_aggregate, 15: top_of, 17: mark((0, 1)),
                         18: mark((2, 3)), 19: compare, 20: invert(0), 21: invert(1), 22: invert(2), 23: invert(3), 25: add_up,
                         26: add_eps, 27: normalise, 31: gates_low}

                def step(n, r, chunk):
                    if isinstance(n, int) and n == 0:
                        for turn in sorted(route):
                            if turn > 2:
                                route[turn](0, 0)
                            for gate_step, behind in ((ends, 10), (fourth_powers, 15), (denominator, 15), (weights, 23), (gates_of, 27)):
                                if turn == behind:
                                    gate_step(dve, nc.vector, "dve", 0)
                    if live(n, 0, turns):
                        pair = r % PAIRS
                        at_least(dve, silued, n + 1)
                        if live(n, 3, turns + 3):
                            await_low(dve, (r - 3) % PAIRS, chunk(3))
                        if pair in by_pe:
                            i = by_pe.index(pair)
                            at_least(dve, gate_done, chunk(0) * len(by_pe) + i + 1)
                            ins = nc.vector.tensor_tensor(m[:, r % 3, :], s[:, r % 3, :], pg[i % 2][:], ALU.mult)
                        elif pair in by_dma:
                            i = by_dma.index(pair)
                            at_least(dve, spread[i % 2], chunk(0) * (16 * len(by_dma)) + 32 * (i // 2 + 1))
                            ins = nc.vector.tensor_tensor(m[:, r % 3, :], s[:, r % 3, :], gt[:, i % 2, :], ALU.mult)
                        else:
                            ins = nc.vector.tensor_scalar(m[:, r % 3, :], s[:, r % 3, :], 1.0, None, ALU.mult)
                        ins.then_inc(gated, 1)
                    if live(n, 1, turns) and (r - 1) % PAIRS in low_by_dve:
                        at_least(dve, m_high, n)
                        at_least(dve, down_done, n - 3)
                        nc.vector.tensor_tensor(ml[:, (r - 1) % 3, :], m[:, (r - 1) % 3, :], mh[:, (r - 1) % 3, :].bitcast(F32),
                                                ALU.subtract).then_inc(m_low[0], 1)
                    if live(n, 0, turns) and r % PAIRS in route:
                        route[r % PAIRS](chunk(0) + 1, (r // PAIRS + 1) % 2)
                    if live(n, 8, turns) and (r - 8) % PAIRS == PAIRS - 1:
                        c = chunk(8)
                        at_least(dve, y_turned, c + 1)
                        nc.vector.tensor_tensor(x_res[:, bass.ds(c * 4, 4), :], x_res[:, bass.ds(c * 4, 4), :], pt[:],
                                                ALU.add).then_inc(y_added, 1)
                drive(dve, step)
                y_stats_of(chunks + 1, 0)
                y_aggregate(chunks + 1, 0)

            @block.scalar
            def _(act):
                def turned_copy(c, b):
                    at_least(act, turned, c + 1)
                    nc.scalar.copy(xs[:], pt[:])

                def high_part(c, b):
                    at_least(act, up_done, (c - 1) * PAIRS)
                    nc.scalar.copy(xh[:, b, :], pt[:].rearrange("p j t -> p (j t)")).then_inc(turned_out, 1)

                def affinities(c, b):
                    at_least(act, affine, c + 1)
                    nc.scalar.copy(aff[:], pt_aff)
                    nc.scalar.activation(th[:], pt_aff, ACT.Tanh, scale=0.125).then_inc(aff_out, 1)

                def gates_copy(c, b):
                    at_least(act, g_turned, c + 1)
                    at_least(act, stored, 16 * c)
                    nc.scalar.copy(cwF[:], pt[0:E])
                    nc.scalar.copy(cwT[0:E, b, :], pt[0:E].rearrange("e j t -> e (j t)")).then_inc(g_out, 1)

                route = {10: turned_copy, 11: high_part, 13: affinities, 29: gates_copy}

                def step(n, r, chunk):
                    if isinstance(n, int) and n == 0:
                        for route_step in route.values():
                            route_step(0, 0)
                    if live(n, 0, turns):
                        at_least(act, up_done, n + 1)
                        at_least(act, gated, n - 2)
                        nc.scalar.activation(s[:, r % 3, :], pu[r % 3][:], ACT.Silu).then_inc(silued, 1)
                    if live(n, 1, turns):
                        at_least(act, gated, n)
                        at_least(act, down_done, n - 3)
                        nc.scalar.copy(mh[:, (r - 1) % 3, :], m[:, (r - 1) % 3, :]).then_inc(m_high, 1)
                    if live(n, 0, turns) and r % PAIRS in route:
                        route[r % PAIRS](chunk(0) + 1, (r // PAIRS + 1) % 2)
                    if live(n, 4, turns) and (r - 4) % PAIRS == PAIRS - 1:
                        c = chunk(4)
                        at_least(act, down_done, (c + 1) * PAIRS)
                        at_least(act, y_turned, c)
                        nc.scalar.copy(yT[:], py[((r - 4) // PAIRS) % 2][:]).then_inc(y_out, 1)
                drive(act, step)

            @block.tensor
            def _(pe):
                def turn_in(c, b):
                    at_least(pe, norms.normed, c + 1)
                    at_least(pe, y_added, c - 1)
                    for j in range(4):
                        ins = nc.tensor.transpose(pt[:, j, :], norms.xn[:, j, :], cst["ident"][:])
                    ins.then_inc(turned, 1)

                def affinities(c, b):
                    at_least(pe, turned_out, c + 1)
                    for j in range(4):
                        ins = nc.tensor.matmul(pt_aff[:, j, :], xs[:, j, :], cst["centT"][:], start=True, stop=True)
                    ins.then_inc(affine, 1)

                def turn_gates(c, b):
                    wait_apart(pe, gates, c + 1, idle["pe"])
                    wait_apart(pe, aff_out, c + 1, idle["pe"])
                    for j in range(4):
                        ins = nc.tensor.transpose(pt[0:E, j, :], cw[:, j, :], cst["ident"][:])
                    ins.then_inc(g_turned, 1)

                route = {9: turn_in, 12: affinities, 29: turn_gates}

                def step(n, r, chunk):
                    if isinstance(n, int) and n == 0:
                        turn_in(0, 0)
                        affinities(0, 0)
                    pair = r % PAIRS
                    w = slice(pair * P, pair * P + P)
                    if live(n, 0, turns):
                        b = (r // PAIRS) % 2
                        at_least(pe, x_low, chunk(0) + 1)
                        at_least(pe, silued, n - 2)
                        nc.tensor.matmul(pu[r % 3][:], cst["wuh"][:, w], xh[:, b, :], start=True, stop=False)
                        nc.tensor.matmul(pu[r % 3][:], cst["wul"][:, w], xh[:, b, :], start=False, stop=False)
                        nc.tensor.matmul(pu[r % 3][:], cst["wuh"][:, w], xl[:, b, :], start=False, stop=True).then_inc(up_done, 1)
                        if isinstance(n, int) and n == 0:
                            turn_gates(0, 0)
                            pe.wait_ge(landed, 16)
                        if pair in by_pe:
                            at_least(pe, gated, n - 1)
                            at_least(pe, g_low, chunk(0) + 1)
                            nc.tensor.matmul(pg[by_pe.index(pair) % 2][:], sel[:, w], cwT[:, b, :],
                                             start=True, stop=True).then_inc(gate_done, 1)
                    if live(n, 3, turns):
                        pd = (r - 3) % PAIRS
                        w = slice(pd * P, pd * P + P)
                        k = (r - 3) % 3
                        out = py[((r - 3) // PAIRS) % 2][:]
                        await_low(pe, pd, chunk(3))
                        if pd == 0:
                            at_least(pe, y_out, chunk(3) - 1)
                        nc.tensor.matmul(out, cst["wdh"][:, w], mh[:, k, :], start=(pd == 0), stop=False)
                        nc.tensor.matmul(out, cst["wdl"][:, w], mh[:, k, :], start=False, stop=False)
                        nc.tensor.matmul(out, cst["wdh"][:, w], ml[:, k, :], start=False, stop=(pd == PAIRS - 1)).then_inc(down_done, 1)
                    if live(n, 6, turns) and (r - 6) % PAIRS == PAIRS - 1:
                        c = chunk(6)
                        at_least(pe, y_out, c + 1)
                        at_least(pe, g_out, c + 2)
                        for j in range(4):
                            ins = nc.tensor.transpose(pt[:, j, :], yT[:, j * P:(j + 1) * P], cst["ident"][:])
                        ins.then_inc(y_turned, 1)
                    if live(n, 0, turns) and r % PAIRS in route:
                        route[r % PAIRS](chunk(0) + 1, (r // PAIRS + 1) % 2)
                drive(pe, step)


def dft_tables():
    f = np.concatenate([np.arange(S // 2 + 1), np.arange(1, S // 2)])
    second = np.arange(S) > S // 2
    angle = 2 * np.pi * np.outer(f, np.arange(S)) / S
    cos, sin = np.cos(angle), np.sin(angle)
    weight = np.where((f == 0) | (f == S // 2), 1.0, 2.0)[:, None] / S
    sign = np.where(second, -1.0, 1.0)[:, None]
    both = lambda m: np.kron(np.eye(2), m)
    return {
        "dft": np.concatenate([both(np.where(second[:, None], -sin, cos).T), both(np.where(second[:, None], cos, -sin).T)], 1),
        "idft_corr": np.concatenate([both(weight * cos), both(weight * sign * sin)], 1) / HD,
        "idft_conv": np.concatenate([both(weight * sign * cos), both(-weight * sin)], 1),
    }


def spectrum(nc, cst, ctx, x_res, y_mean, y_rstd, vf, sums, sem, n_tiles=TILES):
    with ExitStack() as mem:
        def sb(name, shape, dt=F32):
            return mem.enter_context(nc.sbuf_tensor(name, shape, dt))

        def psum(name, shape, dt=F32):
            return mem.enter_context(nc.psum_tensor(name, shape, dt))

        cin = sb("c_cin", [P, 4, D])
        xn = sb("c_xn", [P, 2, D])
        xf = sb("c_xf", [P, 2, 3, P])
        qf = sb("c_qf", [P, 2, 3, D])
        pp = sb("c_pp", [P, 2, 2, D])
        pf = [psum(f"c_pf{i}", [P, 4, P]) for i in range(2)]
        pq = [psum(f"c_pq{i}", [P, 4, P]) for i in range(2)]

        loaded = [sem(f"c_loaded{r}") for r in range(4)]
        normed = sem("c_normed")
        transformed = sem("c_transformed")
        f_out = sem("c_f_out")
        projected = sem("c_projected")
        q_out = sem("c_q_out")
        products = sem("c_products")
        summed = sem("c_summed")
        idle = {e: sem(f"c_idle_{e}") for e in ("dve", "sp", "pool")}

        with nc.Block() as block:
            @block.sync
            def _(sp):
                def load(t, k):
                    wait_apart(sp, transformed, t - 3, idle["sp"])
                    sp.dma_start(cin[:, k:k + 1, :], ctx[bass.ds(t, 1)].rearrange("a p d -> p a d")).then_inc(loaded[k], 16)
                pipeline(sp, n_tiles, 8, 4, in_order(((load, 0),), n_tiles))

            @block.vector
            def _(dve):
                def norm(t, k):
                    at_least(dve, transformed, t - 1)
                    nc.vector.tensor_scalar(xn[:, k % 2, :], x_res[:, bass.ds(t, 1), :], y_mean[:, bass.ds(t, 1)],
                                            y_rstd[:, bass.ds(t, 1)], ALU.subtract, ALU.mult).then_inc(normed, 1)

                def bias(t, k):
                    at_least(dve, projected, t + 1)
                    at_least(dve, products, t - 1)
                    nc.vector.tensor_tensor(qf[:, k % 2], pq[k % 2][:, 0:3, :], cst["fbias"][:, 0:3, :], ALU.add)
                    nc.vector.tensor_tensor(vf[:, bass.ds(t, 1), :], pq[k % 2][:, 3:4, :], cst["fbias"][:, 3:4, :],
                                            ALU.add).then_inc(q_out, 1)

                def head_sum(t, k):
                    wait_apart(dve, products, t + 1, idle["dve"])
                    nc.vector.tensor_reduce(sums[:, :, bass.ds(t, 1), :].rearrange("p j a h -> p j (a h)"),
                                            pp[:, k % 2].rearrange("p j (h d) -> p j h d", d=HD), AX.X, ALU.add).then_inc(summed, 1)

                order = ((norm, 1), (head_sum, 6), (bias, 4))
                pipeline(dve, n_tiles, 12, 4, in_order(order, n_tiles))

            @block.gpsimd
            def _(pool):
                def multiply(t, k):
                    at_least(pool, q_out, t + 1)
                    at_least(pool, summed, t - 1)
                    nc.gpsimd.tensor_tensor(pp[:, k % 2], qf[:, k % 2, 0, :].unsqueeze(1).to_broadcast([P, 2, D]), qf[:, k % 2, 1:3, :],
                                            ALU.mult).then_inc(products, 1)

                def residual_bias(t, k):
                    wait_apart(pool, normed, t + 1, idle["pool"])
                    nc.gpsimd.tensor_tensor(x_res[:, bass.ds(t, 1), :], x_res[:, bass.ds(t, 1), :], cst["bo1"][:].unsqueeze(1), ALU.add)

                pipeline(pool, n_tiles, 12, 4, in_order(((multiply, 4), (residual_bias, 3)), n_tiles))

            @block.scalar
            def _(act):
                def spectra_out(t, k):
                    at_least(act, transformed, t + 1)
                    at_least(act, projected, t - 1)
                    nc.scalar.copy(xf[:, k % 2], pf[k % 2][:, 0:3, :]).then_inc(f_out, 1)

                pipeline(act, n_tiles, 12, 4, in_order(((spectra_out, 2),), n_tiles))

            @block.tensor
            def _(pe):
                def transform(t, k):
                    at_least(pe, normed, t + 1)
                    at_least(pe, loaded[k], (t // 4) * 16 + 16 if isinstance(t, int) else (t - k) * 4 + 16)
                    at_least(pe, f_out, t - 1)
                    nc.tensor.matmul(pf[k % 2][:, 0, :], xn[:, k % 2, :], cst["dft"][:, 0:P], start=True, stop=True)
                    nc.tensor.matmul(pf[k % 2][:, 1:3, :], cin[:, k, :], cst["dft"][:], start=True, stop=True).then_inc(transformed, 1)

                def project(t, k):
                    at_least(pe, f_out, t + 1)
                    at_least(pe, q_out, t - 1)
                    for j, (src, w) in enumerate(((0, 0), (1, 1), (2, 1), (1, 2))):
                        ins = nc.tensor.matmul(pq[k % 2][:, j, :], xf[:, k % 2, src, :], cst["w1T"][:, w, :], start=True, stop=True)
                    ins.then_inc(projected, 1)

                pipeline(pe, n_tiles, 12, 4, in_order(((project, 4), (transform, 2)), n_tiles))


def delays(nc, cst, sums, cf, sem):
    PARTS = 2
    G = TILES // 8 // PARTS
    with ExitStack() as mem:
        def sb(name, shape, dt=F32):
            return mem.enter_context(nc.sbuf_tensor(name, shape, dt))

        ext = sb("d_ext", [P, PARTS, 2 * G, S + TOP - DELAYS])
        rep = sb("d_rep", [P, PARTS, 2 * G, S + TOP - DELAYS])
        m8 = sb("d_m8", [P, PARTS, 2 * G, TOP])
        e = sb("d_e", [P, PARTS, 2 * G, S])
        w = sb("d_w", [P, PARTS, 2 * G, S])
        wsum = sb("d_wsum", [P, PARTS, 2 * G])
        cT = sb("d_cT", [P, PARTS, G, P])
        pc = [mem.enter_context(nc.psum_tensor(f"d_pc{i}", [P, G, P], F32)) for i in range(PARTS)]
        pw = [mem.enter_context(nc.psum_tensor(f"d_pw{i}", [P, G, P], F32)) for i in range(PARTS)]
        pab = [mem.enter_context(nc.psum_tensor(f"d_pab{i}", [P, 2, G, P], F32)) for i in range(PARTS)]
        inverted = sem("d_inverted")
        preset = sem("d_preset")
        copied = sem("d_copied")
        top = sem("d_top")
        shifted = sem("d_shifted")
        marked = sem("d_marked")
        chosen = sem("d_chosen")
        exped = sem("d_exped")
        kept = sem("d_kept")
        summed = sem("d_summed")
        inverse = sem("d_inverse")
        weights = sem("d_weights")
        w_turned = sem("d_w_turned")
        w_out = sem("d_w_out")
        transformed = sem("d_transformed")

        with nc.Block() as block:
            @block.tensor
            def _(pe):
                for i in range(PARTS):
                    for g in range(G):
                        for j in range(2):
                            tiles = slice(8 * (i * G + g), 8 * (i * G + g) + 8)
                            ins = nc.tensor.matmul(pc[i][:, g, :], sums[:, j, tiles, :].rearrange("p t h -> p (t h)"),
                                                   cst["idft_corr"][:, j * P:j * P + P], start=(j == 0), stop=(j == 1))
                    ins.then_inc(inverted, 1)
                for i in range(PARTS):
                    pe.wait_ge(weights, i + 1)
                    for g in range(G):
                        ins = nc.tensor.transpose(pw[i][:, g, :], w[:, i, 2 * g:2 * g + 2, :].rearrange("p b d -> p (b d)"), cst["ident"][:])
                    ins.then_inc(w_turned, 1)
                    pe.wait_ge(w_out, i + 1)
                    for k in range(2):
                        ins = nc.tensor.matmul(pab[i][:, k], cst["dft"][:, k * P:k * P + P], cT[:, i], start=True, stop=True)
                    ins.then_inc(transformed, 1)

            @block.vector
            def _(dve):
                nc.vector.memset(ext[:, :, :, S:], SENTINEL).then_inc(preset, 1)
                dve.wait_ge(preset, 1)

                def copy(i):
                    dve.wait_ge(inverted, i + 1)
                    nc.vector.tensor_copy(ext[:, i, :, 0:S], pc[i][:].rearrange("p g (b d) -> p (g b) d", b=2)).then_inc(copied, 1)

                def top_of(i):
                    dve.wait_ge(copied, i + 1)
                    for g in range(2 * G):
                        ins = nc.vector.max(out=m8[:, i, g, :], in_=ext[:, i, g, :])
                    ins.then_inc(top, 1)

                def shift(i):
                    dve.wait_ge(top, i + 1)
                    nc.vector.tensor_tensor(e[:, i], ext[:, i, :, 0:S],
                                            m8[:, i, :, TOP - DELAYS:TOP - DELAYS + 1].to_broadcast([P, 2 * G, S]),
                                            ALU.subtract).then_inc(shifted, 1)

                def mark(i):
                    for g in range(2 * G):
                        ins = nc.vector.match_replace(out=rep[:, i, g, :], in_to_replace=m8[:, i, g, :], in_values=ext[:, i, g, :],
                                                      imm_value=-SENTINEL)
                    ins.then_inc(marked, 1)

                def choose(i):
                    dve.wait_ge(marked, i + 1)
                    nc.vector.tensor_tensor(w[:, i], rep[:, i, :, 0:S], ext[:, i, :, 0:S], ALU.not_equal).then_inc(chosen, 1)

                def keep(i):
                    dve.wait_ge(chosen, i + 1)
                    dve.wait_ge(exped, i + 1)
                    nc.vector.tensor_tensor(w[:, i], w[:, i], e[:, i], ALU.mult).then_inc(kept, 1)

                def add_up(i):
                    dve.wait_ge(kept, i + 1)
                    nc.vector.tensor_reduce(wsum[:, i, :], w[:, i], AX.X, ALU.add).then_inc(summed, 1)

                def invert(i):
                    dve.wait_ge(summed, i + 1)
                    nc.vector.reciprocal(wsum[:, i, :], wsum[:, i, :]).then_inc(inverse, 1)

                def scale(i):
                    dve.wait_ge(inverse, i + 1)
                    nc.vector.tensor_tensor(w[:, i], w[:, i], wsum[:, i, :].unsqueeze(2).to_broadcast([P, 2 * G, S]),
                                            ALU.mult).then_inc(weights, 1)

                for i, steps in ((0, (copy, top_of, shift, mark)), (1, (copy, top_of, shift))):
                    for step in steps:
                        step(i)
                choose(0)
                mark(1)
                keep(0)
                choose(1)
                add_up(0)
                keep(1)
                invert(0)
                add_up(1)
                scale(0)
                invert(1)
                scale(1)

            @block.scalar
            def _(act):
                for i in range(PARTS):
                    act.wait_ge(shifted, i + 1)
                    nc.scalar.activation(e[:, i], e[:, i], ACT.Exp).then_inc(exped, 1)
                for i in range(PARTS):
                    act.wait_ge(w_turned, i + 1)
                    nc.scalar.copy(cT[:, i], pw[i][:]).then_inc(w_out, 1)
                    act.wait_ge(transformed, i + 1)
                    for k in range(2):
                        nc.scalar.copy(cf[:, k, 8 * i * G:8 * (i + 1) * G, :].rearrange("p t h -> p (t h)"),
                                       pab[i][:, k].rearrange("p g c -> p (g c)"))


def mix(nc, cst, x_res, vf, cf, xnT, amax, sem):
    W = 2
    groups = TILES // W
    with ExitStack() as mem:
        def sb(name, shape, dt=F32):
            return mem.enter_context(nc.sbuf_tensor(name, shape, dt))

        rr = sb("m_rr", [P, 2, 2, W, D])
        oT = sb("m_oT", [P, 2, W, P])
        st = sb("m_st", [P, 2, W, 6])
        mv = sb("m_mv", [P, 2, W, 2])
        ve = sb("m_ve", [P, 2, W])
        rstd = sb("m_rstd", [P, 2, W])
        xn = sb("m_xn", [P, 2, W, D])
        po = [mem.enter_context(nc.psum_tensor(f"m_po{i}", [P, 4, P], F32)) for i in range(2)]
        py = [mem.enter_context(nc.psum_tensor(f"m_py{i}", [P, 4, P], F32)) for i in range(2)]
        pt = [mem.enter_context(nc.psum_tensor(f"m_pt{i}", [P, 4, P], F32)) for i in range(2)]
        products = [sem(f"m_products{j}") for j in range(2)]
        inverted = sem("m_inverted")
        o_out = sem("m_o_out")
        projected = sem("m_projected")
        added = sem("m_added")
        stats = sem("m_stats")
        rstd_done = sem("m_rstd")
        normed = sem("m_normed")
        turned = sem("m_turned")
        t_out = sem("m_t_out")
        idle = {e: sem(f"m_idle_{e}") for e in ("dve", "act", "pool")}

        with nc.Block() as block:
            def product(eng, g, k, j):
                return eng.tensor_tensor(
                    rr[:, k % 2, j].rearrange("p t (h d) -> p (t h) d", d=HD),
                    vf[:, bass.ds(g * W, W), :].rearrange("p t (h d) -> p (t h) d", d=HD),
                    cf[:, j, bass.ds(g * W, W), :].rearrange("p t h -> p (t h)").unsqueeze(2).to_broadcast([P, W * H, HD]), ALU.mult)

            @block.gpsimd
            def _(pool):
                def multiply(g, k):
                    wait_apart(pool, inverted, g - 1, idle["pool"])
                    product(nc.gpsimd, g, k, 0).then_inc(products[0], 1)

                def inverse_root(g, k):
                    wait_apart(pool, stats, 2 * g + 2, idle["pool"])
                    wait_apart(pool, normed, g - 1, idle["pool"])
                    nc.gpsimd.tensor_scalar(ve[:, k % 2, :], mv[:, k % 2, :, 1], 1e-3, None, ALU.add).then_inc(rstd_done, 1)
                    at_least(pool, rstd_done, 2 * g + 1)
                    nc.gpsimd.tensor_tensor(rstd[:, k % 2, :], ve[:, k % 2, :], cst["mhalf"][:].to_broadcast([P, W]),
                                            ALU.pow).then_inc(rstd_done, 1)

                pipeline(pool, groups, 10, 2, in_order(((multiply, 0), (inverse_root, 4)), groups))

            @block.vector
            def _(dve):
                def multiply(g, k):
                    at_least(dve, inverted, g - 1)
                    product(nc.vector, g, k, 1).then_inc(products[1], 1)

                def stats_of(g, k):
                    wait_apart(dve, added, g + 1, idle["dve"])
                    wait_apart(dve, rstd_done, 2 * (g - 1), idle["dve"])
                    for j in range(W):
                        ins = nc.vector.bn_stats(st[:, k % 2, j, :], x_res[:, bass.ds(g * W + j, 1), :])
                    ins.then_inc(stats, 1)

                def aggregate(g, k):
                    wait_apart(dve, stats, 2 * g + 1, idle["dve"])
                    for j in range(W):
                        ins = nc.vector.bn_aggr(mv[:, k % 2, j, :], st[:, k % 2, j, :])
                    ins.then_inc(stats, 1)

                def norm(g, k):
                    at_least(dve, rstd_done, 2 * g + 2)
                    at_least(dve, turned, g - 1)
                    for j in range(W):
                        ins = nc.vector.tensor_scalar(xn[:, k % 2, j, :], x_res[:, bass.ds(g * W + j, 1), :], mv[:, k % 2, j, 0:1],
                                                      rstd[:, k % 2, j:j + 1], ALU.subtract, ALU.mult)
                    ins.then_inc(normed, 1)

                def largest(g, k):
                    wait_apart(dve, t_out, g + 1, idle["dve"])
                    nc.vector.tensor_reduce(amax[:, bass.ds(g, 1)], xnT[:, bass.ds(g * W * P, W * P)], AX.X, ALU.max,
                                            apply_absolute_value=True)

                order = ((multiply, 0), (stats_of, 4), (norm, 5), (aggregate, 4), (largest, 7))
                pipeline(dve, groups, 10, 2, in_order(order, groups))

            @block.scalar
            def _(act):
                def o_copy(g, k):
                    at_least(act, inverted, g + 1)
                    at_least(act, projected, g - 1)
                    nc.scalar.copy(oT[:, k % 2], po[k % 2][:, 0:W, :]).then_inc(o_out, 1)

                def affine(g, k):
                    wait_apart(act, turned, g + 1, idle["act"])
                    nc.scalar.activation(xnT[:, bass.ds(g * W * P, W * P)], pt[k % 2][:, 0:W, :], ACT.Identity,
                                         bias=cst["ln_beta"][:], scale=cst["ln_gamma"][:]).then_inc(t_out, 1)

                def sum_out(g, k):
                    wait_apart(act, projected, g + 1, idle["act"])
                    nc.scalar.copy(x_res[:, bass.ds(g * W, W), :], py[k % 2][:, 0:W, :]).then_inc(added, 1)

                pipeline(act, groups, 10, 2, in_order(((sum_out, 3), (o_copy, 1), (affine, 6)), groups))

            @block.tensor
            def _(pe):
                def invert(g, k):
                    for q in products:
                        at_least(pe, q, g + 1)
                    at_least(pe, o_out, g - 1)
                    for j in range(W):
                        for i in range(2):
                            ins = nc.tensor.matmul(po[k % 2][:, j, :], rr[:, k % 2, i, j, :], cst["idft_conv"][:, i * P:i * P + P],
                                                   start=(i == 0), stop=(i == 1))
                    ins.then_inc(inverted, 1)

                def project(g, k):
                    at_least(pe, o_out, g + 1)
                    at_least(pe, added, g - 1)
                    for j in range(W):
                        nc.tensor.matmul(py[k % 2][:, j, :], oT[:, k % 2, j, :], cst["w1T"][:, 3, :], start=True, stop=False)
                        ins = nc.tensor.matmul(py[k % 2][:, j, :], cst["ident"][:], x_res[:, bass.ds(g * W + j, 1), :],
                                               start=False, stop=True)
                    ins.then_inc(projected, 1)

                def turn(g, k):
                    at_least(pe, normed, g + 1)
                    at_least(pe, t_out, g - 1)
                    for j in range(W):
                        ins = nc.tensor.transpose(pt[k % 2][:, j, :], xn[:, k % 2, j, :], cst["ident"][:])
                    ins.then_inc(turned, 1)

                pipeline(pe, groups, 10, 2, in_order(((project, 3), (invert, 1), (turn, 6)), groups))


def ternary(nc, cst, x_res, xnT, amax, out, sem, chunks=TILES // 4):
    with ExitStack() as mem:
        def sb(name, shape, dt=F32):
            return mem.enter_context(nc.sbuf_tensor(name, shape, dt))

        gcol = sb("t_gcol", [P, 1])
        grow = sb("t_grow", [1, 1])
        bound = sb("t_bound", [P, 2])
        xq = sb("t_xq", [P, 2, 4, P])
        res = sb("t_res", [P, 4, 4, D])
        pg = mem.enter_context(nc.psum_tensor("t_pg", [P, 512], F32))
        py = [mem.enter_context(nc.psum_tensor(f"t_py{i}", [P, 4, P], F32)) for i in range(2)]
        chain = sem("t_chain")
        across = sem("t_across")
        clipped = sem("t_clipped")
        multiplied = sem("t_multiplied")
        summed = sem("t_summed")
        stored = [sem(f"t_stored{i}") for i in range(4)]
        idle = {e: sem(f"t_idle_{e}") for e in ("dve", "sp")}

        with nc.Block() as block:
            @block.vector
            def _(dve):
                nc.vector.tensor_reduce(gcol[:], amax[:], AX.X, ALU.max).then_inc(chain, 1)
                dve.wait_ge(across, 1)
                nc.vector.tensor_reduce(grow[:], pg[0:1, 0:P], AX.X, ALU.max).then_inc(chain, 1)
                dve.wait_ge(across, 2)
                edge = float(np.float32(QB - 1e-5)) / QB
                nc.vector.tensor_scalar(bound[:, 0:1], pg[:, P:P + 1], edge, None, ALU.mult)
                nc.vector.tensor_scalar(bound[:, 1:2], pg[:, P:P + 1], -edge, None, ALU.mult).then_inc(chain, 1)
                dve.wait_ge(chain, 3)

                def clip(c, k):
                    at_least(dve, multiplied, c - 1)
                    nc.vector.tensor_scalar(xq[:, k % 2].rearrange("p j t -> p (j t)"), xnT[:, bass.ds(c * 512, 512)],
                                            bound[:, 0:1], bound[:, 1:2], ALU.min, ALU.max).then_inc(clipped, 1)

                def sum_up(c, k):
                    at_least(dve, multiplied, c + 1)
                    at_least(dve, stored[k], c // 4 * 16 if isinstance(c, int) else (c - k) * 4)
                    nc.vector.scalar_tensor_tensor(res[:, k].rearrange("p j d -> p (j d)"), py[k % 2][:].rearrange("p j d -> p (j d)"),
                                                   cst["beta"][:], x_res[:, bass.ds(c * 4, 4), :].rearrange("p j d -> p (j d)"),
                                                   ALU.mult, ALU.add).then_inc(summed, 1)
                pipeline(dve, chunks, 5, 4, in_order(((clip, 0), (sum_up, 1)), chunks))

            @block.tensor
            def _(pe):
                pe.wait_ge(chain, 1)
                nc.tensor.transpose(pg[0:1, 0:P], gcol[:], cst["ident"][:]).then_inc(across, 1)
                pe.wait_ge(chain, 2)
                nc.tensor.matmul(pg[:, P:P + 1], cst["ones"][0:1, :], grow[:], start=True, stop=True).then_inc(across, 1)

                def multiply(c, k):
                    at_least(pe, clipped, c + 1)
                    at_least(pe, summed, c - 1)
                    for j in range(4):
                        ins = nc.tensor.matmul(py[k % 2][:, j, :], xq[:, k % 2, j, :], cst["wt"][:], start=True, stop=True)
                    ins.then_inc(multiplied, 1)
                pipeline(pe, chunks, 5, 4, in_order(((multiply, 0),), chunks))

            @block.sync
            def _(sp):
                def store(c, k):
                    wait_apart(sp, summed, c + 1, idle["sp"])
                    sp.dma_start(out[bass.ds(c * 4, 4)].rearrange("j p d -> p j d"), res[:, k]).then_inc(stored[k], 16)
                pipeline(sp, chunks, 5, 4, in_order(((store, 1),), chunks))
                for q in stored:
                    sp.wait_ge(q, 16 * (chunks // 4))


def host_tables():
    r = np.arange(S)
    return {
        "ident": np.eye(P, dtype=np.float32),
        "ident16": np.eye(P, dtype=np.float16),
        "hmask": np.kron(np.ones((2, 1)), np.kron(np.eye(8), np.ones((HD, 1)))).astype(np.float32),
        "maskq": np.tile(np.where(r[:, None] > r[None, :], -BIG, 0.0), (2, 2)).astype(np.float32),
        "maskk": np.tile(np.eye(S), (2, 8)).astype(np.float32),
        "sel": np.kron(np.arange(P)[:, None] % E == np.arange(E)[None, :], np.ones((1, FH))).astype(np.float16),
        **{k: v.astype(np.float32) for k, v in dft_tables().items()},
    }


def two_layers(nc, d, out):
    with ExitStack() as mem:
        def sb(name, shape, dt=F32):
            return mem.enter_context(nc.sbuf_tensor(name, shape, dt))

        def sem(name):
            return mem.enter_context(nc.semaphore(name))

        shapes = {
            "ident": ([P, P], F32), "ident16": ([P, P], F16), "hmask": ([P, 8], F32), "maskq": ([P, P], BF16),
            "maskk": ([P, 512], BF16), "ones": ([P, P], F32), "mhalf": ([P, 1], F32),
            "Wq": ([D, D], F32), "Wo": ([D, D], F32), "bqc": ([P, 1], F32), "bqs": ([P, 1], F32), "boe": ([P, D], F32),
            "centT": ([D, E], F32), "eb": ([P, E], F32),
            "w1T": ([D, 4, D], F32), "fbias": ([P, 4, D], F32), "bo1": ([P, D], F32),
            "dft": ([P, 2 * P], F32), "idft_corr": ([P, 2 * P], F32), "idft_conv": ([P, 2 * P], F32),
            "ln_gamma": ([D, 1], F32), "ln_beta": ([D, 1], F32), "beta": ([P, 1], F32), "wt": ([D, D], F32),
        }
        cst = {name: sb(name, shape, dt) for name, (shape, dt) in shapes.items()}
        x_res = sb("x_res", [P, TILES + 4, D])
        tile = "(t p) s d -> t (p s) d"
        x = d["x"].rearrange(tile, p=2)
        ctx = d["ctx"].rearrange(tile, p=2)
        y_mean = sb("y_mean", [P, TILES])
        y_rstd = sb("y_rstd", [P, TILES])
        with ExitStack() as ffn:
            for name in ("wuh", "wul", "wdh", "wdl"):
                cst[name] = ffn.enter_context(nc.sbuf_tensor(name, [P, PAIRS * P], F32R))
            norms = ChunkNorm(nc, ffn, sem)
            setup(nc, cst, d, sem)
            attention(nc, cst, d, x, d["ctxT"], x_res, norms, sem)
            experts(nc, cst, d, x_res, norms, y_mean, y_rstd, sem)
        xnT2 = sb("xnT2", [P, TILES * P])
        vf = sb("vf", [P, TILES, D])
        sums = sb("sums", [P, 2, TILES, H])
        cf = sb("cf", [P, 2, TILES, H])
        amax = sb("amax", [P, TILES // 2])
        spectrum(nc, cst, ctx, x_res, y_mean, y_rstd, vf, sums, sem)
        delays(nc, cst, sums, cf, sem)
        mix(nc, cst, x_res, vf, cf, xnT2, amax, sem)
        ternary(nc, cst, x_res, xnT2, amax, out.rearrange(tile, p=2), sem)


_NAMES = {
    "x": "x", "ctx": "ctx_1024", "Wq": "L0_xattn_Wq", "bq": "L0_xattn_bq", "Wo": "L0_xattn_Wo", "bo": "L0_xattn_bo",
    "centroids": "L0_ffn_centroids", "eb": "L0_ffn_expert_biases", "Ws_up": "L0_ffn_Ws_up", "Ws_down": "L0_ffn_Ws_down",
    "W_up": "L0_ffn_W_up", "W_down": "L0_ffn_W_down",
    "Wq1": "L1_xattn_Wq", "bq1": "L1_xattn_bq", "Wk1": "L1_xattn_Wk", "bk1": "L1_xattn_bk",
    "Wv1": "L1_xattn_Wv", "bv1": "L1_xattn_bv", "Wo1": "L1_xattn_Wo", "bo1": "L1_xattn_bo",
    "wt": "L1_ffn_weight", "ln_gamma": "L1_ffn_ln_gamma", "ln_beta": "L1_ffn_ln_beta",
}


def kernel(**inputs):
    import concourse.bacc as _bacc
    from concourse.bass_utils import run_bass_kernel_spmd as _run

    nc = _bacc.Bacc("TRN2", target_bir_lowering=False, num_devices=1)
    arrays, d = {}, {}
    for short, name in _NAMES.items():
        a = np.ascontiguousarray(inputs[name])
        arrays[f"in_{name}_dram"] = a
        d[short] = nc.dram_tensor(f"in_{name}_dram", a.shape, mybir.dt.from_np(a.dtype), kind="ExternalInput").ap()
    a = np.ascontiguousarray(np.transpose(inputs["ctx_1024"], (2, 0, 1)).reshape(D, TILES * P))
    arrays["in_ctxT_dram"] = a
    d["ctxT"] = nc.dram_tensor("in_ctxT_dram", a.shape, mybir.dt.from_np(a.dtype), kind="ExternalInput").ap()
    for name, a in host_tables().items():
        arrays[f"table_{name}_dram"] = a
        d[name] = nc.dram_tensor(f"table_{name}_dram", a.shape, mybir.dt.from_np(a.dtype), kind="ExternalInput").ap()
    out = nc.dram_tensor("out_0_dram", (2 * TILES, S, D), F32, kind="ExternalOutput").ap()
    two_layers(nc, d, out)
    r = _run(nc, [arrays], core_ids=[0])
    return r.results[0]["out_0_dram"]
```
